# Optimizing a Trainium2 kernel written in Bass

```python
import numpy as np
import jax
import jax.numpy as jnp

def _softmax(x, axis=-1):
    return jax.nn.softmax(x, axis=axis)

def _gelu(x):
    return jax.nn.gelu(x, approximate=True)

def _silu(x):
    return jax.nn.silu(x)

def _sigmoid(x):
    return jax.nn.sigmoid(x)

def _layernorm(x, axis=-1, eps=1e-05):
    m = jnp.mean(x, axis=axis, keepdims=True)
    v = jnp.var(x, axis=axis, keepdims=True)
    return (x - m) / jnp.sqrt(v + eps)

def _scatter_add(tgt, idx, src, axis=0):
    return tgt.at[idx].add(src)

def _segment_sum(src, seg, n):
    return jax.ops.segment_sum(src, seg, n)
kernel_name = 'mk_decoder_preln_d2_seqx_r4_35be61'

def setup_inputs(seed: int=0):
    np.random.seed(seed)
    _w = jnp.asarray

    def _rec_inputs():
        import jax
        import jax.numpy as jnp
        _rk = jax.random.key(seed)
        x = -0.0002928 + 1 * jax.random.normal(jax.random.fold_in(_rk, 1), (32, 128, 256), jnp.float32)
        _lenS = 128 - jax.random.randint(jax.random.fold_in(_rk, 7), (32,), 0, max(1, 128 // 4) + 1, jnp.int32)
        _lenS2 = 128 - jax.random.randint(jax.random.fold_in(_rk, 8), (32,), 0, max(1, 128 // 4) + 1, jnp.int32)
        _ctx_1024P = jax.random.normal(jax.random.fold_in(_rk, 11), (32, 16, 256), jnp.float32)
        _ctx_1024c = jax.random.dirichlet(jax.random.fold_in(_rk, 511), 0.3 * jnp.ones((16,), jnp.float32), (32, 128))
        _ctx_1024t = jnp.einsum('bsk,bkd->bsd', _ctx_1024c, _ctx_1024P)
        _ctx_1024t = _ctx_1024t * jax.lax.rsqrt(jnp.mean(jnp.square(_ctx_1024t)) + 1e-12) * 0.953939
        ctx_1024 = -1.39393e-06 + 0.999914 * (_ctx_1024t + 0.3 * jax.random.normal(jax.random.fold_in(_rk, 611), (32, 128, 256), jnp.float32))
        _validS = jnp.arange(128)[None, :] < _lenS[:, None]
        _validS2 = jnp.arange(128)[None, :] < _lenS2[:, None]
        _causal = jnp.tril(jnp.ones((128, 128), dtype=bool))
        mask_BxS2_bf1 = jnp.ones((32, 128), dtype=bool)
        return (x, ctx_1024, mask_BxS2_bf1)
    x, ctx_1024, mask_BxS2_bf1 = _rec_inputs()

    def _L0_attn_setup():
        import math
        import jax, jax.numpy as jnp
        import numpy as np
        N_HEAD = 16
        N_CLUSTER = 64
        GROUP_SIZE = 64

        def _sinusoidal(n, d):
            pos = jnp.arange(n, dtype=jnp.float32)[:, None]
            div = jnp.exp(jnp.arange(0, d, 2, dtype=jnp.float32) * (-math.log(10000.0) / d))
            ang = pos * div
            return jnp.stack([jnp.sin(ang), jnp.cos(ang)], axis=-1).reshape(n, d)

        def _rotary(pe, x):
            d = x.shape[-1]
            sin, cos = (pe[..., :d // 2], pe[..., d // 2:])
            x_even, x_odd = (x[..., ::2], x[..., 1::2])
            out = jnp.stack([-x_odd * cos, x_even * sin], axis=-1)
            return out.reshape(jnp.broadcast_shapes(x.shape[:-1] + (d // 2,), out.shape[:-1]) + (2,)).reshape(x.shape) if False else jnp.broadcast_to(out, x.shape[:-1] + (d // 2, 2)).reshape(x.shape)

        def _forward(x, w_attn, b_attn, w_proj, b_proj, w_assign):
            B, T, C = x.shape
            H, nc, gs = (N_HEAD, N_CLUSTER, GROUP_SIZE)
            hd = C // H
            ntpc = T // nc
            G = T // gs
            ncpg = gs // ntpc
            c_max = (G - 1) * ncpg
            qkv = x @ w_attn.T + b_attn
            q, k, v = jnp.split(qkv, 3, axis=-1)
            x_r = x.reshape(B, nc, ntpc, C)
            logits = jnp.einsum('bctd,cd->bct', x_r, w_assign)
            w = jax.nn.softmax(logits, axis=-1)
            ck = jnp.einsum('bct,bctd->bcd', w, k.reshape(B, nc, ntpc, C))
            cv = jnp.einsum('bct,bctd->bcd', w, v.reshape(B, nc, ntpc, C))
            qg = q.reshape(B, G, gs, H, hd).transpose(0, 1, 3, 2, 4)
            kl = k.reshape(B, G, gs, H, hd).transpose(0, 1, 3, 2, 4)
            vl = v.reshape(B, G, gs, H, hd).transpose(0, 1, 3, 2, 4)
            kc = ck[:, :c_max].reshape(B, c_max, H, hd)
            vc = cv[:, :c_max].reshape(B, c_max, H, hd)
            S = _sinusoidal(c_max + gs, hd)
            qr = _rotary(S[:gs], qg)
            kcr = _rotary(S[:c_max, None, :], kc)
            pos_local = jnp.arange(G)[:, None] * ncpg + jnp.arange(gs)[None, :]
            klr = _rotary(S[pos_local][None, :, None], kl)
            scale = 1.0 / math.sqrt(hd)
            sc = jnp.einsum('bghqd,bchd->bghqc', qr, kcr) * scale
            sl = jnp.einsum('bghqd,bghkd->bghqk', qr, klr) * scale
            cmask = jnp.arange(c_max)[None, :] < (jnp.arange(G) * ncpg)[:, None]
            sc = jnp.where(cmask[None, :, None, None, :], sc, -jnp.inf)
            lmask = jnp.tril(jnp.ones((gs, gs), dtype=bool))
            sl = jnp.where(lmask, sl, -jnp.inf)
            p = jax.nn.softmax(jnp.concatenate([sc, sl], axis=-1), axis=-1)
            pc, pl = (p[..., :c_max], p[..., c_max:])
            y = jnp.einsum('bghqc,bchd->bghqd', pc, vc) + jnp.einsum('bghqk,bghkd->bghqd', pl, vl)
            y = y.transpose(0, 1, 3, 2, 4).reshape(B, T, C)
            return y @ w_proj.T + b_proj
        key = jax.random.key(seed)
        ks = jax.random.split(key, 4)
        B, T, C, NC = (4, 1024, 256, N_CLUSTER)
        x = jax.random.normal(ks[0], (B, T, C), jnp.float32)
        w_attn = jax.random.normal(ks[1], (3 * C, C), jnp.float32) * 0.02
        b_attn = jnp.zeros((3 * C,), jnp.float32)
        w_proj = jax.random.normal(ks[2], (C, C), jnp.float32) * 0.02
        b_proj = jnp.zeros((C,), jnp.float32)
        w_assign = jax.random.normal(ks[3], (NC, C), jnp.float32) * 0.02
        return {'x': x, 'w_attn': w_attn, 'b_attn': b_attn, 'w_proj': w_proj, 'b_proj': b_proj, 'w_assign': w_assign}
    _L0_attn_all = _L0_attn_setup()
    _L0_attn_in = {k: v for k, v in _L0_attn_all.items() if k in ('w_attn', 'b_attn', 'w_proj', 'b_proj', 'w_assign')}
    del _L0_attn_all

    def _L0_xattn_setup():
        import jax, jax.numpy as jnp
        import numpy as np
        N_HEADS = 16
        D_MODEL = 256
        HEAD_DIM = D_MODEL // N_HEADS
        MASK_FILL = -100000000.0

        def _split_heads(x):
            B, S, _ = x.shape
            return x.reshape(B, S, N_HEADS, HEAD_DIM).transpose(0, 2, 1, 3)
        key = jax.random.key(seed)
        ks = jax.random.split(key, 12)
        B, L, P = (2, 512, 512)
        s = 1.0 / np.sqrt(D_MODEL).astype(np.float32)
        inp = {'q': jax.random.normal(ks[0], (B, L, D_MODEL), dtype=jnp.float32), 'k': jax.random.normal(ks[1], (B, P, D_MODEL), dtype=jnp.float32), 'v': jax.random.normal(ks[2], (B, P, D_MODEL), dtype=jnp.float32), 'attention_mask': jnp.ones((B, P), dtype=bool), 'Wq': jax.random.normal(ks[3], (D_MODEL, D_MODEL), dtype=jnp.float32) * s, 'bq': jnp.zeros((D_MODEL,), dtype=jnp.float32), 'Wk': jax.random.normal(ks[4], (D_MODEL, D_MODEL), dtype=jnp.float32) * s, 'bk': jnp.zeros((D_MODEL,), dtype=jnp.float32), 'Wv': jax.random.normal(ks[5], (D_MODEL, D_MODEL), dtype=jnp.float32) * s, 'bv': jnp.zeros((D_MODEL,), dtype=jnp.float32), 'Wo': jax.random.normal(ks[6], (D_MODEL, D_MODEL), dtype=jnp.float32) * s, 'bo': jnp.zeros((D_MODEL,), dtype=jnp.float32)}
        return inp
    _L0_xattn_all = _L0_xattn_setup()
    _L0_xattn_in = {k: v for k, v in _L0_xattn_all.items() if k in ('Wq', 'bq', 'Wk', 'bk', 'Wv', 'bv', 'Wo', 'bo')}
    del _L0_xattn_all

    def _L0_ffn_setup():
        import jax, jax.numpy as jnp
        import numpy as np
        HIDDEN = 256
        INNER = 1024

        def _weight_quant(w):
            scale = 1.0 / jnp.clip(jnp.mean(jnp.abs(w)), 1e-05)
            wq = jnp.clip(jnp.round(w * scale), -1.0, 1.0) / scale
            return w + jax.lax.stop_gradient(wq - w)

        def _act_quant(x):
            scale = 127.0 / jnp.clip(jnp.max(jnp.abs(x), axis=-1, keepdims=True), 1e-05)
            xq = jnp.clip(jnp.round(x * scale), -128.0, 127.0) / scale
            return x + jax.lax.stop_gradient(xq - x)

        def _bitlinear(x, w):
            return jnp.einsum('bsi,oi->bso', _act_quant(x), _weight_quant(w))
        key = jax.random.key(seed)
        k0, k1, k2, k3 = jax.random.split(key, 4)
        x = jax.random.normal(k0, (4, 512, HIDDEN), dtype=jnp.float32)
        w_gate = jax.random.normal(k1, (INNER, HIDDEN), dtype=jnp.float32) / np.sqrt(HIDDEN)
        w_up = jax.random.normal(k2, (INNER, HIDDEN), dtype=jnp.float32) / np.sqrt(HIDDEN)
        w_down = jax.random.normal(k3, (HIDDEN, INNER), dtype=jnp.float32) / np.sqrt(INNER)
        return {'x': x, 'w_gate': w_gate, 'w_up': w_up, 'w_down': w_down}
    _L0_ffn_all = _L0_ffn_setup()
    _L0_ffn_in = {k: v for k, v in _L0_ffn_all.items() if k in ('w_gate', 'w_up', 'w_down')}
    del _L0_ffn_all

    def _L1_attn_setup():
        import jax, jax.numpy as jnp
        import numpy as np
        B, S, D = (4, 1024, 256)
        H = 16
        K = D // H
        M = 64
        FF = 1024
        EPS = 1e-06

        def _layernorm(x, g, b):
            mu = jnp.mean(x, axis=-1, keepdims=True)
            var = jnp.mean(jnp.square(x - mu), axis=-1, keepdims=True)
            return (x - mu) * jax.lax.rsqrt(var + EPS) * g + b

        def _phi(u, omega):
            proj = jnp.einsum('bhsk,mk->bhsm', u, omega)
            sq = 0.5 * jnp.sum(u * u, axis=-1, keepdims=True)
            stab = jnp.max(proj, axis=-1, keepdims=True)
            m = jnp.asarray(M, u.dtype)
            return jnp.exp(proj - sq - stab) / jnp.sqrt(m) + 1e-06

        def _performer_attn(x, wq, wk, wv, wo, omega):
            q = jnp.einsum('bsd,dhk->bhsk', x, wq)
            k = jnp.einsum('bsd,dhk->bhsk', x, wk)
            v = jnp.einsum('bsd,dhk->bhsk', x, wv)
            scale = jnp.asarray(K, x.dtype) ** (-0.25)
            pq = _phi(q * scale, omega)
            pk = _phi(k * scale, omega)
            kv = jnp.einsum('bhsm,bhsk->bhmk', pk, v)
            z = jnp.sum(pk, axis=2)
            num = jnp.einsum('bhsm,bhmk->bhsk', pq, kv)
            den = jnp.einsum('bhsm,bhm->bhs', pq, z)
            out = num / den[..., None]
            out = out.transpose(0, 2, 1, 3).reshape(x.shape[0], x.shape[1], H * K)
            return out @ wo
        key = jax.random.key(seed)
        ks = jax.random.split(key, 12)
        s_in = 1.0 / np.sqrt(D)
        s_ff = 1.0 / np.sqrt(FF)
        return {'x': jax.random.normal(ks[0], (B, S, D), jnp.float32), 'wq': jax.random.normal(ks[1], (D, H, K), jnp.float32) * s_in, 'wk': jax.random.normal(ks[2], (D, H, K), jnp.float32) * s_in, 'wv': jax.random.normal(ks[3], (D, H, K), jnp.float32) * s_in, 'wo': jax.random.normal(ks[4], (H * K, D), jnp.float32) * s_in, 'omega': jax.random.normal(ks[5], (M, K), jnp.float32), 'ln1_g': jnp.ones((D,), jnp.float32), 'ln1_b': jnp.zeros((D,), jnp.float32), 'w1': jax.random.normal(ks[6], (D, FF), jnp.float32) * s_in, 'b1': jnp.zeros((FF,), jnp.float32), 'w2': jax.random.normal(ks[7], (FF, D), jnp.float32) * s_ff, 'b2': jnp.zeros((D,), jnp.float32), 'ln2_g': jnp.ones((D,), jnp.float32), 'ln2_b': jnp.zeros((D,), jnp.float32)}
    _L1_attn_all = _L1_attn_setup()
    _L1_attn_in = {k: v for k, v in _L1_attn_all.items() if k in ('wq', 'wk', 'wv', 'wo', 'omega', 'ln1_g', 'ln1_b', 'w1', 'b1', 'w2', 'b2', 'ln2_g', 'ln2_b')}
    del _L1_attn_all

    def _L1_xattn_setup():
        import jax, jax.numpy as jnp
        import numpy as np
        D_MODEL = 256
        N_HEADS = 16
        HEAD_DIM = D_MODEL // N_HEADS
        key = jax.random.key(seed)
        k1, k2, k3, k4, k5, k6 = jax.random.split(key, 6)
        B, T_q, T_kv = (4, 256, 1024)
        s = 1.0 / np.sqrt(D_MODEL)
        return {'query': jax.random.normal(k1, (B, T_q, D_MODEL), dtype=jnp.float32), 'kv_source': jax.random.normal(k2, (B, T_kv, D_MODEL), dtype=jnp.float32), 'w_q': jax.random.normal(k3, (D_MODEL, D_MODEL), dtype=jnp.float32) * s, 'w_k': jax.random.normal(k4, (D_MODEL, D_MODEL), dtype=jnp.float32) * s, 'w_v': jax.random.normal(k5, (D_MODEL, D_MODEL), dtype=jnp.float32) * s, 'w_o': jax.random.normal(k6, (D_MODEL, D_MODEL), dtype=jnp.float32) * s}
    _L1_xattn_all = _L1_xattn_setup()
    _L1_xattn_in = {k: v for k, v in _L1_xattn_all.items() if k in ('w_q', 'w_k', 'w_v', 'w_o')}
    del _L1_xattn_all

    def _L1_ffn_setup():
        import jax, jax.numpy as jnp
        import numpy as np
        HIDDEN = 256
        INTER = 512
        NUM_EXPERTS = 8
        TOPK = 2
        STD = 0.02
        key = jax.random.key(seed)
        k1, k2, k3, k4 = jax.random.split(key, 4)
        return {'hidden_states': jax.random.normal(k1, (1, 512, HIDDEN), dtype=jnp.float32), 'w1': jax.random.normal(k2, (NUM_EXPERTS, 2 * INTER, HIDDEN), dtype=jnp.float32) * STD, 'w2': jax.random.normal(k3, (NUM_EXPERTS, HIDDEN, INTER), dtype=jnp.float32) * STD, 'router_w': jax.random.normal(k4, (NUM_EXPERTS, HIDDEN), dtype=jnp.float32) * STD}
    _L1_ffn_all = _L1_ffn_setup()
    _L1_ffn_in = {k: v for k, v in _L1_ffn_all.items() if k in ('w1', 'w2', 'router_w')}
    del _L1_ffn_all
    return {'x': x, 'ctx_1024': ctx_1024, 'mask_BxS2_bf1': mask_BxS2_bf1, 'L0_attn_w_attn': _L0_attn_in['w_attn'], 'L0_attn_b_attn': _L0_attn_in['b_attn'], 'L0_attn_w_proj': _L0_attn_in['w_proj'], 'L0_attn_b_proj': _L0_attn_in['b_proj'], 'L0_attn_w_assign': _L0_attn_in['w_assign'], 'L0_xattn_Wq': _L0_xattn_in['Wq'], 'L0_xattn_bq': _L0_xattn_in['bq'], 'L0_xattn_Wk': _L0_xattn_in['Wk'], 'L0_xattn_bk': _L0_xattn_in['bk'], 'L0_xattn_Wv': _L0_xattn_in['Wv'], 'L0_xattn_bv': _L0_xattn_in['bv'], 'L0_xattn_Wo': _L0_xattn_in['Wo'], 'L0_xattn_bo': _L0_xattn_in['bo'], 'L0_ffn_w_gate': _L0_ffn_in['w_gate'], 'L0_ffn_w_up': _L0_ffn_in['w_up'], 'L0_ffn_w_down': _L0_ffn_in['w_down'], 'L1_attn_wq': _L1_attn_in['wq'], 'L1_attn_wk': _L1_attn_in['wk'], 'L1_attn_wv': _L1_attn_in['wv'], 'L1_attn_wo': _L1_attn_in['wo'], 'L1_attn_omega': _L1_attn_in['omega'], 'L1_attn_ln1_g': _L1_attn_in['ln1_g'], 'L1_attn_ln1_b': _L1_attn_in['ln1_b'], 'L1_attn_w1': _L1_attn_in['w1'], 'L1_attn_b1': _L1_attn_in['b1'], 'L1_attn_w2': _L1_attn_in['w2'], 'L1_attn_b2': _L1_attn_in['b2'], 'L1_attn_ln2_g': _L1_attn_in['ln2_g'], 'L1_attn_ln2_b': _L1_attn_in['ln2_b'], 'L1_xattn_w_q': _L1_xattn_in['w_q'], 'L1_xattn_w_k': _L1_xattn_in['w_k'], 'L1_xattn_w_v': _L1_xattn_in['w_v'], 'L1_xattn_w_o': _L1_xattn_in['w_o'], 'L1_ffn_w1': _L1_ffn_in['w1'], 'L1_ffn_w2': _L1_ffn_in['w2'], 'L1_ffn_router_w': _L1_ffn_in['router_w']}

def reference(x, ctx_1024, mask_BxS2_bf1, L0_attn_w_attn, L0_attn_b_attn, L0_attn_w_proj, L0_attn_b_proj, L0_attn_w_assign, L0_xattn_Wq, L0_xattn_bq, L0_xattn_Wk, L0_xattn_bk, L0_xattn_Wv, L0_xattn_bv, L0_xattn_Wo, L0_xattn_bo, L0_ffn_w_gate, L0_ffn_w_up, L0_ffn_w_down, L1_attn_wq, L1_attn_wk, L1_attn_wv, L1_attn_wo, L1_attn_omega, L1_attn_ln1_g, L1_attn_ln1_b, L1_attn_w1, L1_attn_b1, L1_attn_w2, L1_attn_b2, L1_attn_ln2_g, L1_attn_ln2_b, L1_xattn_w_q, L1_xattn_w_k, L1_xattn_w_v, L1_xattn_w_o, L1_ffn_w1, L1_ffn_w2, L1_ffn_router_w):
    import jax
    import jax.numpy as jnp

    def _L0_attn_ref(x, w_attn, b_attn, w_proj, b_proj, w_assign):
        import math
        import jax, jax.numpy as jnp
        import numpy as np
        N_HEAD = 16
        N_CLUSTER = 64
        GROUP_SIZE = 64

        def _sinusoidal(n, d):
            pos = jnp.arange(n, dtype=jnp.float32)[:, None]
            div = jnp.exp(jnp.arange(0, d, 2, dtype=jnp.float32) * (-math.log(10000.0) / d))
            ang = pos * div
            return jnp.stack([jnp.sin(ang), jnp.cos(ang)], axis=-1).reshape(n, d)

        def _rotary(pe, x):
            d = x.shape[-1]
            sin, cos = (pe[..., :d // 2], pe[..., d // 2:])
            x_even, x_odd = (x[..., ::2], x[..., 1::2])
            out = jnp.stack([-x_odd * cos, x_even * sin], axis=-1)
            return out.reshape(jnp.broadcast_shapes(x.shape[:-1] + (d // 2,), out.shape[:-1]) + (2,)).reshape(x.shape) if False else jnp.broadcast_to(out, x.shape[:-1] + (d // 2, 2)).reshape(x.shape)

        def _forward(x, w_attn, b_attn, w_proj, b_proj, w_assign):
            B, T, C = x.shape
            H, nc, gs = (N_HEAD, N_CLUSTER, GROUP_SIZE)
            hd = C // H
            ntpc = T // nc
            G = T // gs
            ncpg = gs // ntpc
            c_max = (G - 1) * ncpg
            qkv = x @ w_attn.T + b_attn
            q, k, v = jnp.split(qkv, 3, axis=-1)
            x_r = x.reshape(B, nc, ntpc, C)
            logits = jnp.einsum('bctd,cd->bct', x_r, w_assign)
            w = jax.nn.softmax(logits, axis=-1)
            ck = jnp.einsum('bct,bctd->bcd', w, k.reshape(B, nc, ntpc, C))
            cv = jnp.einsum('bct,bctd->bcd', w, v.reshape(B, nc, ntpc, C))
            qg = q.reshape(B, G, gs, H, hd).transpose(0, 1, 3, 2, 4)
            kl = k.reshape(B, G, gs, H, hd).transpose(0, 1, 3, 2, 4)
            vl = v.reshape(B, G, gs, H, hd).transpose(0, 1, 3, 2, 4)
            kc = ck[:, :c_max].reshape(B, c_max, H, hd)
            vc = cv[:, :c_max].reshape(B, c_max, H, hd)
            S = _sinusoidal(c_max + gs, hd)
            qr = _rotary(S[:gs], qg)
            kcr = _rotary(S[:c_max, None, :], kc)
            pos_local = jnp.arange(G)[:, None] * ncpg + jnp.arange(gs)[None, :]
            klr = _rotary(S[pos_local][None, :, None], kl)
            scale = 1.0 / math.sqrt(hd)
            sc = jnp.einsum('bghqd,bchd->bghqc', qr, kcr) * scale
            sl = jnp.einsum('bghqd,bghkd->bghqk', qr, klr) * scale
            cmask = jnp.arange(c_max)[None, :] < (jnp.arange(G) * ncpg)[:, None]
            sc = jnp.where(cmask[None, :, None, None, :], sc, -jnp.inf)
            lmask = jnp.tril(jnp.ones((gs, gs), dtype=bool))
            sl = jnp.where(lmask, sl, -jnp.inf)
            p = jax.nn.softmax(jnp.concatenate([sc, sl], axis=-1), axis=-1)
            pc, pl = (p[..., :c_max], p[..., c_max:])
            y = jnp.einsum('bghqc,bchd->bghqd', pc, vc) + jnp.einsum('bghqk,bghkd->bghqd', pl, vl)
            y = y.transpose(0, 1, 3, 2, 4).reshape(B, T, C)
            return y @ w_proj.T + b_proj
        return _forward(x, w_attn, b_attn, w_proj, b_proj, w_assign)

    def _L0_xattn_ref(q, k, v, attention_mask, Wq, bq, Wk, bk, Wv, bv, Wo, bo):
        import jax, jax.numpy as jnp
        import numpy as np
        N_HEADS = 16
        D_MODEL = 256
        HEAD_DIM = D_MODEL // N_HEADS
        MASK_FILL = -100000000.0

        def _split_heads(x):
            B, S, _ = x.shape
            return x.reshape(B, S, N_HEADS, HEAD_DIM).transpose(0, 2, 1, 3)
        qm = _split_heads(q @ Wq.T + bq)
        km = _split_heads(k @ Wk.T + bk)
        vm = _split_heads(v @ Wv.T + bv)
        scores = jnp.einsum('bnlh,bnph->bnlp', qm, km) / np.sqrt(HEAD_DIM).astype(np.float32)
        mask = attention_mask[:, None, None, :]
        scores = jnp.where(mask, scores, MASK_FILL)
        attn = jax.nn.softmax(scores, axis=-1)
        out = jnp.einsum('bnlp,bnph->bnlh', attn, vm)
        B, _, L, _ = out.shape
        out = out.transpose(0, 2, 1, 3).reshape(B, L, D_MODEL)
        return out @ Wo.T + bo

    def _L0_ffn_ref(x, w_gate, w_up, w_down):
        import jax, jax.numpy as jnp
        import numpy as np
        HIDDEN = 256
        INNER = 1024

        def _weight_quant(w):
            scale = 1.0 / jnp.clip(jnp.mean(jnp.abs(w)), 1e-05)
            wq = jnp.clip(jnp.round(w * scale), -1.0, 1.0) / scale
            return w + jax.lax.stop_gradient(wq - w)

        def _act_quant(x):
            scale = 127.0 / jnp.clip(jnp.max(jnp.abs(x), axis=-1, keepdims=True), 1e-05)
            xq = jnp.clip(jnp.round(x * scale), -128.0, 127.0) / scale
            return x + jax.lax.stop_gradient(xq - x)

        def _bitlinear(x, w):
            return jnp.einsum('bsi,oi->bso', _act_quant(x), _weight_quant(w))
        gate = jax.nn.silu(_bitlinear(x, w_gate))
        up = _bitlinear(x, w_up)
        return _bitlinear(gate * up, w_down)

    def _L1_attn_ref(x, wq, wk, wv, wo, omega, ln1_g, ln1_b, w1, b1, w2, b2, ln2_g, ln2_b):
        import jax, jax.numpy as jnp
        import numpy as np
        B, S, D = (4, 1024, 256)
        H = 16
        K = D // H
        M = 64
        FF = 1024
        EPS = 1e-06

        def _layernorm(x, g, b):
            mu = jnp.mean(x, axis=-1, keepdims=True)
            var = jnp.mean(jnp.square(x - mu), axis=-1, keepdims=True)
            return (x - mu) * jax.lax.rsqrt(var + EPS) * g + b

        def _phi(u, omega):
            proj = jnp.einsum('bhsk,mk->bhsm', u, omega)
            sq = 0.5 * jnp.sum(u * u, axis=-1, keepdims=True)
            stab = jnp.max(proj, axis=-1, keepdims=True)
            m = jnp.asarray(M, u.dtype)
            return jnp.exp(proj - sq - stab) / jnp.sqrt(m) + 1e-06

        def _performer_attn(x, wq, wk, wv, wo, omega):
            q = jnp.einsum('bsd,dhk->bhsk', x, wq)
            k = jnp.einsum('bsd,dhk->bhsk', x, wk)
            v = jnp.einsum('bsd,dhk->bhsk', x, wv)
            scale = jnp.asarray(K, x.dtype) ** (-0.25)
            pq = _phi(q * scale, omega)
            pk = _phi(k * scale, omega)
            kv = jnp.einsum('bhsm,bhsk->bhmk', pk, v)
            z = jnp.sum(pk, axis=2)
            num = jnp.einsum('bhsm,bhmk->bhsk', pq, kv)
            den = jnp.einsum('bhsm,bhm->bhs', pq, z)
            out = num / den[..., None]
            out = out.transpose(0, 2, 1, 3).reshape(x.shape[0], x.shape[1], H * K)
            return out @ wo
        h = _performer_attn(x, wq, wk, wv, wo, omega)
        x = _layernorm(x + h, ln1_g, ln1_b)
        h2 = jax.nn.gelu(x @ w1 + b1, approximate=False) @ w2 + b2
        x = _layernorm(x + h2, ln2_g, ln2_b)
        return x

    def _L1_xattn_ref(query, kv_source, w_q, w_k, w_v, w_o):
        import jax, jax.numpy as jnp
        import numpy as np
        D_MODEL = 256
        N_HEADS = 16
        HEAD_DIM = D_MODEL // N_HEADS
        B, T_q, _ = query.shape
        T_kv = kv_source.shape[1]
        q = (query @ w_q.T).reshape(B, T_q, N_HEADS, HEAD_DIM)
        k = (kv_source @ w_k.T).reshape(B, T_kv, N_HEADS, HEAD_DIM)
        v = (kv_source @ w_v.T).reshape(B, T_kv, N_HEADS, HEAD_DIM)
        scale = HEAD_DIM ** (-0.5)
        attn = jax.nn.softmax(jnp.einsum('bqhd,bkhd->bhqk', q, k) * scale, axis=-1)
        out = jnp.einsum('bhqk,bkhd->bqhd', attn, v).reshape(B, T_q, D_MODEL)
        return out @ w_o.T

    def _L1_ffn_ref(hidden_states, w1, w2, router_w):
        import jax, jax.numpy as jnp
        import numpy as np
        HIDDEN = 256
        INTER = 512
        NUM_EXPERTS = 8
        TOPK = 2
        STD = 0.02
        orig_shape = hidden_states.shape
        dtype = hidden_states.dtype
        x = hidden_states.reshape(-1, orig_shape[-1])
        E = w1.shape[0]
        gating = x @ router_w.T
        probs = jax.nn.softmax(gating.astype(jnp.float32), axis=-1)
        topk_w, sel = jax.lax.top_k(probs, TOPK)
        topk_w = topk_w.astype(dtype)
        combine = (jax.nn.one_hot(sel, E, dtype=dtype) * topk_w[..., None]).sum(axis=1)
        h = jnp.einsum('td,eid->tei', x, w1)
        gate = jax.nn.silu(h[..., :INTER])
        y = h[..., INTER:] * gate
        out = jnp.einsum('tei,ehi,te->th', y, w2, combine)
        return out.reshape(orig_shape)
    x = x + _L0_attn_ref(_layernorm(x, axis=-1), L0_attn_w_attn, L0_attn_b_attn, L0_attn_w_proj, L0_attn_b_proj, L0_attn_w_assign)
    x = x + _L0_xattn_ref(_layernorm(x, axis=-1), ctx_1024, ctx_1024, mask_BxS2_bf1, L0_xattn_Wq, L0_xattn_bq, L0_xattn_Wk, L0_xattn_bk, L0_xattn_Wv, L0_xattn_bv, L0_xattn_Wo, L0_xattn_bo)
    x = x + _L0_ffn_ref(_layernorm(x, axis=-1), L0_ffn_w_gate, L0_ffn_w_up, L0_ffn_w_down)
    x = x + _L1_attn_ref(_layernorm(x, axis=-1), L1_attn_wq, L1_attn_wk, L1_attn_wv, L1_attn_wo, L1_attn_omega, L1_attn_ln1_g, L1_attn_ln1_b, L1_attn_w1, L1_attn_b1, L1_attn_w2, L1_attn_b2, L1_attn_ln2_g, L1_attn_ln2_b)
    x = x + _L1_xattn_ref(_layernorm(x, axis=-1), ctx_1024, L1_xattn_w_q, L1_xattn_w_k, L1_xattn_w_v, L1_xattn_w_o)
    x = x + _L1_ffn_ref(_layernorm(x, axis=-1), L1_ffn_w1, L1_ffn_w2, L1_ffn_router_w)
    return x

_drawn_inputs = setup_inputs


def setup_inputs(seed=0):
    import zlib

    import numpy as np

    out = dict(_drawn_inputs(seed))
    spreads = {'L0_attn_b_attn': (0.0, 0.1),
     'L0_attn_b_proj': (0.0, 0.1),
     'L0_xattn_bq': (0.0, 0.362),
     'L0_xattn_bk': (0.0, 0.8),
     'L0_xattn_bv': (0.0, 0.1),
     'L0_xattn_bo': (0.0, 0.1),
     'L1_attn_ln1_g': (1.0, 0.2),
     'L1_attn_ln1_b': (0.0, 0.1),
     'L1_attn_b1': (0.0, 0.277),
     'L1_attn_b2': (0.0, 0.1),
     'L1_attn_ln2_g': (1.0, 0.2),
     'L1_attn_ln2_b': (0.0, 0.1)}
    factors = {'L0_attn_w_attn': 2.849,
     'L0_attn_w_assign': 8.0,
     'L1_ffn_w1': 8.0,
     'L1_ffn_w2': 8.0,
     'L1_ffn_router_w': 8.0}
    for name, (base, spread) in spreads.items():
        noise = np.random.default_rng([zlib.crc32(name.encode()), seed]).standard_normal(out[name].shape)
        drawn = base * np.exp(spread * noise) if base else spread * noise
        out[name] = jnp.asarray(drawn.astype(out[name].dtype))
    for name, factor in factors.items():
        out[name] = (out[name] * factor).astype(out[name].dtype)
    return out
```

```python
from contextlib import ExitStack

import numpy as np

import concourse.bass as bass
import concourse.mybir as mybir

F32 = mybir.dt.float32
BF16 = mybir.dt.bfloat16
U8 = mybir.dt.uint8
ALU = mybir.AluOpType
ACT = mybir.ActivationFunctionType
AX = mybir.AxisListType

P = 128
B, S, D = 32, 128, 256
CH = D // P
H, HD = 16, 16
HH = H // CH
VW = HD + 1
G = 4
GROUPS = B // G
UH = 4
UNITS = G * H // UH
NC = 32
GS = 64
KS = S + NC
KL = GS + NC
EPS = 1e-5
EPS_IN = 1e-6
ROUND = 1.5 * 2.0**23
MASK_FILL = -1e8
INNER = 1024
IC = INNER // P
NF = 64
E, EI = 8, 512
EC = EI // P


class Tally:

    def __init__(self, nc, name, per_turn, start=None):
        self.sem = nc.alloc_semaphore(name)
        self.per_turn = per_turn
        if per_turn and start is None:
            nc.gpsimd.sem_inc(self.sem, per_turn)

    def at(self, r, k):
        return r * self.per_turn + k


class Ring:

    def __init__(self, ctx, nc, name, banks, jobs):
        self.banks = [ctx.enter_context(nc.psum_tensor(f"{name}_bank{b}", [P, 512], F32)) for b in range(banks)]
        self._filled = [nc.alloc_semaphore(f"{name}_filled{b}") for b in range(banks)]
        self._drained = [nc.alloc_semaphore(f"{name}_drained{b}") for b in range(banks)]
        self.place = {job: (i % banks, i // banks) for i, job in enumerate(jobs)}
        self.uses = [len(jobs[b::banks]) for b in range(banks)]
        for b in range(banks):
            for sem in (self._filled[b], self._drained[b]):
                nc.gpsimd.sem_inc(sem, self.uses[b])

    def bank(self, job):
        return self.banks[self.place[job][0]]

    def filled(self, job):
        return self._filled[self.place[job][0]]

    def drained(self, job):
        return self._drained[self.place[job][0]]

    def full(self, r, job):
        b, turn = self.place[job]
        return r * self.uses[b] + turn + 1

    def free(self, r, job):
        b, turn = self.place[job]
        return r * self.uses[b] + turn


def bc(ap, shape):
    return ap.to_broadcast(shape)


class Stream:

    def __init__(self, ctx, nc):
        def sb(n, s):
            return ctx.enter_context(nc.sbuf_tensor(n, s, F32))
        self.x = sb("stream", [P, B * D])
        self.mean = [sb(f"mean{i}", [P, B]) for i in range(2)]
        self.rstd = [sb(f"rstd{i}", [P, B]) for i in range(2)]
        self.mean_in, self.rstd_in = sb("mean_in", [P, B]), sb("rstd_in", [P, B])
        self.now = 0

    def turn(self):
        self.now ^= 1


def seq(r, t, width=D):
    return bass.ds(r * (G * width) + (t - G) * width, width)


def group(r, width):
    return bass.ds(r * (G * width) - G * width, G * width)


class Rows:

    def __init__(self, ctx, nc, name, dest, mean, rstd, eps):
        def sb(n, s):
            return ctx.enter_context(nc.sbuf_tensor(f"{name}_{n}", s, F32))

        self.dest, self.mean, self.rstd, self.eps = dest, mean, rstd, eps
        self.slot = sb("rows", [P, 2, D])
        self.raw = sb("rows_raw", [P, 2, 6])
        self.mv = sb("rows_mean_var", [P, G, 2])
        self.var = sb("rows_var", [P, G])
        self.mhalf = sb("rows_mhalf", [P, G])
        self.const_ready = Tally(nc, f"{name}_mhalf_ready", 0)
        self.stored = Tally(nc, f"{name}_rows_stored", G)
        self.raw_ready = Tally(nc, f"{name}_rows_stats", G)
        self.aggr_ready = Tally(nc, f"{name}_rows_aggr", G)
        self.mean_stored = Tally(nc, f"{name}_mean_stored", 1)
        self.var_ready = Tally(nc, f"{name}_rstd_step", 2)

    def pool_start(self, pool):
        pool.memset(self.mhalf[:, :], -0.5).then_inc(self.const_ready.sem, 1)
        pool.wait_ge(self.const_ready.sem, 1)

    def wait_slot(self, dve, r, t):
        dve.wait_ge(self.stored.sem, self.stored.at(r, t - 1 if t >= 2 else 0))

    def take_stats(self, dve, r, t, written, count):
        dve.wait_ge(written, count)
        dve.bn_stats(self.raw[:, t % 2, :], self.slot[:, t % 2, :]).then_inc(self.raw_ready.sem, 1)
        dve.wait_ge(self.const_ready.sem, 1)
        dve.wait_ge(self.raw_ready.sem, self.raw_ready.at(r, t + 1))
        if t == 0:
            dve.wait_ge(self.mean_stored.sem, self.mean_stored.at(r, 0))
            dve.wait_ge(self.var_ready.sem, self.var_ready.at(r, 0))
        dve.bn_aggr(self.mv[:, t, :], self.raw[:, t % 2, :]).then_inc(self.aggr_ready.sem, 1)

    def store(self, pool, r, t):
        pool.wait_ge(self.const_ready.sem, 1)
        pool.wait_ge(self.raw_ready.sem, self.raw_ready.at(r, t + 1))
        pool.tensor_copy(self.dest[:, seq(r, t)], self.slot[:, t % 2, :]).then_inc(self.stored.sem, 1)

    def store_stats(self, pool, r):
        pool.wait_ge(self.const_ready.sem, 1)
        pool.wait_ge(self.aggr_ready.sem, self.aggr_ready.at(r, G))
        pool.tensor_copy(self.mean[:, group(r, 1)], self.mv[:, :, 0]).then_inc(self.mean_stored.sem, 1)
        pool.tensor_scalar(self.var[:, :], self.mv[:, :, 1], self.eps, None, ALU.add).then_inc(self.var_ready.sem, 1)
        pool.wait_ge(self.const_ready.sem, 1)
        pool.wait_ge(self.var_ready.sem, self.var_ready.at(r, 1))
        pool.tensor_tensor(self.rstd[:, group(r, 1)], self.var[:, :], self.mhalf[:, :], ALU.pow).then_inc(self.var_ready.sem, 1)


def load_phase(nc, st, io, ident):
    with ExitStack() as ctx:
        x_loaded = Tally(nc, "ld_x_loaded", 0)
        const_loaded = Tally(nc, "ld_const_loaded", 0)
        stats_ready = Tally(nc, "ld_stats_ready", 0)
        half_ready = Tally(nc, "ld_half_ready", 0)
        aggr_ready = Tally(nc, "ld_aggr_ready", 0)
        var_ready = Tally(nc, "ld_var_ready", 0)
        raw = ctx.enter_context(nc.sbuf_tensor("ld_raw", [P, B, 6], F32))
        mv = ctx.enter_context(nc.sbuf_tensor("ld_mv", [P, B, 2], F32))
        var = ctx.enter_context(nc.sbuf_tensor("ld_var", [P, B], F32))
        mhalf = ctx.enter_context(nc.sbuf_tensor("ld_mhalf", [P, B], F32))
        block = ctx.enter_context(nc.Block())

        @block.sync
        def _(sp):
            for q in range(4):
                n = B // 4
                sp.dma_start(st.x[:, q * n * D:(q + 1) * n * D].rearrange("p (n d) -> p n d", n=n),
                             io["x"].rearrange("(n p) d -> p n d", p=P)[:, q * n:(q + 1) * n, :]).then_inc(x_loaded.sem, 16)
            sp.dma_start(ident[:, :], io["ident"]).then_inc(const_loaded.sem, 16)
            sp.wait_ge(const_loaded.sem, 16)

        @block.vector
        def _(dve):
            dve.wait_ge(x_loaded.sem, 64)
            for b in range(B):
                dve.bn_stats(raw[:, b, :], st.x[:, b * D:(b + 1) * D]).then_inc(stats_ready.sem, 1)
            dve.wait_ge(stats_ready.sem, B)
            for b in range(B):
                dve.bn_aggr(mv[:, b, :], raw[:, b, :]).then_inc(aggr_ready.sem, 1)

        @block.gpsimd
        def _(pool):
            pool.memset(mhalf[:, :], -0.5).then_inc(half_ready.sem, 1)
            pool.wait_ge(aggr_ready.sem, B)
            pool.tensor_copy(st.mean[0][:, :], mv[:, :, 0])
            pool.tensor_scalar(var[:, :], mv[:, :, 1], EPS, None, ALU.add).then_inc(var_ready.sem, 1)
            pool.wait_ge(var_ready.sem, 1)
            pool.wait_ge(half_ready.sem, 1)
            pool.tensor_tensor(st.rstd[0][:, :], var[:, :], mhalf[:, :], ALU.pow).then_inc(var_ready.sem, 1)


def attention_phase(nc, st, io, ident, name, kind):
    own = kind == "self"
    biased = kind != "cross"
    KC = KS if own else S
    KU = KL if own else S
    VR = KL if own else S
    VG = 2 if own else 1
    mean, rstd = st.mean[st.now], st.rstd[st.now]
    mean_next, rstd_next = st.mean[st.now ^ 1], st.rstd[st.now ^ 1]

    if own:
        jobs = ([("xT", c) for c in range(CH)] + [("qT", c) for c in range(CH)] + ["logits"]
                + [("kT", c, i) for c in range(CH) for i in range(2)] + [("v", t) for t in range(G)])
    else:
        jobs = ([("xT", c) for c in range(CH)] + [("cT", c) for c in range(CH)]
                + [("qT", c) for c in range(CH)] + [("kT", c) for c in range(CH)]
                + [("v", i) for i in range(G // 2)])
    jobs += [(what, t) for t in range(G) for what in ("oT", "y")]

    with ExitStack() as ctx:
        def sb(n, s, dt=F32):
            return ctx.enter_context(nc.sbuf_tensor(f"{name}_{n}", s, dt))

        def tally(n, per, start=None):
            return Tally(nc, f"{name}_{n}", per, start)

        wq, wk, wv, wo = (sb(n, [P, CH, D]) for n in ("wq", "wk", "wv", "wo"))
        if biased:
            bq, bk = sb("bq", [P, CH]), sb("bk", [P, CH])
            bv, bo = sb("bv", [P, D]), sb("bo", [P, D])
        if own:
            assign = sb("assign", [P, CH, GS])
            rot_q = sb("rot_q", [P, S])
            spread = sb("spread", [P, HH, KS])
            causal = sb("causal", [P, UH, KL], BF16)
            identb = sb("identb", [P, P], BF16)
            ones = sb("ones", [P, P])
            prod = sb("prod", [P, CH, G, GS])
            expo = sb("expo", [P, G, GS])
            pair = sb("pair", [P, G * GS // 2])
            wts = sb("wts", [P, G, GS])
        else:
            spread = sb("spread", [P, HH])
            cin = sb("cin", [P, G, D])
            cT = sb("cT", [P, CH, G * S])
        if kind == "masked":
            mrow = sb("mrow", [P, G * S], U8)
            mask = sb("mask", [P, G * S])
            fill = sb("fill", [P, G, 1, S], BF16)
            parts = sb("parts", [P, 1])
            onesb = sb("onesb", [P, P], BF16)
        xn = sb("xn", [P, G, D])
        xT = sb("xT", [P, CH, G, KC])
        qT = sb("qT", [P, CH, G * S])
        kT = sb("kT", [P, CH, G, KC])
        KB = 4
        kbd = sb("kbd", [P, KB, HH, KC])
        v = sb("v", [VR, G, VG, H, VW])
        sc = sb("sc", [P, 4, UH, KU])
        mx = sb("mx", [P, 4, UH])
        pT = sb("pT", [VR, 2, UH * S])
        rs = sb("rs", [P, 2, H])
        o = sb("o", [P, 2, D])
        oT = sb("oT", [P, 2, CH, P])

        loaded = tally("weights_loaded", 0)
        ctx_loaded = tally("context_loaded", 32 if kind == "masked" else 16, 0)
        const_ready = tally("const_ready", 0)
        xn_ready = tally("xn_ready", G)
        mask_ready = tally("mask_ready", 2)
        prod_ready = tally("prod_ready", CH)
        v_step = tally("v_step", 3 * G)
        cl_ready = tally("cluster_step", 6)
        expo_ready = tally("cluster_exp_ready", 1)
        xc_ready = tally("clusters_ready", CH)
        kbd_ready = tally("kbd_ready", 2 * G)
        mx_ready = tally("rowmax_ready", UNITS)
        ex_ready = tally("exp_ready", UNITS)
        rs_ready = tally("recip_ready", G)
        xb_ready = tally("bias_added", G)
        rows = Rows(ctx, nc, name, st.x, mean_next, rstd_next, EPS)
        proj = Ring(ctx, nc, f"{name}_proj", 2, jobs)
        score = Ring(ctx, nc, f"{name}_score", 2, list(range(UNITS)))
        turned = Ring(ctx, nc, f"{name}_turned", 2, list(range(UNITS)))
        out = Ring(ctx, nc, f"{name}_out", 2, list(range(G)))
        n_const = 4 + (4 if biased else 0) + (5 if own else 1) + (1 if kind == "masked" else 0)
        block = ctx.enter_context(nc.Block())

        @block.sync
        def _(sp):
            for tile, key in ((wq, "wq"), (wk, "wk"), (wv, "wv"), (wo, "wo")):
                sp.dma_start(tile[:, :, :], io[f"{name}_{key}"].rearrange("(c p) o -> p c o", p=P)).then_inc(loaded.sem, 16)
            if biased:
                for tile, key in ((bq, "bq"), (bk, "bk")):
                    sp.dma_start(tile[:, :], io[f"{name}_{key}"]).then_inc(loaded.sem, 16)
                for tile, key in ((bv, "bv"), (bo, "bo")):
                    sp.dma_start(tile[:, :], io[f"{name}_{key}"].partition_broadcast(P)).then_inc(loaded.sem, 16)
            if own:
                sp.dma_start(assign[:, :, :], io[f"{name}_assign"].rearrange("(c p) o -> p c o", p=P)).then_inc(loaded.sem, 16)
                sp.dma_start(rot_q[:, :], io["rot_q"]).then_inc(loaded.sem, 16)
                sp.dma_start(spread[:, :, :], io["rot_k"]).then_inc(loaded.sem, 16)
                sp.dma_start(causal[:, :, :], io["causal"]).then_inc(loaded.sem, 16)
                sp.dma_start(identb[:, :], io["identb"]).then_inc(loaded.sem, 16)
            else:
                sp.dma_start(spread[:, :], io["heads"]).then_inc(loaded.sem, 16)
                if kind == "masked":
                    sp.dma_start(parts[:, :], io["parts"]).then_inc(loaded.sem, 16)
                context = io["ctx"].rearrange("(n p) d -> p n d", p=P)
                sp.dma_start(cin[:, :, :], context[:, 0:G, :]).then_inc(ctx_loaded.sem, 16)
                if kind == "masked":
                    sp.dma_start(mrow[:, :], io["mask"][1, :].partition_broadcast(P)).then_inc(ctx_loaded.sem, 16)
                with sp.Fori(1, GROUPS, 1) as r:
                    sp.wait_ge(proj.filled(("cT", CH - 1)), proj.full(r, ("cT", CH - 1)))
                    sp.dma_start(cin[:, :, :], context[:, bass.ds(r * G, G), :]).then_inc(ctx_loaded.sem, 16)
                    if kind == "masked":
                        sp.wait_ge(mask_ready.sem, mask_ready.at(r, 1))
                        sp.dma_start(mrow[:, :].rearrange("p (a k) -> p a k", a=1),
                                     io["mask"][bass.ds(r + 1, 1), :].partition_broadcast(P)).then_inc(ctx_loaded.sem, 16)
            sp.wait_ge(loaded.sem, 16 * n_const)

        @block.gpsimd
        def _(pool):
            rows.pool_start(pool)
            pool.memset(v[:, :, :, :, HD:VW], 1.0).then_inc(const_ready.sem, 1)
            if own:
                pool.memset(ones[:, :], 1.0).then_inc(const_ready.sem, 1)
            elif kind == "masked":
                pool.memset(onesb[:, :], 1.0).then_inc(const_ready.sem, 1)
            pool.wait_ge(loaded.sem, 16 * n_const)

            with pool.Fori(1, GROUPS + 1, 1) as r:
                if biased:
                    for t in range(G):
                        pool.wait_ge(xn_ready.sem, xn_ready.at(r, t + 1))
                        pool.tensor_tensor(st.x[:, seq(r, t)], st.x[:, seq(r, t)], bo[:, :], ALU.add).then_inc(xb_ready.sem, 1)
                for j in range(2 * G):
                    t, c = j // 2, j % 2
                    job = ("kT", c, t // 2) if own else ("kT", c)
                    pool.wait_ge(proj.drained(job), proj.full(r, job))
                    table = spread[:, :, :] if own else bc(spread[:, :, None], [P, HH, KC])
                    if j >= KB:
                        u = 2 * (j - KB) + 1
                        pool.wait_ge(score.filled(u), score.full(r, u))
                    else:
                        pool.wait_ge(score.filled(1), score.free(r, 1))
                    pool.tensor_tensor(kbd[:, j % KB, :, :], bc(kT[:, c, t, :][:, None, :], [P, HH, KC]),
                                       table, ALU.mult).then_inc(kbd_ready.sem, 1)
                for t in range(G):
                    rows.store(pool, r, t)
                rows.store_stats(pool, r)

        @block.tensor
        def _(pe):
            pe.wait_ge(loaded.sem, 16 * n_const)
            pe.wait_ge(const_ready.sem, 2 if own or kind == "masked" else 1)

            def wait_copied(r, jobs):
                for job in jobs:
                    pe.wait_ge(proj.drained(job), proj.full(r, job))

            def project(r, job, weights, c, moving):
                pe.wait_ge(proj.drained(job), proj.free(r, job))
                n = moving[0].free_size()
                for k in range(CH):
                    mm = pe.matmul(proj.bank(job)[:, 0:n], weights[:, k, c * P:(c + 1) * P], moving[k],
                                   start=(k == 0), stop=(k == CH - 1))
                mm.then_inc(proj.filled(job), 1)

            with pe.Fori(1, GROUPS + 1, 1) as r:
                for c in range(CH):
                    pe.wait_ge(proj.drained(("xT", c)), proj.free(r, ("xT", c)))
                    for t in range(G):
                        pe.wait_ge(xn_ready.sem, xn_ready.at(r, t + 1))
                        mm = pe.transpose(proj.bank(("xT", c))[:, t * P:(t + 1) * P], xn[:, t, c * P:(c + 1) * P], ident[:, :])
                    mm.then_inc(proj.filled(("xT", c)), 1)
                if own:
                    wait_copied(r, [("xT", c) for c in range(CH)])
                    for c in range(CH):
                        project(r, ("qT", c), wq, c, [xT[:, k, :, 0:S] for k in range(CH)])
                    pe.wait_ge(prod_ready.sem, prod_ready.at(r, CH))
                    pe.wait_ge(proj.drained("logits"), proj.free(r, "logits"))
                    for k in range(CH):
                        mm = pe.matmul(proj.bank("logits")[:, 0:G * GS], ones[:, :], prod[:, k, :, :],
                                       start=(k == 0), stop=(k == CH - 1))
                    mm.then_inc(proj.filled("logits"), 1)
                    pe.wait_ge(xc_ready.sem, xc_ready.at(r, CH))
                    for c in range(CH):
                        for i in range(2):
                            project(r, ("kT", c, i), wk, c, [xT[:, k, 2 * i:2 * i + 2, :] for k in range(CH)])
                    for t in range(G):
                        pe.wait_ge(proj.drained(("v", t)), proj.free(r, ("v", t)))
                        for rows, at, n in ((0, 0, GS), (0, GS, GS), (GS, S, NC)):
                            col = D if at == GS else 0
                            for k in range(CH):
                                mm = pe.matmul(proj.bank(("v", t))[rows:rows + n, col:col + D], xT[:, k, t, at:at + n],
                                               wv[:, k, :], start=(k == 0), stop=(k == CH - 1))
                        mm.then_inc(proj.filled(("v", t)), 1)
                else:
                    pe.wait_ge(ctx_loaded.sem, ctx_loaded.at(r, 0))
                    for c in range(CH):
                        pe.wait_ge(proj.drained(("cT", c)), proj.free(r, ("cT", c)))
                        for t in range(G):
                            mm = pe.transpose(proj.bank(("cT", c))[:, t * P:(t + 1) * P], cin[:, t, c * P:(c + 1) * P], ident[:, :])
                        mm.then_inc(proj.filled(("cT", c)), 1)
                    wait_copied(r, [("xT", c) for c in range(CH)])
                    for c in range(CH):
                        project(r, ("qT", c), wq, c, [xT[:, k, :, :] for k in range(CH)])
                    wait_copied(r, [("cT", c) for c in range(CH)])
                    for c in range(CH):
                        project(r, ("kT", c), wk, c, [cT[:, k, :] for k in range(CH)])
                    for i in range(G // 2):
                        pe.wait_ge(proj.drained(("v", i)), proj.free(r, ("v", i)))
                        for t in (2 * i, 2 * i + 1):
                            for k in range(CH):
                                mm = pe.matmul(proj.bank(("v", i))[:, (t % 2) * D:(t % 2 + 1) * D], cT[:, k, t * P:(t + 1) * P],
                                               wv[:, k, :], start=(k == 0), stop=(k == CH - 1))
                        mm.then_inc(proj.filled(("v", i)), 1)
                if kind == "masked":
                    pe.wait_ge(mask_ready.sem, mask_ready.at(r, 2))
                wait_copied(r, [("qT", c) for c in range(CH)])

                def scores(u):
                    t, g = u // 4, u % 4
                    c, half = g // 2, g % 2
                    bank = score.bank(u)
                    pe.wait_ge(score.drained(u), score.free(r, u))
                    if half == 0:
                        pe.wait_ge(kbd_ready.sem, kbd_ready.at(r, u // 2 + 1))
                    keys = kbd[:, (u // 2) % KB, half * UH:(half + 1) * UH, :]
                    if own:
                        view = bank[:, 0:UH * KL].rearrange("p (h k) -> p h k", h=UH)
                        pe.matmul(bank[:, 0:UH * KL], identb[:, :], causal[:, :, :], start=True, stop=False, skip_group_check=True)
                        pe.matmul(view[0:GS, :, 0:GS], qT[:, c, t * S:t * S + GS], keys[:, :, 0:GS],
                                  start=False, stop=True, skip_group_check=True)
                        mm = pe.matmul(view[GS:S, :, :], qT[:, c, t * S + GS:(t + 1) * S], keys[:, :, GS:KS],
                                       start=False, stop=True, skip_group_check=True)
                    elif kind == "masked":
                        pe.matmul(bank[:, :], onesb[:, :], bc(fill[:, t, :, :], [P, UH, S]), start=True, stop=False)
                        mm = pe.matmul(bank[:, :], qT[:, c, t * S:(t + 1) * S], keys, start=False, stop=True)
                    else:
                        mm = pe.matmul(bank[:, :], qT[:, c, t * S:(t + 1) * S], keys, start=True, stop=True)
                    mm.then_inc(score.filled(u), 1)

                def turn(u):
                    pe.wait_ge(ex_ready.sem, ex_ready.at(r, u + 1))
                    pe.wait_ge(turned.drained(u), turned.free(r, u))
                    for h in range(UH):
                        mm = pe.transpose(turned.bank(u)[0:VR, h * P:(h + 1) * P], sc[:, u % 4, h, :], ident[:, :])
                    mm.then_inc(turned.filled(u), 1)

                def values(u):
                    t, g = u // 4, u % 4
                    pe.wait_ge(turned.drained(u), turned.full(r, u))
                    if g == 0:
                        pe.wait_ge(out.drained(t), out.free(r, t))
                        wait_copied(r, [("v", t if own else t // 2)])
                    for h in range(UH):
                        col = (g * UH + h) * VW
                        for i in range(VG):
                            q = slice(i * GS, (i + 1) * GS) if own else slice(0, S)
                            mm = pe.matmul(out.bank(t)[q, col:col + VW], pT[:, u % 2, h * P + q.start:h * P + q.stop],
                                           v[:, t, i, g * UH + h, :], start=True, stop=True)
                    if g == 3:
                        mm.then_inc(out.filled(t), 1)

                def output(t):
                    pe.wait_ge(out.drained(t), out.full(r, t))
                    pe.wait_ge(proj.drained(("oT", t)), proj.free(r, ("oT", t)))
                    for c in range(CH):
                        mm = pe.transpose(proj.bank(("oT", t))[:, c * P:(c + 1) * P], o[:, t % 2, c * P:(c + 1) * P], ident[:, :])
                    mm.then_inc(proj.filled(("oT", t)), 1)

                def output_product(t):
                    wait_copied(r, [("oT", t)])
                    pe.wait_ge(proj.drained(("y", t)), proj.free(r, ("y", t)))
                    for k in range(CH):
                        mm = pe.matmul(proj.bank(("y", t))[:, 0:D], oT[:, t % 2, k, :], wo[:, k, :],
                                       start=(k == 0), stop=(k == CH - 1))
                    mm.then_inc(proj.filled(("y", t)), 1)

                for s in range(UNITS + 8):
                    if s < UNITS:
                        scores(s)
                    if 0 <= s - 2 < UNITS:
                        turn(s - 2)
                    if 0 <= s - 3 < UNITS:
                        values(s - 3)
                    if s >= 8 and (s - 8) % 4 == 0 and (s - 8) // 4 < G:
                        output((s - 8) // 4)
                    if s >= 10 and (s - 10) % 4 == 0 and (s - 10) // 4 < G:
                        output_product((s - 10) // 4)

        @block.scalar
        def _(act):
            act.wait_ge(loaded.sem, 16 * n_const)
            with act.Fori(1, GROUPS + 1, 1) as r:
                def drain(job, write):
                    act.wait_ge(proj.filled(job), proj.full(r, job))
                    write(proj.bank(job)).then_inc(proj.drained(job), 1)

                for c in range(CH):
                    drain(("xT", c), lambda bank: act.copy(
                        xT[:, c, :, 0:S], bank[:, :].rearrange("p (t k) -> p t k", t=G)))
                if own:
                    act.wait_ge(cl_ready.sem, cl_ready.at(r, 2))
                    act.activation(expo[:, :, :], expo[:, :, :], ACT.Exp).then_inc(expo_ready.sem, 1)
                    for c in range(CH):
                        for i in range(2):
                            drain(("kT", c, i), lambda bank: act.activation(
                                kT[:, c, 2 * i:2 * i + 2, :], bank[:, 0:2 * KC].rearrange("p (t k) -> p t k", t=2),
                                ACT.Identity, bias=bk[:, c:c + 1]))
                else:
                    for c in range(CH):
                        drain(("qT", c), lambda bank: act.activation(
                            qT[:, c, :], bank[:, :], ACT.Identity, bias=bq[:, c:c + 1]) if biased else act.copy(qT[:, c, :], bank[:, :]))
                    if not biased:
                        for i in range(G // 2):
                            drain(("v", i), lambda bank: act.copy(
                                v[:, 2 * i:2 * i + 2, 0, :, 0:HD], bank[:, :].rearrange("p (t h d) -> p t h d", t=2, h=H)))

                for s in range(UNITS + 8):
                    if s < UNITS:
                        act.wait_ge(score.drained(s), score.full(r, s))
                        act.activation(sc[:, s % 4, :, :], sc[:, s % 4, :, :], ACT.Exp, scale=HD ** -0.5).then_inc(ex_ready.sem, 1)
                    u = s - 2
                    if 0 <= u < UNITS and u % 2 == 0:
                        act.wait_ge(turned.filled(u), turned.full(r, u))
                        act.copy(pT[:, u % 2, :], turned.bank(u)[0:VR, :]).then_inc(turned.drained(u), 1)
                    if s >= 9 and (s - 9) % 4 == 0 and (s - 9) // 4 < G:
                        t = (s - 9) // 4
                        drain(("oT", t), lambda bank: act.copy(
                            oT[:, t % 2, :, :], bank[:, 0:D].rearrange("p (c k) -> p c k", c=CH)))

        @block.vector
        def _(dve):
            dve.wait_ge(loaded.sem, 16 * n_const)
            dve.wait_ge(const_ready.sem, 1)
            with dve.Fori(1, GROUPS + 1, 1) as r:
                def drain(job, write):
                    dve.wait_ge(proj.filled(job), proj.full(r, job))
                    write(proj.bank(job)).then_inc(proj.drained(job), 1)

                for t in range(G):
                    dve.tensor_scalar(xn[:, t, :], st.x[:, seq(r, t)], mean[:, seq(r, t, 1)],
                                      rstd[:, seq(r, t, 1)], ALU.subtract, ALU.mult).then_inc(xn_ready.sem, 1)
                if own:
                    for c in range(CH):
                        dve.wait_ge(proj.drained(("xT", c)), proj.full(r, ("xT", c)))
                        dve.tensor_tensor(prod[:, c, :, :], xT[:, c, :, 0:GS], bc(assign[:, c, :][:, None, :], [P, G, GS]),
                                          ALU.mult).then_inc(prod_ready.sem, 1)
                    for c in range(CH):
                        drain(("qT", c), lambda bank: dve.scalar_tensor_tensor(
                            qT[:, c, :].rearrange("p (t k) -> p t k", t=G), bank[:, :].rearrange("p (t k) -> p t k", t=G),
                            bq[:, c:c + 1], bc(rot_q[:, None, :], [P, G, S]), ALU.add, ALU.mult))
                    pairs = [P, G * GS // 2, 2]
                    logits = proj.bank("logits")[:, 0:G * GS].rearrange("p (n k) -> p n k", k=2)
                    e2, w2 = (a[:, :, :].rearrange("p t (n k) -> p (t n) k", k=2) for a in (expo, wts))
                    dve.wait_ge(proj.filled("logits"), proj.full(r, "logits"))
                    dve.tensor_reduce(pair[:, :], logits, AX.X, ALU.max).then_inc(cl_ready.sem, 1)
                    dve.wait_ge(cl_ready.sem, cl_ready.at(r, 1))
                    dve.tensor_tensor(e2, logits, bc(pair[:, :, None], pairs), ALU.subtract).then_inc(cl_ready.sem, 1)
                    dve.wait_ge(cl_ready.sem, cl_ready.at(r, 2))
                    dve.wait_ge(expo_ready.sem, expo_ready.at(r, 1))
                    dve.tensor_reduce(pair[:, :], e2, AX.X, ALU.add).then_inc(proj.drained("logits"), 1)
                    dve.wait_ge(proj.drained("logits"), proj.full(r, "logits"))
                    dve.reciprocal(pair[:, :], pair[:, :]).then_inc(cl_ready.sem, 1)
                    dve.wait_ge(cl_ready.sem, cl_ready.at(r, 3))
                    dve.tensor_tensor(w2, e2, bc(pair[:, :, None], pairs), ALU.mult).then_inc(cl_ready.sem, 1)
                    dve.wait_ge(cl_ready.sem, cl_ready.at(r, 4))
                    for c in range(CH):
                        dve.tensor_tensor(prod[:, c, :, :], xT[:, c, :, 0:GS], wts[:, :, :], ALU.mult).then_inc(cl_ready.sem, 1)
                    for c in range(CH):
                        dve.wait_ge(cl_ready.sem, cl_ready.at(r, 5 + c))
                        dve.tensor_reduce(xT[:, c, :, S:KC], prod[:, c, :, :].rearrange("p t (n k) -> p t n k", k=2),
                                          AX.X, ALU.add).then_inc(xc_ready.sem, 1)
                    dve.wait_ge(xc_ready.sem, xc_ready.at(r, CH))
                    for t in range(G):
                        job = ("v", t)
                        dve.wait_ge(proj.filled(job), proj.full(r, job))
                        local = proj.bank(job)[0:GS, :].rearrange("p (i h d) -> p i h d", i=2, h=H)
                        cluster = proj.bank(job)[GS:KL, 0:D].rearrange("p (h d) -> p h d", h=H)
                        bias = bv[:, :].rearrange("p (h d) -> p h d", h=H)
                        for i in range(2):
                            dve.tensor_tensor(v[0:GS, t, i, :, 0:HD], local[:, i], bias[0:GS], ALU.add).then_inc(v_step.sem, 1)
                        dve.tensor_tensor(v[GS:KL, t, 0, :, 0:HD], cluster, bias[GS:KL], ALU.add).then_inc(v_step.sem, 1)
                        dve.tensor_tensor(v[GS:KL, t, 1, :, 0:HD], cluster, bias[GS:KL], ALU.add).then_inc(proj.drained(job), 1)
                else:
                    if kind == "masked":
                        dve.wait_ge(ctx_loaded.sem, ctx_loaded.at(r, 0))
                        dve.tensor_copy(mask[:, :], mrow[:, :]).then_inc(mask_ready.sem, 1)
                        dve.wait_ge(mask_ready.sem, mask_ready.at(r, 1))
                        dve.tensor_scalar(fill[:, :, 0, :], mask[:, :].rearrange("p (t k) -> p t k", t=G), -1.0, parts[:, 0:1],
                                          ALU.add, ALU.mult).then_inc(mask_ready.sem, 1)
                    for c in range(CH):
                        drain(("cT", c), lambda bank: dve.tensor_copy(cT[:, c, :], bank[:, :]))
                    for c in range(CH):
                        out_k = kT[:, c, :, :].rearrange("p t k -> p (t k)")
                        drain(("kT", c), lambda bank: dve.scalar_tensor_tensor(
                            out_k, bank[:, :], bk[:, c:c + 1], mask[:, :], ALU.add, ALU.mult) if kind == "masked"
                            else dve.tensor_copy(out_k, bank[:, :]))
                    if biased:
                        for i in range(G // 2):
                            drain(("v", i), lambda bank: dve.tensor_tensor(
                                v[:, 2 * i:2 * i + 2, 0, :, 0:HD], bank[:, :].rearrange("p (t h d) -> p t h d", t=2, h=H),
                                bc(bv[:, :].rearrange("p (a h d) -> p a h d", a=1, h=H), [P, 2, H, HD]), ALU.add))

                for s in range(UNITS + 8):
                    if s < UNITS:
                        dve.wait_ge(score.filled(s), score.full(r, s))
                        unit = score.bank(s)[:, 0:UH * KU].rearrange("p (h k) -> p h k", h=UH)
                        dve.tensor_reduce(mx[:, s % 4, :], unit, AX.X, ALU.max).then_inc(mx_ready.sem, 1)
                        dve.wait_ge(mx_ready.sem, mx_ready.at(r, s + 1))
                        dve.tensor_tensor(sc[:, s % 4, :, :], unit, bc(mx[:, s % 4, :, None], [P, UH, KU]),
                                          ALU.subtract).then_inc(score.drained(s), 1)
                    u = s - 2
                    if 0 <= u < UNITS and u % 2 == 1:
                        dve.wait_ge(turned.filled(u), turned.full(r, u))
                        dve.tensor_copy(pT[:, u % 2, :], turned.bank(u)[0:VR, :]).then_inc(turned.drained(u), 1)
                    if s >= 7 and (s - 7) % 4 == 0 and (s - 7) // 4 < G:
                        t = (s - 7) // 4
                        dve.wait_ge(out.filled(t), out.full(r, t))
                        heads = out.bank(t)[:, 0:H * VW].rearrange("p (h d) -> p h d", h=H)
                        dve.reciprocal(rs[:, t % 2, :], heads[:, :, HD]).then_inc(rs_ready.sem, 1)
                        dve.wait_ge(rs_ready.sem, rs_ready.at(r, t + 1))
                        dve.tensor_tensor(o[:, t % 2, :].rearrange("p (h d) -> p h d", h=H), heads[:, :, 0:HD],
                                          bc(rs[:, t % 2, :, None], [P, H, HD]), ALU.mult).then_inc(out.drained(t), 1)
                    if s >= 11 and (s - 11) % 4 == 0 and (s - 11) // 4 < G:
                        t = (s - 11) // 4
                        if biased:
                            dve.wait_ge(xb_ready.sem, xb_ready.at(r, t + 1))
                        rows.wait_slot(dve, r, t)
                        drain(("y", t), lambda bank: dve.tensor_tensor(
                            rows.slot[:, t % 2, :], st.x[:, seq(r, t)], bank[:, 0:D], ALU.add))
                        rows.take_stats(dve, r, t, proj.drained(("y", t)), proj.full(r, ("y", t)))
    st.turn()


def bitlinear_phase(nc, st, io, ident):
    mean, rstd = st.mean[st.now], st.rstd[st.now]
    HI = INNER // 2
    halves = [(t, i) for t in range(G) for i in range(2)]
    with ExitStack() as ctx:
        def sb(n, s, dt=F32):
            return ctx.enter_context(nc.sbuf_tensor(f"bit_{n}", s, dt))

        def tally(n, per):
            return Tally(nc, f"bit_{n}", per)

        shapes = {"gate": [P, CH, INNER], "up": [P, CH, INNER], "down": [P, IC, D]}
        names = list(shapes)
        rawf = {n: sb(f"raw_{n}", [P, CH * INNER]) for n in names}
        quant = {n: sb(f"w_{n}", shapes[n], BF16) for n in names}
        identb = sb("identb", [P, P], BF16)
        ones = sb("ones", [P, P])
        sums, wmean, wscale = sb("sums", [P, 3]), sb("wmean", [P, 3]), sb("wscale", [P, 3])
        xn = sb("xn", [P, G, D])
        amax, alim, arec, ascale = (sb(n, [P, G]) for n in ("amax", "alim", "arec", "ascale"))
        dgate, dup, ddown = (sb(n, [P, G]) for n in ("dgate", "dup", "ddown"))
        xq = sb("xq", [P, G, D], BF16)
        xqT = sb("xqT", [P, CH, G * S], BF16)
        sg = sb("sg", [P, 2, HI])
        h = sb("h", [P, 2, INNER])
        hmax, hlim, hrec, hscale = (sb(n, [P, G]) for n in ("hmax", "hlim", "hrec", "hscale"))
        hq = sb("hq", [P, 2, INNER], BF16)
        hqT = sb("hqT", [P, 2, IC, P], BF16)
        round_col = sb("round", [P, 1])

        loaded = tally("weights_loaded", 0)
        ones_ready = tally("ones_ready", 0)
        sums_ready = tally("sums_ready", 0)
        total_ready = tally("total_ready", 0)
        wstep = tally("weight_step", 0)
        ascale_ready = tally("ascale_ready", 1)
        ddown_ready = tally("ddown_ready", G)
        xstep = tally("x_step", G + 5 + G)
        xq_ready = tally("xq_ready", G)
        sg_ready = tally("silu_ready", 2 * G)
        hstep = tally("h_step", 4 * G)
        hr_ready = tally("h_rounded", G)
        hq_ready = tally("hq_ready", G)
        rows = Rows(ctx, nc, "bit", st.x, st.mean[st.now ^ 1], st.rstd[st.now ^ 1], EPS)
        turned = Ring(ctx, nc, "bit_turned", 2, ["xT"] + [("hT", t) for t in range(G)])
        gates = Ring(ctx, nc, "bit_gates", 2, halves)
        ups = Ring(ctx, nc, "bit_ups", 2, halves)
        outs = Ring(ctx, nc, "bit_outs", 2, list(range(G)))
        block = ctx.enter_context(nc.Block())

        @block.sync
        def _(sp):
            for n in names:
                sp.dma_start(rawf[n][:, :].rearrange("p (c o) -> p c o", c=shapes[n][1]),
                             io[f"bit_{n}"].rearrange("(c p) o -> p c o", p=P)).then_inc(loaded.sem, 16)
            sp.dma_start(identb[:, :], io["identb"]).then_inc(loaded.sem, 16)
            sp.wait_ge(loaded.sem, 64)

        @block.gpsimd
        def _(pool):
            rows.pool_start(pool)
            pool.memset(ones[:, :], 1.0).then_inc(ones_ready.sem, 1)
            with pool.Fori(1, GROUPS + 1, 1) as r:
                for t in range(G):
                    rows.store(pool, r, t)
                rows.store_stats(pool, r)

        @block.tensor
        def _(pe):
            pe.wait_ge(loaded.sem, 64)
            pe.wait_ge(ones_ready.sem, 1)
            pe.wait_ge(sums_ready.sem, 3)
            pe.matmul(outs.banks[1][:, 0:3], ones[:, :], sums[:, :], start=True, stop=True).then_inc(total_ready.sem, 1)
            pe.wait_ge(wstep.sem, 12)
            with pe.Fori(1, GROUPS + 1, 1) as r:
                pe.wait_ge(turned.drained("xT"), turned.free(r, "xT"))
                xT = turned.bank("xT")[:, :].bitcast(BF16)
                for t in range(G):
                    pe.wait_ge(xq_ready.sem, xq_ready.at(r, t + 1))
                    for c in range(CH):
                        col = c * G * S + t * S
                        mm = pe.transpose(xT[:, col:col + S], xq[:, t, c * P:(c + 1) * P], identb[:, :])
                mm.then_inc(turned.filled("xT"), 1)
                pe.wait_ge(turned.drained("xT"), turned.full(r, "xT"))

                def widen(t):
                    for i in range(2):
                        for ring, n in ((gates, "gate"), (ups, "up")):
                            pe.wait_ge(ring.drained((t, i)), ring.free(r, (t, i)))
                            for k in range(CH):
                                mm = pe.matmul(ring.bank((t, i))[:, :], xqT[:, k, t * S:(t + 1) * S],
                                               quant[n][:, k, i * HI:(i + 1) * HI], start=(k == 0), stop=(k == CH - 1))
                            mm.then_inc(ring.filled((t, i)), 1)

                def turn(t):
                    pe.wait_ge(turned.drained(("hT", t)), turned.free(r, ("hT", t)))
                    pe.wait_ge(hq_ready.sem, hq_ready.at(r, t + 1))
                    hT = turned.bank(("hT", t))[:, :].bitcast(BF16)
                    for k in range(IC):
                        mm = pe.transpose(hT[:, k * P:(k + 1) * P], hq[:, t % 2, k * P:(k + 1) * P], identb[:, :])
                    mm.then_inc(turned.filled(("hT", t)), 1)

                def narrow(t):
                    pe.wait_ge(turned.drained(("hT", t)), turned.full(r, ("hT", t)))
                    pe.wait_ge(outs.drained(t), outs.free(r, t))
                    for k in range(IC):
                        mm = pe.matmul(outs.bank(t)[:, 0:D], hqT[:, t % 2, k, :], quant["down"][:, k, :],
                                       start=(k == 0), stop=(k == IC - 1))
                    mm.then_inc(outs.filled(t), 1)

                for s in range(G + 3):
                    if s < G:
                        widen(s)
                    if 0 <= s - 2 < G:
                        turn(s - 2)
                    if 0 <= s - 3 < G:
                        narrow(s - 3)

        @block.scalar
        def _(act):
            with act.Fori(1, GROUPS + 1, 1) as r:
                for s in range(G + 1):
                    if s < G:
                        for i in range(2):
                            act.wait_ge(xstep.sem, xstep.at(r, G + 5))
                            act.wait_ge(gates.filled((s, i)), gates.full(r, (s, i)))
                            if (s, i) >= (1, 0):
                                j = 2 * s + i - 2
                                act.wait_ge(ups.drained(halves[j]), ups.full(r, halves[j]))
                            act.activation(sg[:, i, :], gates.bank((s, i))[:, :], ACT.Silu,
                                           scale=dgate[:, s:s + 1]).then_inc(gates.drained((s, i)), 1)
                    if s >= 1:
                        t = s - 1
                        act.wait_ge(hstep.sem, hstep.at(r, 4 * t + 4))
                        act.activation(h[:, t % 2, :], h[:, t % 2, :], ACT.Identity, bias=round_col[:, 0:1],
                                       scale=hscale[:, t:t + 1]).then_inc(hr_ready.sem, 1)

        @block.vector
        def _(dve):
            dve.memset(round_col[:, :], ROUND).then_inc(wstep.sem, 1)
            dve.wait_ge(loaded.sem, 64)
            for i, n in enumerate(names):
                dve.tensor_reduce(sums[:, i:i + 1], rawf[n][:, :], AX.X, ALU.add, apply_absolute_value=True).then_inc(sums_ready.sem, 1)
            dve.wait_ge(total_ready.sem, 1)
            dve.tensor_scalar(wmean[:, :], outs.banks[1][:, 0:3], 1.0 / (D * INNER), 1e-5, ALU.mult, ALU.max).then_inc(wstep.sem, 1)
            dve.wait_ge(wstep.sem, 2)
            dve.reciprocal(wscale[:, :], wmean[:, :]).then_inc(wstep.sem, 1)
            dve.wait_ge(wstep.sem, 3)
            for i, n in enumerate(names):
                dve.tensor_scalar(rawf[n][:, :], rawf[n][:, :], wscale[:, i:i + 1], ROUND, ALU.mult, ALU.add).then_inc(wstep.sem, 1)
            for i, n in enumerate(names):
                dve.wait_ge(wstep.sem, 4 + i)
                dve.tensor_scalar(rawf[n][:, :], rawf[n][:, :], ROUND, 1.0, ALU.subtract, ALU.min).then_inc(wstep.sem, 1)
            for i, n in enumerate(names):
                dve.wait_ge(wstep.sem, 7 + i)
                last = dve.tensor_scalar(quant[n][:, :, :].rearrange("p c o -> p (c o)"), rawf[n][:, :], -1.0, None, ALU.max)
                last.then_inc(wstep.sem, 1)
            with dve.Fori(1, GROUPS + 1, 1) as r:
                for t in range(G):
                    dve.tensor_scalar(xn[:, t, :], st.x[:, seq(r, t)], mean[:, seq(r, t, 1)],
                                      rstd[:, seq(r, t, 1)], ALU.subtract, ALU.mult).then_inc(xstep.sem, 1)
                dve.wait_ge(xstep.sem, xstep.at(r, G))
                dve.tensor_reduce(amax[:, :], xn[:, :, :], AX.X, ALU.max, apply_absolute_value=True).then_inc(xstep.sem, 1)
                dve.wait_ge(xstep.sem, xstep.at(r, G + 1))
                dve.tensor_scalar(alim[:, :], amax[:, :], 1e-5, None, ALU.max).then_inc(xstep.sem, 1)
                dve.wait_ge(xstep.sem, xstep.at(r, G + 2))
                dve.reciprocal(arec[:, :], alim[:, :]).then_inc(xstep.sem, 1)
                dve.tensor_scalar(dgate[:, :], alim[:, :], wmean[:, 0:1], 1.0 / 127, ALU.mult, ALU.mult).then_inc(xstep.sem, 1)
                dve.tensor_scalar(dup[:, :], alim[:, :], wmean[:, 1:2], 1.0 / 127, ALU.mult, ALU.mult).then_inc(xstep.sem, 1)
                dve.wait_ge(xstep.sem, xstep.at(r, G + 5))
                dve.tensor_scalar(ascale[:, :], arec[:, :], 127.0, None, ALU.mult).then_inc(ascale_ready.sem, 1)
                dve.wait_ge(ascale_ready.sem, ascale_ready.at(r, 1))
                for t in range(G):
                    dve.tensor_scalar(xn[:, t, :], xn[:, t, :], ascale[:, t:t + 1], ROUND, ALU.mult, ALU.add).then_inc(xstep.sem, 1)
                for t in range(G):
                    dve.wait_ge(xstep.sem, xstep.at(r, G + 6 + t))
                    dve.tensor_scalar(xq[:, t, :], xn[:, t, :], ROUND, 127.0, ALU.subtract, ALU.min).then_inc(xq_ready.sem, 1)
                dve.wait_ge(turned.filled("xT"), turned.full(r, "xT"))
                dve.tensor_scalar(xqT[:, :, :].rearrange("p c k -> p (c k)"), turned.bank("xT")[:, :].bitcast(BF16),
                                  -128.0, None, ALU.max).then_inc(turned.drained("xT"), 1)

                for s in range(G + 4):
                    if s < G:
                        for i in range(2):
                            dve.wait_ge(ups.filled((s, i)), ups.full(r, (s, i)))
                            dve.wait_ge(gates.drained((s, i)), gates.full(r, (s, i)))
                            dve.scalar_tensor_tensor(h[:, s % 2, i * HI:(i + 1) * HI], ups.bank((s, i))[:, :], dup[:, s:s + 1],
                                                     sg[:, i, :], ALU.mult, ALU.mult).then_inc(ups.drained((s, i)), 1)
                    if 0 <= s - 1 < G:
                        t = s - 1
                        dve.wait_ge(hr_ready.sem, hr_ready.at(r, t + 1))
                        dve.tensor_scalar(hq[:, t % 2, :], h[:, t % 2, :], ROUND, 127.0, ALU.subtract, ALU.min).then_inc(hq_ready.sem, 1)
                    if s < G:
                        dve.wait_ge(ups.drained((s, 0)), ups.full(r, (s, 0)))
                        dve.wait_ge(ups.drained((s, 1)), ups.full(r, (s, 1)))
                        one = slice(s, s + 1)
                        dve.tensor_reduce(hmax[:, one], h[:, s % 2, :], AX.X, ALU.max, apply_absolute_value=True).then_inc(hstep.sem, 1)
                        dve.wait_ge(hstep.sem, hstep.at(r, 4 * s + 1))
                        dve.tensor_scalar(hlim[:, one], hmax[:, one], 1e-5, None, ALU.max).then_inc(hstep.sem, 1)
                        dve.wait_ge(hstep.sem, hstep.at(r, 4 * s + 2))
                        dve.reciprocal(hrec[:, one], hlim[:, one]).then_inc(hstep.sem, 1)
                        dve.tensor_scalar(ddown[:, one], hlim[:, one], wmean[:, 2:3], 1.0 / 127, ALU.mult, ALU.mult).then_inc(ddown_ready.sem, 1)
                        dve.wait_ge(hstep.sem, hstep.at(r, 4 * s + 3))
                        dve.tensor_scalar(hscale[:, one], hrec[:, one], 127.0, None, ALU.mult).then_inc(hstep.sem, 1)
                    if 0 <= s - 2 < G:
                        t = s - 2
                        dve.wait_ge(turned.filled(("hT", t)), turned.full(r, ("hT", t)))
                        dve.tensor_scalar(hqT[:, t % 2, :, :].rearrange("p c k -> p (c k)"), turned.bank(("hT", t))[:, :].bitcast(BF16),
                                          -128.0, None, ALU.max).then_inc(turned.drained(("hT", t)), 1)
                    if 0 <= s - 3 < G:
                        t = s - 3
                        rows.wait_slot(dve, r, t)
                        dve.wait_ge(ddown_ready.sem, ddown_ready.at(r, t + 1))
                        dve.wait_ge(outs.filled(t), outs.full(r, t))
                        dve.scalar_tensor_tensor(rows.slot[:, t % 2, :], outs.bank(t)[:, 0:D], ddown[:, t:t + 1],
                                                 st.x[:, seq(r, t)], ALU.mult, ALU.add).then_inc(outs.drained(t), 1)
                        rows.take_stats(dve, r, t, outs.drained(t), outs.full(r, t))
    st.turn()


def second_layer_self(nc, st, io, ident):
    with ExitStack() as ctx:
        y = ctx.enter_context(nc.sbuf_tensor("inner_stream", [P, B * D], F32))
        performer_phase(nc, st, io, ident, y)
        mlp_phase(nc, st, io, ident, y)


def performer_phase(nc, st, io, ident, y):
    mean, rstd = st.mean[st.now], st.rstd[st.now]
    jobs = ([("xT", c) for c in range(CH)] + [("qT", c) for c in range(CH)] + [("kT", c) for c in range(CH)]
            + ["squares"] + [("v", i) for i in range(G // 2)] + [(what, t) for t in range(G) for what in ("oT", "y")])
    PAIRS = H // 2
    PW = 2 * VW
    mids = [(what, t) for t in range(G) for what in ("kv", "q0", "q1")]
    with ExitStack() as ctx:
        def sb(n, s, dt=F32):
            return ctx.enter_context(nc.sbuf_tensor(f"perf_{n}", s, dt))

        def tally(n, per):
            return Tally(nc, f"perf_{n}", per)

        wq, wk, wv, wo = (sb(n, [P, CH, D]) for n in ("wq", "wk", "wv", "wo"))
        omega = sb("omega", [P, HH * NF])
        half_heads = sb("half_heads", [P, HH])
        floor = sb("floor", [P, 1])
        xn = sb("xn", [P, G, D])
        xT = sb("xT", [P, CH, G * S])
        qk = sb("qk", [P, 2, CH, G * S])
        qk2 = sb("qk2", [P, 2, CH, G * S])
        half2 = sb("half2", [P, G, 2, H])
        v = sb("v", [P, G, H, VW])
        f = sb("f", [P, 4, HH, NF])
        mx, off = sb("mx", [P, 4, HH]), sb("off", [P, 4, HH])
        fT = sb("fT", [P, 2, 4 * P])
        kv = sb("kv", [P, 2, PAIRS, PW])
        rs = sb("rs", [P, 2, H])
        o = sb("o", [P, 2, D])
        oT = sb("oT", [P, 2, CH, P])

        loaded = tally("weights_loaded", 0)
        const_ready = tally("const_ready", 0)
        xn_ready = tally("xn_ready", G)
        square_ready = tally("squares_ready", 2 * CH)
        copied = tally("scaled_ready", CH)
        mx_ready = tally("max_ready", UNITS)
        off_ready = tally("offset_ready", UNITS)
        ex_ready = tally("exp_ready", UNITS)
        f_ready = tally("features_ready", UNITS)
        kv_half = tally("kv_half", G)
        rs_ready = tally("recip_ready", G)
        rows = Rows(ctx, nc, "perf", y, st.mean_in, st.rstd_in, EPS_IN)
        proj = Ring(ctx, nc, "perf_proj", 2, jobs)
        score = Ring(ctx, nc, "perf_score", 2, list(range(UNITS)))
        mid = Ring(ctx, nc, "perf_mid", 2, mids)
        out = Ring(ctx, nc, "perf_out", 2, list(range(G)))
        block = ctx.enter_context(nc.Block())

        @block.sync
        def _(sp):
            for tile, key in ((wq, "wq"), (wk, "wk"), (wv, "wv"), (wo, "wo")):
                sp.dma_start(tile[:, :, :], io[f"perf_{key}"].rearrange("(c p) o -> p c o", p=P)).then_inc(loaded.sem, 16)
            sp.dma_start(omega[:, :], io["omega"]).then_inc(loaded.sem, 16)
            sp.dma_start(half_heads[:, :], io["half_heads"]).then_inc(loaded.sem, 16)
            sp.wait_ge(loaded.sem, 96)

        @block.gpsimd
        def _(pool):
            rows.pool_start(pool)
            pool.memset(v[:, :, :, HD:VW], 1.0).then_inc(const_ready.sem, 1)
            pool.memset(kv[:, :, :, :], 0.0).then_inc(const_ready.sem, 1)
            pool.memset(floor[:, :], 1e-6 * NF ** 0.5).then_inc(const_ready.sem, 1)
            pool.wait_ge(const_ready.sem, 3)
            with pool.Fori(1, GROUPS + 1, 1) as r:
                for s in range(UNITS + 8):
                    if s < UNITS:
                        pool.wait_ge(ex_ready.sem, ex_ready.at(r, s + 1))
                        flat = f[:, s % 4, :, :].rearrange("p h m -> p (h m)")
                        pool.tensor_tensor(flat, flat, bc(floor[:, :], [P, HH * NF]), ALU.add).then_inc(f_ready.sem, 1)
                    if s >= 11 and (s - 11) % 4 == 0 and (s - 11) // 4 < G:
                        t = (s - 11) // 4
                        rows.store(pool, r, t)
                rows.store_stats(pool, r)

        @block.tensor
        def _(pe):
            pe.wait_ge(loaded.sem, 96)
            pe.wait_ge(const_ready.sem, 3)
            with pe.Fori(1, GROUPS + 1, 1) as r:
                for c in range(CH):
                    pe.wait_ge(proj.drained(("xT", c)), proj.free(r, ("xT", c)))
                    for t in range(G):
                        pe.wait_ge(xn_ready.sem, xn_ready.at(r, t + 1))
                        mm = pe.transpose(proj.bank(("xT", c))[:, t * P:(t + 1) * P], xn[:, t, c * P:(c + 1) * P], ident[:, :])
                    mm.then_inc(proj.filled(("xT", c)), 1)
                for c in range(CH):
                    pe.wait_ge(proj.drained(("xT", c)), proj.full(r, ("xT", c)))
                for what, w in (("qT", wq), ("kT", wk)):
                    for c in range(CH):
                        pe.wait_ge(proj.drained((what, c)), proj.free(r, (what, c)))
                        for k in range(CH):
                            mm = pe.matmul(proj.bank((what, c))[:, :], w[:, k, c * P:(c + 1) * P], xT[:, k, :],
                                           start=(k == 0), stop=(k == CH - 1))
                        mm.then_inc(proj.filled((what, c)), 1)
                pe.wait_ge(square_ready.sem, square_ready.at(r, 2 * CH))
                pe.wait_ge(proj.drained("squares"), proj.free(r, "squares"))
                for t in range(G):
                    for w in range(2):
                        for c in range(CH):
                            col = (t * 2 + w) * H + c * HH
                            mm = pe.matmul(proj.bank("squares")[:, col:col + HH], qk2[:, w, c, t * S:(t + 1) * S], half_heads[:, :],
                                           start=True, stop=True)
                mm.then_inc(proj.filled("squares"), 1)
                for i in range(G // 2):
                    pe.wait_ge(proj.drained(("v", i)), proj.free(r, ("v", i)))
                    for t in (2 * i, 2 * i + 1):
                        for k in range(CH):
                            mm = pe.matmul(proj.bank(("v", i))[:, (t % 2) * D:(t % 2 + 1) * D], xT[:, k, t * P:(t + 1) * P],
                                           wv[:, k, :], start=(k == 0), stop=(k == CH - 1))
                    mm.then_inc(proj.filled(("v", i)), 1)

                def features(u):
                    t, w, c = u // 4, 1 - (u % 4) // 2, u % 2
                    pe.wait_ge(score.drained(u), score.free(r, u))
                    pe.matmul(score.bank(u)[:, :], qk[:, w, c, t * S:(t + 1) * S], omega[:, :],
                              start=True, stop=True).then_inc(score.filled(u), 1)

                def use(u):
                    t, c = u // 4, u % 2
                    pe.wait_ge(f_ready.sem, f_ready.at(r, u + 1))
                    keys = u % 4 < 2
                    job = ("kv" if keys else f"q{c}", t)
                    if c == 0 or not keys:
                        pe.wait_ge(mid.drained(job), mid.free(r, job))
                    if keys and c == 0:
                        pe.wait_ge(proj.drained(("v", t // 2)), proj.full(r, ("v", t // 2)))
                    for j in range(4):
                        pair = c * 4 + j
                        two = f[:, u % 4, 2 * j:2 * j + 2, :].rearrange("p h m -> p (h m)")
                        if keys:
                            mm = pe.matmul(mid.bank(job)[:, pair * PW:(pair + 1) * PW], two, v[:, t, 2 * pair:2 * pair + 2, :],
                                           start=True, stop=True)
                        else:
                            mm = pe.transpose(mid.bank(job)[:, j * P:(j + 1) * P], two, ident[:, :])
                    if c == 1 or not keys:
                        mm.then_inc(mid.filled(job), 1)

                def attend(u):
                    t, c = u // 4, u % 2
                    job = (f"q{c}", t)
                    pe.wait_ge(mid.drained(job), mid.full(r, job))
                    if c == 0:
                        pe.wait_ge(mid.drained(("kv", t)), mid.full(r, ("kv", t)))
                        pe.wait_ge(out.drained(t), out.free(r, t))
                    for j in range(4):
                        pair = c * 4 + j
                        mm = pe.matmul(out.bank(t)[:, pair * PW:(pair + 1) * PW], fT[:, c, j * P:(j + 1) * P], kv[:, t % 2, pair, :],
                                       start=True, stop=True)
                    if c == 1:
                        mm.then_inc(out.filled(t), 1)

                def output(t):
                    pe.wait_ge(out.drained(t), out.full(r, t))
                    pe.wait_ge(proj.drained(("oT", t)), proj.free(r, ("oT", t)))
                    for c in range(CH):
                        mm = pe.transpose(proj.bank(("oT", t))[:, c * P:(c + 1) * P], o[:, t % 2, c * P:(c + 1) * P], ident[:, :])
                    mm.then_inc(proj.filled(("oT", t)), 1)

                def output_product(t):
                    pe.wait_ge(proj.drained(("oT", t)), proj.full(r, ("oT", t)))
                    pe.wait_ge(proj.drained(("y", t)), proj.free(r, ("y", t)))
                    for k in range(CH):
                        mm = pe.matmul(proj.bank(("y", t))[:, 0:D], oT[:, t % 2, k, :], wo[:, k, :],
                                       start=(k == 0), stop=(k == CH - 1))
                    mm.then_inc(proj.filled(("y", t)), 1)

                for s in range(UNITS + 8):
                    if s < UNITS:
                        features(s)
                    if 0 <= s - 2 < UNITS:
                        use(s - 2)
                    if 0 <= s - 3 < UNITS and (s - 3) % 4 >= 2:
                        attend(s - 3)
                    if s >= 8 and (s - 8) % 4 == 0 and (s - 8) // 4 < G:
                        output((s - 8) // 4)
                    if s >= 10 and (s - 10) % 4 == 0 and (s - 10) // 4 < G:
                        output_product((s - 10) // 4)

        @block.scalar
        def _(act):
            act.wait_ge(loaded.sem, 96)
            with act.Fori(1, GROUPS + 1, 1) as r:
                def drain(job, write):
                    act.wait_ge(proj.filled(job), proj.full(r, job))
                    write(proj.bank(job)).then_inc(proj.drained(job), 1)

                for c in range(CH):
                    drain(("xT", c), lambda bank: act.copy(xT[:, c, :], bank[:, :]))
                for c in range(CH):
                    drain(("qT", c), lambda bank: act.mul(qk[:, 0, c, :], bank[:, :], HD ** -0.25))
                for c in range(CH):
                    act.wait_ge(proj.drained(("qT", c)), proj.full(r, ("qT", c)))
                    act.activation(qk2[:, 0, c, :], qk[:, 0, c, :], ACT.Square).then_inc(square_ready.sem, 1)
                for i in range(G // 2):
                    drain(("v", i), lambda bank: act.copy(
                        v[:, 2 * i:2 * i + 2, :, 0:HD], bank[:, :].rearrange("p (t h d) -> p t h d", t=2, h=H)))
                for s in range(UNITS + 8):
                    if s < UNITS:
                        act.wait_ge(score.drained(s), score.full(r, s))
                        act.activation(f[:, s % 4, :, :], f[:, s % 4, :, :], ACT.Exp).then_inc(ex_ready.sem, 1)
                    u = s - 2
                    if 0 <= u < UNITS and u % 4 >= 2:
                        job = (f"q{u % 2}", u // 4)
                        act.wait_ge(mid.filled(job), mid.full(r, job))
                        act.copy(fT[:, u % 2, :], mid.bank(job)[:, :]).then_inc(mid.drained(job), 1)
                    if s >= 9 and (s - 9) % 4 == 0 and (s - 9) // 4 < G:
                        t = (s - 9) // 4
                        drain(("oT", t), lambda bank: act.copy(
                            oT[:, t % 2, :, :], bank[:, 0:D].rearrange("p (c k) -> p c k", c=CH)))

        @block.vector
        def _(dve):
            dve.wait_ge(loaded.sem, 96)
            dve.wait_ge(const_ready.sem, 3)
            with dve.Fori(1, GROUPS + 1, 1) as r:
                def drain(job, write):
                    dve.wait_ge(proj.filled(job), proj.full(r, job))
                    write(proj.bank(job)).then_inc(proj.drained(job), 1)

                for t in range(G):
                    dve.tensor_scalar(xn[:, t, :], st.x[:, seq(r, t)], mean[:, seq(r, t, 1)],
                                      rstd[:, seq(r, t, 1)], ALU.subtract, ALU.mult).then_inc(xn_ready.sem, 1)
                for c in range(CH):
                    drain(("kT", c), lambda bank: dve.tensor_scalar(qk[:, 1, c, :], bank[:, :], HD ** -0.25, None, ALU.mult))
                for c in range(CH):
                    dve.wait_ge(proj.drained(("kT", c)), proj.full(r, ("kT", c)))
                    dve.tensor_tensor(qk2[:, 1, c, :], qk[:, 1, c, :], qk[:, 1, c, :], ALU.mult).then_inc(square_ready.sem, 1)
                drain("squares", lambda bank: dve.tensor_copy(half2[:, :, :, :].rearrange("p t w h -> p (t w h)"), bank[:, 0:G * 2 * H]))
                dve.wait_ge(proj.drained("squares"), proj.full(r, "squares"))
                for s in range(UNITS + 8):
                    if s < UNITS:
                        t, w, c = s // 4, 1 - (s % 4) // 2, s % 2
                        dve.wait_ge(score.filled(s), score.full(r, s))
                        unit = score.bank(s)[:, :].rearrange("p (h m) -> p h m", h=HH)
                        dve.tensor_reduce(mx[:, s % 4, :], unit, AX.X, ALU.max).then_inc(mx_ready.sem, 1)
                        dve.wait_ge(mx_ready.sem, mx_ready.at(r, s + 1))
                        dve.tensor_tensor(off[:, s % 4, :], mx[:, s % 4, :], half2[:, t, w, c * HH:(c + 1) * HH], ALU.add).then_inc(off_ready.sem, 1)
                        dve.wait_ge(off_ready.sem, off_ready.at(r, s + 1))
                        dve.tensor_tensor(f[:, s % 4, :, :], unit, bc(off[:, s % 4, :, None], [P, HH, NF]),
                                          ALU.subtract).then_inc(score.drained(s), 1)
                    u = s - 2
                    if 0 <= u < UNITS and u % 4 == 1:
                        t = u // 4
                        job = ("kv", t)
                        dve.wait_ge(mid.filled(job), mid.full(r, job))
                        both = mid.bank(job)[:, 0:PAIRS * PW].rearrange("p (a k) -> p a k", a=PAIRS)
                        dve.tensor_copy(kv[0:NF, t % 2, :, 0:VW], both[0:NF, :, 0:VW]).then_inc(kv_half.sem, 1)
                        dve.tensor_copy(kv[NF:P, t % 2, :, VW:PW], both[NF:P, :, VW:PW]).then_inc(mid.drained(job), 1)
                    if s >= 7 and (s - 7) % 4 == 0 and (s - 7) // 4 < G:
                        t = (s - 7) // 4
                        dve.wait_ge(out.filled(t), out.full(r, t))
                        heads = out.bank(t)[:, 0:H * VW].rearrange("p (h d) -> p h d", h=H)
                        dve.reciprocal(rs[:, t % 2, :], heads[:, :, HD]).then_inc(rs_ready.sem, 1)
                        dve.wait_ge(rs_ready.sem, rs_ready.at(r, t + 1))
                        dve.tensor_tensor(o[:, t % 2, :].rearrange("p (h d) -> p h d", h=H), heads[:, :, 0:HD],
                                          bc(rs[:, t % 2, :, None], [P, H, HD]), ALU.mult).then_inc(out.drained(t), 1)
                    if s >= 11 and (s - 11) % 4 == 0 and (s - 11) // 4 < G:
                        t = (s - 11) // 4
                        rows.wait_slot(dve, r, t)
                        drain(("y", t), lambda bank: dve.tensor_tensor(rows.slot[:, t % 2, :], xn[:, t, :], bank[:, 0:D], ALU.add))
                        rows.take_stats(dve, r, t, proj.drained(("y", t)), proj.full(r, ("y", t)))


def mlp_phase(nc, st, io, ident, y):
    wide = [("xT", c) for c in range(CH)] + [("hT", k) for k in range(IC)]
    with ExitStack() as ctx:
        def sb(n, s, dt=F32):
            return ctx.enter_context(nc.sbuf_tensor(f"mlp_{n}", s, dt))

        def tally(n, per):
            return Tally(nc, f"mlp_{n}", per)

        w1, w2, b1 = sb("w1", [P, CH, INNER]), sb("w2", [P, IC, D]), sb("b1", [P, IC])
        g1, c1, g2, c2, b2 = (sb(n, [P, D]) for n in ("g1", "c1", "g2", "c2", "b2"))
        u = sb("u", [P, G, D])
        ub = sb("ub", [P, G, D])
        uT = sb("uT", [P, CH, G * S])
        hT = sb("hT", [P, IC, G * S])
        z = sb("z", [P, G, D])
        zraw, zmv = sb("zraw", [P, G, 6]), sb("zmv", [P, G, 2])
        zvar, zrstd, mhalf, eps = (sb(n, [P, G]) for n in ("zvar", "zrstd", "mhalf", "eps"))

        loaded = tally("weights_loaded", 0)
        const_ready = tally("const_ready", 0)
        u_step = tally("u_step", G + 1)
        u_ready = tally("u_ready", 1)
        ub_ready = tally("ub_ready", 1)
        zraw_ready = [tally(f"z_stats{t}", 1) for t in range(G)]
        zmv_ready = tally("z_aggr", G)
        zr_ready = tally("z_rstd_step", 2)
        zn_ready = tally("z_norm_step", G + 2)
        x_ready = tally("x_ready", G)
        rows = Rows(ctx, nc, "mlp", st.x, st.mean[st.now ^ 1], st.rstd[st.now ^ 1], EPS)
        hid = Ring(ctx, nc, "mlp_hid", 4, wide)
        outs = Ring(ctx, nc, "mlp_outs", 4, list(range(G)))
        block = ctx.enter_context(nc.Block())

        @block.sync
        def _(sp):
            sp.dma_start(w1[:, :, :], io["mlp_w1"].rearrange("(c p) o -> p c o", p=P)).then_inc(loaded.sem, 16)
            sp.dma_start(w2[:, :, :], io["mlp_w2"].rearrange("(c p) o -> p c o", p=P)).then_inc(loaded.sem, 16)
            sp.dma_start(b1[:, :], io["mlp_b1"]).then_inc(loaded.sem, 16)
            for tile, key in ((g1, "ln1_g"), (c1, "ln1_b"), (g2, "ln2_g"), (c2, "ln2_b"), (b2, "b2")):
                sp.dma_start(tile[:, :], io[f"mlp_{key}"].partition_broadcast(P)).then_inc(loaded.sem, 16)
            sp.wait_ge(loaded.sem, 128)

        @block.gpsimd
        def _(pool):
            rows.pool_start(pool)
            pool.memset(mhalf[:, :], -0.5).then_inc(const_ready.sem, 1)
            pool.memset(eps[:, :], EPS_IN).then_inc(const_ready.sem, 1)
            pool.wait_ge(loaded.sem, 128)
            pool.wait_ge(const_ready.sem, 2)
            with pool.Fori(1, GROUPS + 1, 1) as r:
                pool.wait_ge(u_ready.sem, u_ready.at(r, 1))
                pool.tensor_tensor(ub[:, :, :], u[:, :, :], bc(b2[:, None, :], [P, G, D]), ALU.add).then_inc(ub_ready.sem, 1)
                pool.wait_ge(zmv_ready.sem, zmv_ready.at(r, G))
                pool.tensor_tensor(zvar[:, :], zmv[:, :, 1], eps[:, :], ALU.add).then_inc(zr_ready.sem, 1)
                pool.wait_ge(zr_ready.sem, zr_ready.at(r, 1))
                pool.tensor_tensor(zrstd[:, :], zvar[:, :], mhalf[:, :], ALU.pow).then_inc(zr_ready.sem, 1)
                for t in range(G):
                    rows.store(pool, r, t)
                rows.store_stats(pool, r)

        @block.tensor
        def _(pe):
            pe.wait_ge(loaded.sem, 128)
            with pe.Fori(1, GROUPS + 1, 1) as r:
                pe.wait_ge(u_ready.sem, u_ready.at(r, 1))
                for c in range(CH):
                    job = ("xT", c)
                    pe.wait_ge(hid.drained(job), hid.free(r, job))
                    for t in range(G):
                        mm = pe.transpose(hid.bank(job)[:, t * P:(t + 1) * P], u[:, t, c * P:(c + 1) * P], ident[:, :])
                    mm.then_inc(hid.filled(job), 1)
                for c in range(CH):
                    pe.wait_ge(hid.drained(("xT", c)), hid.full(r, ("xT", c)))
                for i in range(IC):
                    job = ("hT", i)
                    pe.wait_ge(hid.drained(job), hid.free(r, job))
                    for k in range(CH):
                        mm = pe.matmul(hid.bank(job)[:, :], w1[:, k, i * P:(i + 1) * P], uT[:, k, :],
                                       start=(k == 0), stop=(k == CH - 1))
                    mm.then_inc(hid.filled(job), 1)
                for i in range(IC):
                    pe.wait_ge(hid.drained(("hT", i)), hid.full(r, ("hT", i)))
                for t in range(G):
                    pe.wait_ge(outs.drained(t), outs.free(r, t))
                    for i in range(IC):
                        mm = pe.matmul(outs.bank(t)[:, 0:D], hT[:, i, t * S:(t + 1) * S], w2[:, i, :],
                                       start=(i == 0), stop=(i == IC - 1))
                    mm.then_inc(outs.filled(t), 1)

        @block.scalar
        def _(act):
            act.wait_ge(loaded.sem, 128)
            with act.Fori(1, GROUPS + 1, 1) as r:
                for c in range(CH):
                    act.wait_ge(hid.filled(("xT", c)), hid.full(r, ("xT", c)))
                    act.copy(uT[:, c, :], hid.bank(("xT", c))[:, :]).then_inc(hid.drained(("xT", c)), 1)
                for i in range(IC):
                    if i == 0:
                        act.wait_ge(outs.filled(G - 1), outs.free(r, G - 1))
                    act.wait_ge(hid.filled(("hT", i)), hid.full(r, ("hT", i)))
                    act.activation(hT[:, i, :], hid.bank(("hT", i))[:, :], ACT.Gelu, bias=b1[:, i:i + 1]).then_inc(hid.drained(("hT", i)), 1)

        @block.vector
        def _(dve):
            dve.wait_ge(loaded.sem, 128)
            with dve.Fori(1, GROUPS + 1, 1) as r:
                for t in range(G):
                    dve.tensor_scalar(z[:, t, :], y[:, seq(r, t)], st.mean_in[:, seq(r, t, 1)],
                                      st.rstd_in[:, seq(r, t, 1)], ALU.subtract, ALU.mult).then_inc(u_step.sem, 1)
                dve.wait_ge(u_step.sem, u_step.at(r, G))
                dve.tensor_tensor(z[:, :, :], z[:, :, :], bc(g1[:, None, :], [P, G, D]), ALU.mult).then_inc(u_step.sem, 1)
                dve.wait_ge(u_step.sem, u_step.at(r, G + 1))
                dve.tensor_tensor(u[:, :, :], z[:, :, :], bc(c1[:, None, :], [P, G, D]), ALU.add).then_inc(u_ready.sem, 1)
                dve.wait_ge(ub_ready.sem, ub_ready.at(r, 1))
                for t in range(G):
                    dve.wait_ge(outs.filled(t), outs.full(r, t))
                    dve.tensor_tensor(ub[:, t, :], ub[:, t, :], outs.bank(t)[:, 0:D], ALU.add).then_inc(outs.drained(t), 1)
                    dve.wait_ge(outs.drained(t), outs.full(r, t))
                    dve.bn_stats(zraw[:, t, :], ub[:, t, :]).then_inc(zraw_ready[t].sem, 1)
                    dve.wait_ge(loaded.sem, 128)
                    dve.wait_ge(zraw_ready[t].sem, zraw_ready[t].at(r, 1))
                    dve.bn_aggr(zmv[:, t, :], zraw[:, t, :]).then_inc(zmv_ready.sem, 1)
                dve.wait_ge(zr_ready.sem, zr_ready.at(r, 2))
                for t in range(G):
                    dve.tensor_scalar(z[:, t, :], ub[:, t, :], zmv[:, t, 0:1], zrstd[:, t:t + 1],
                                      ALU.subtract, ALU.mult).then_inc(zn_ready.sem, 1)
                dve.wait_ge(zn_ready.sem, zn_ready.at(r, G))
                dve.tensor_tensor(z[:, :, :], z[:, :, :], bc(g2[:, None, :], [P, G, D]), ALU.mult).then_inc(zn_ready.sem, 1)
                dve.wait_ge(zn_ready.sem, zn_ready.at(r, G + 1))
                dve.tensor_tensor(z[:, :, :], z[:, :, :], bc(c2[:, None, :], [P, G, D]), ALU.add).then_inc(zn_ready.sem, 1)
                dve.wait_ge(zn_ready.sem, zn_ready.at(r, G + 2))
                for t in range(G):
                    rows.wait_slot(dve, r, t)
                    dve.tensor_tensor(rows.slot[:, t % 2, :], st.x[:, seq(r, t)], z[:, t, :], ALU.add).then_inc(x_ready.sem, 1)
                    rows.take_stats(dve, r, t, x_ready.sem, x_ready.at(r, t + 1))
    st.turn()


def experts_phase(nc, st, io, ident):
    mean, rstd = st.mean[st.now], st.rstd[st.now]
    with ExitStack() as ctx:
        xall = ctx.enter_context(nc.sbuf_tensor("moe_xT", [P, CH, B * S], F32))
        weight = ctx.enter_context(nc.sbuf_tensor("moe_weight", [P, B * E], F32))
        w1 = ctx.enter_context(nc.sbuf_tensor("moe_w1", [P, 2, CH, 2 * EI], F32))
        w2 = ctx.enter_context(nc.sbuf_tensor("moe_w2", [P, 2, EC, D], F32))
        w_loaded = [Tally(nc, f"moe_weights_loaded{b}", 32, 0) for b in range(2)]

        def load_expert(sp, b, e):
            sp.dma_start(w1[:, b, :, :], io["moe_w1"][e].rearrange("e (c p) o -> p (e c) o", p=P)).then_inc(w_loaded[b].sem, 16)
            sp.dma_start(w2[:, b, :, :], io["moe_w2"][e].rearrange("e (c p) o -> p (e c) o", p=P)).then_inc(w_loaded[b].sem, 16)

        with ExitStack() as ctx2:
            def sb(n, s, dt=F32):
                return ctx2.enter_context(nc.sbuf_tensor(f"route_{n}", s, dt))

            def tally(n, per):
                return Tally(nc, f"route_{n}", per)

            router, before = sb("router", [P, CH, E]), sb("before", [P, 1, E * E])
            xn, xT = sb("xn", [P, G, D]), sb("xT", [P, CH, G * S])
            top, total, recip = sb("top", [P, G]), sb("total", [P, G]), sb("recip", [P, G])
            prob = sb("prob", [P, G, E])
            above, tied = sb("above", [P, G, E, E]), sb("tied", [P, G, E, E])
            rank = sb("rank", [P, G, E])
            loaded = tally("weights_loaded", 0)
            xn_ready = tally("xn_ready", G)
            step = tally("step", 9)
            exp_ready = tally("exp_ready", 1)
            kept = tally("xT_kept", CH)
            ring = Ring(ctx2, nc, "route_ring", 3, [("xT", c) for c in range(CH)] + ["logits"])
            block = ctx2.enter_context(nc.Block())

            @block.sync
            def _(sp):
                sp.dma_start(router[:, :, :], io["router"].rearrange("(c p) e -> p c e", p=P)).then_inc(loaded.sem, 16)
                sp.dma_start(before[:, 0, :], io["before"]).then_inc(loaded.sem, 16)
                for b in range(2):
                    load_expert(sp, b, slice(b, b + 1))
                sp.wait_ge(loaded.sem, 32)

            @block.tensor
            def _(pe):
                pe.wait_ge(loaded.sem, 32)
                with pe.Fori(1, GROUPS + 1, 1) as r:
                    for c in range(CH):
                        pe.wait_ge(ring.drained(("xT", c)), ring.free(r, ("xT", c)))
                        for t in range(G):
                            pe.wait_ge(xn_ready.sem, xn_ready.at(r, t + 1))
                            mm = pe.transpose(ring.bank(("xT", c))[:, t * P:(t + 1) * P], xn[:, t, c * P:(c + 1) * P], ident[:, :])
                        mm.then_inc(ring.filled(("xT", c)), 1)
                    for c in range(CH):
                        pe.wait_ge(ring.drained(("xT", c)), ring.full(r, ("xT", c)))
                    pe.wait_ge(ring.drained("logits"), ring.free(r, "logits"))
                    for t in range(G):
                        for k in range(CH):
                            mm = pe.matmul(ring.bank("logits")[:, t * E:(t + 1) * E], xT[:, k, t * S:(t + 1) * S], router[:, k, :],
                                           start=(k == 0), stop=(k == CH - 1))
                    mm.then_inc(ring.filled("logits"), 1)

            @block.scalar
            def _(act):
                with act.Fori(1, GROUPS + 1, 1) as r:
                    for c in range(CH):
                        act.wait_ge(ring.filled(("xT", c)), ring.full(r, ("xT", c)))
                        act.wait_ge(kept.sem, kept.at(r, 0))
                        act.wait_ge(ring.filled("logits"), ring.free(r, "logits"))
                        act.copy(xT[:, c, :], ring.bank(("xT", c))[:, :]).then_inc(ring.drained(("xT", c)), 1)
                    act.wait_ge(step.sem, step.at(r, 2))
                    act.activation(prob[:, :, :], prob[:, :, :], ACT.Exp).then_inc(exp_ready.sem, 1)

            @block.gpsimd
            def _(pool):
                with pool.Fori(1, GROUPS + 1, 1) as r:
                    for c in range(CH):
                        pool.wait_ge(loaded.sem, 32)
                        pool.wait_ge(ring.drained(("xT", c)), ring.full(r, ("xT", c)))
                        pool.tensor_copy(xall[:, c, group(r, S)], xT[:, c, :]).then_inc(kept.sem, 1)

            @block.vector
            def _(dve):
                dve.wait_ge(loaded.sem, 32)
                with dve.Fori(1, GROUPS + 1, 1) as r:
                    for t in range(G):
                        dve.tensor_scalar(xn[:, t, :], st.x[:, seq(r, t)], mean[:, seq(r, t, 1)],
                                          rstd[:, seq(r, t, 1)], ALU.subtract, ALU.mult).then_inc(xn_ready.sem, 1)
                    logits = ring.bank("logits")[:, 0:G * E].rearrange("p (t e) -> p t e", e=E)
                    dve.wait_ge(ring.filled("logits"), ring.full(r, "logits"))
                    dve.tensor_reduce(top[:, :], logits, AX.X, ALU.max).then_inc(step.sem, 1)
                    dve.wait_ge(step.sem, step.at(r, 1))
                    dve.tensor_tensor(prob[:, :, :], logits, bc(top[:, :, None], [P, G, E]), ALU.subtract).then_inc(step.sem, 1)
                    dve.wait_ge(exp_ready.sem, exp_ready.at(r, 1))
                    dve.tensor_reduce(total[:, :], prob[:, :, :], AX.X, ALU.add).then_inc(ring.drained("logits"), 1)
                    dve.wait_ge(ring.drained("logits"), ring.full(r, "logits"))
                    dve.reciprocal(recip[:, :], total[:, :]).then_inc(step.sem, 1)
                    dve.wait_ge(step.sem, step.at(r, 3))
                    dve.tensor_tensor(prob[:, :, :], prob[:, :, :], bc(recip[:, :, None], [P, G, E]), ALU.mult).then_inc(step.sem, 1)
                    dve.wait_ge(step.sem, step.at(r, 4))
                    other, this = (bc(a, [P, G, E, E]) for a in (prob[:, :, None, :], prob[:, :, :, None]))
                    dve.tensor_tensor(above[:, :, :, :], other, this, ALU.is_gt).then_inc(step.sem, 1)
                    dve.tensor_tensor(tied[:, :, :, :], other, this, ALU.is_equal).then_inc(step.sem, 1)
                    flat_above, flat_tied = (a[:, :, :, :].rearrange("p t i j -> p t (i j)") for a in (above, tied))
                    dve.wait_ge(step.sem, step.at(r, 6))
                    dve.tensor_tensor(flat_tied, flat_tied, bc(before[:, :, :], [P, G, E * E]), ALU.mult).then_inc(step.sem, 1)
                    dve.wait_ge(step.sem, step.at(r, 7))
                    dve.tensor_tensor(flat_above, flat_above, flat_tied, ALU.add).then_inc(step.sem, 1)
                    dve.wait_ge(step.sem, step.at(r, 8))
                    dve.tensor_reduce(rank[:, :, :], above[:, :, :, :], AX.X, ALU.add).then_inc(step.sem, 1)
                    dve.wait_ge(step.sem, step.at(r, 9))
                    dve.scalar_tensor_tensor(weight[:, group(r, E)].rearrange("p (t e) -> p t e", e=E), rank[:, :, :], 2.0,
                                             prob[:, :, :], ALU.is_lt, ALU.mult)

        yT = ctx.enter_context(nc.sbuf_tensor("moe_yT", [P, 2, EC, G * S], F32))
        sg = ctx.enter_context(nc.sbuf_tensor("moe_silu", [P, 2, G * S], F32))
        TURNS = GROUPS // 2
        chunks = [(k, i) for k in range(2) for i in range(EC)]
        tiles = [(k, t) for k in range(2) for t in range(G)]
        gates = Ring(ctx, nc, "moe_gates", 2, chunks)
        ups = Ring(ctx, nc, "moe_ups", 2, chunks)
        outs = Ring(ctx, nc, "moe_outs", 4, tiles)
        block = ctx.enter_context(nc.Block())

        @block.sync
        def _(sp):
            with sp.Fori(1, E // 2, 1) as q:
                for b in range(2):
                    turn = (q * 2 + b) * TURNS - TURNS
                    sp.wait_ge(outs.filled(tiles[-1]), outs.full(turn, tiles[-1]))
                    load_expert(sp, b, bass.ds(q * 2 + b, 1))
            for b in range(2):
                sp.wait_ge(w_loaded[b].sem, w_loaded[b].at(E // 2, 0))

        @block.tensor
        def _(pe):
            with pe.Fori(0, E // 2, 1) as q:
                for b in range(2):
                    with pe.Fori(1, TURNS + 1, 1) as g:
                        r = (q * 2 + b) * TURNS + g
                        pe.wait_ge(w_loaded[b].sem, w_loaded[b].at(q + 1, 0))
                        for k, i in chunks:
                            tokens = [xall[:, c, bass.ds(g * (2 * G * S) + (k - 2) * G * S, G * S)] for c in range(CH)]
                            for ring, col in ((gates, i * P), (ups, EI + i * P)):
                                pe.wait_ge(ring.drained((k, i)), ring.free(r, (k, i)))
                                for c in range(CH):
                                    mm = pe.matmul(ring.bank((k, i))[:, :], w1[:, b, c, col:col + P], tokens[c],
                                                   start=(c == 0), stop=(c == CH - 1))
                                mm.then_inc(ring.filled((k, i)), 1)
                        for k, t in tiles:
                            if t == 0:
                                for i in (EC - 2, EC - 1):
                                    pe.wait_ge(ups.drained((k, i)), ups.full(r, (k, i)))
                            pe.wait_ge(outs.drained((k, t)), outs.free(r, (k, t)))
                            for i in range(EC):
                                mm = pe.matmul(outs.bank((k, t))[:, 0:D], yT[:, k, i, t * S:(t + 1) * S], w2[:, b, i, :],
                                               start=(i == 0), stop=(i == EC - 1))
                            mm.then_inc(outs.filled((k, t)), 1)

        @block.scalar
        def _(act):
            with act.Fori(1, E * TURNS + 1, 1) as r:
                for n, (k, i) in enumerate(chunks):
                    act.wait_ge(gates.filled((k, i)), gates.full(r, (k, i)))
                    if n >= 2:
                        act.wait_ge(ups.drained(chunks[n - 2]), ups.full(r, chunks[n - 2]))
                    else:
                        act.wait_ge(ups.drained(chunks[n]), ups.free(r, chunks[n]))
                    act.activation(sg[:, n % 2, :], gates.bank((k, i))[:, :], ACT.Silu).then_inc(gates.drained((k, i)), 1)

        @block.vector
        def _(dve):
            with dve.Fori(0, E, 1) as e:
                with dve.Fori(1, TURNS + 1, 1) as g:
                    r = e * TURNS + g
                    for n, (k, i) in enumerate(chunks):
                        dve.wait_ge(ups.filled((k, i)), ups.full(r, (k, i)))
                        dve.wait_ge(gates.drained((k, i)), gates.full(r, (k, i)))
                        dve.tensor_tensor(yT[:, k, i, :], sg[:, n % 2, :], ups.bank((k, i))[:, :], ALU.mult).then_inc(ups.drained((k, i)), 1)
                    for k, t in tiles:
                        row = g * (2 * G) + (k - 2) * G + t
                        dve.wait_ge(outs.drained((k, t)), outs.free(r, (k, t)))
                        dve.wait_ge(outs.filled((k, t)), outs.full(r, (k, t)))
                        here = st.x[:, bass.ds(row * D, D)]
                        dve.scalar_tensor_tensor(here, outs.bank((k, t))[:, 0:D], weight[:, bass.ds(row * E + e, 1)], here,
                                                 ALU.mult, ALU.add).then_inc(outs.drained((k, t)), 1)


def program(nc, io, out, phases=(0, 6)):
    with ExitStack() as ctx:
        ident = ctx.enter_context(nc.sbuf_tensor("ident", [P, P], F32))
        st = Stream(ctx, nc)
        load_phase(nc, st, io, ident)
        every = [lambda: attention_phase(nc, st, io, ident, "self", "self"),
                 lambda: attention_phase(nc, st, io, ident, "mask", "masked"),
                 lambda: bitlinear_phase(nc, st, io, ident),
                 lambda: second_layer_self(nc, st, io, ident),
                 lambda: attention_phase(nc, st, io, ident, "cross", "cross"),
                 lambda: experts_phase(nc, st, io, ident)]
        for phase in every[phases[0]:phases[1]]:
            with nc.cleanup_on_exit():
                phase()
        store_phase(nc, st, out)


def store_phase(nc, st, out):
    with ExitStack() as ctx:
        stored = Tally(nc, "stored", 0)
        block = ctx.enter_context(nc.Block())

        @block.sync
        def _(sp):
            sp.dma_start(out.rearrange("(n p) d -> p n d", p=P), st.x[:, :].rearrange("p (n d) -> p n d", n=B)).then_inc(stored.sem, 16)
            sp.wait_ge(stored.sem, 16)


def tables():
    bf16 = mybir.dt.np(BF16)
    pos = np.arange(NC + GS, dtype=np.float32)[:, None]
    div = np.exp(np.arange(0, HD, 2, dtype=np.float32) * np.float32(-np.log(10000.0) / HD))
    ang = (pos * div).astype(np.float32)
    pe = np.stack([np.sin(ang), np.cos(ang)], axis=-1).reshape(NC + GS, HD)
    rot = np.empty((HD, NC + GS), np.float32)
    rot[0::2] = -pe[:, HD // 2:].T
    rot[1::2] = pe[:, :HD // 2].T
    rows = np.tile(rot, (HH, 1))
    heads = np.repeat(np.eye(HH, dtype=np.float32), HD, axis=0)
    local = np.arange(GS)
    q_pos = np.concatenate([local, local])
    k_pos = np.concatenate([local, NC + local, np.arange(NC)])
    rot_k = heads[:, :, None] * rows[:, None, k_pos]
    seen = np.zeros((P, UH, KL), np.float32)
    seen[:, :, 0:GS] = (local[None, :] <= (np.arange(P) % GS)[:, None])[:, None, :]
    seen[GS:, :, GS:] = 1.0
    parts, rest = np.zeros((P, 1), np.float32), np.float64(-MASK_FILL)
    for i in range(3):
        parts[i] = np.float32(np.float64(rest).astype(bf16))
        rest -= np.float64(parts[i, 0])
    assert rest == 0
    return {
        "ident": np.eye(P, dtype=np.float32),
        "identb": np.eye(P, dtype=np.float32).astype(bf16),
        "rot_q": rows[:, q_pos], "rot_k": rot_k, "heads": heads, "parts": parts,
        "half_heads": 0.5 * heads, "before": np.tile(np.tril(np.ones((E, E), np.float32), -1).reshape(1, -1), (P, 1)),
        "causal": np.where(seen > 0, 0.0, -1e30).astype(bf16),
    }


def chunked(vec):
    return vec.reshape(-1, P).T


def layout(a):
    swap = np.arange(D).reshape(-1, 2)[:, ::-1].reshape(-1)
    io = dict(tables())
    io["x"] = a["x"].reshape(B * S, D)
    io["ctx"] = a["ctx_1024"].reshape(B * S, D)
    mask = a["mask_BxS2_bf1"].reshape(GROUPS, G * S).view(np.uint8)
    io["mask"] = np.concatenate([mask[:1], mask])
    w, b = a["L0_attn_w_attn"], a["L0_attn_b_attn"]
    io["self_wq"], io["self_wk"], io["self_wv"] = w[0:D][swap].T, w[D:2 * D][swap].T, w[2 * D:].T
    io["self_bq"], io["self_bk"], io["self_bv"] = chunked(b[0:D][swap]), chunked(b[D:2 * D][swap]), b[2 * D:]
    io["self_wo"], io["self_bo"] = a["L0_attn_w_proj"].T, a["L0_attn_b_proj"]
    io["self_assign"] = np.repeat(a["L0_attn_w_assign"][0:NC], 2, axis=0).T
    for n in "qkvo":
        io[f"mask_w{n}"] = a[f"L0_xattn_W{n}"].T
        io[f"cross_w{n}"] = a[f"L1_xattn_w_{n}"].T
    io["mask_bq"], io["mask_bk"] = chunked(a["L0_xattn_bq"]), chunked(a["L0_xattn_bk"])
    for n in ("gate", "up", "down"):
        io[f"bit_{n}"] = a[f"L0_ffn_w_{n}"].T
    io["perf_wq"], io["perf_wk"], io["perf_wv"] = (a[f"L1_attn_w{n}"].reshape(D, D) for n in "qkv")
    io["perf_wo"] = a["L1_attn_wo"]
    omega = np.zeros((HH, HD, HH, NF), np.float32)
    for h in range(HH):
        omega[h, :, h, :] = a["L1_attn_omega"].T
    io["omega"] = omega.reshape(P, HH * NF)
    for n in ("ln1_g", "ln1_b", "ln2_g", "ln2_b", "b2"):
        io[f"mlp_{n}"] = a[f"L1_attn_{n}"]
    io["mlp_w1"], io["mlp_w2"], io["mlp_b1"] = a["L1_attn_w1"], a["L1_attn_w2"], chunked(a["L1_attn_b1"])
    io["moe_w1"] = a["L1_ffn_w1"].transpose(0, 2, 1)
    io["moe_w2"] = a["L1_ffn_w2"].transpose(0, 2, 1)
    io["router"] = a["L1_ffn_router_w"].T
    io["mask_bv"], io["mask_bo"] = a["L0_xattn_bv"], a["L0_xattn_bo"]
    return io


def kernel(**inputs):
    import concourse.bacc as bacc
    from concourse.bass_utils import run_bass_kernel_spmd

    arrays = {n: np.ascontiguousarray(v) for n, v in layout({n: np.asarray(v) for n, v in inputs.items()}).items()}
    nc = bacc.Bacc("TRN2", target_bir_lowering=False, num_devices=1)
    io = {n: nc.dram_tensor(f"in_{n}", v.shape, mybir.dt.from_np(v.dtype), kind="ExternalInput").ap()
          for n, v in arrays.items()}
    out = nc.dram_tensor("out_0", (B * S, D), F32, kind="ExternalOutput").ap()
    program(nc, io, out)
    got = run_bass_kernel_spmd(nc, [{f"in_{n}": v for n, v in arrays.items()}], core_ids=[0])
    return got.results[0]["out_0"].reshape(B, S, D)
```

```python
from contextlib import ExitStack

import numpy as np

import concourse.bass as bass
import concourse.mybir as mybir

F32 = mybir.dt.float32
BF16 = mybir.dt.bfloat16
U8 = mybir.dt.uint8
I32 = mybir.dt.int32
ALU = mybir.AluOpType
ACT = mybir.ActivationFunctionType
AX = mybir.AxisListType

P = 128
B, S, D = 32, 128, 256
CH = D // P
H, HD = 16, 16
HH = H // CH
VW = HD + 1
G = 4
GROUPS = B // G
UH = 4
UNITS = G * H // UH
NC = 32
GS = 64
KS = S + NC
KL = GS + NC
EPS = 1e-5
EPS_IN = 1e-6
ROUND = 1.5 * 2.0**23
MASK_FILL = -1e8
INNER = 1024
IC = INNER // P
NF = 64
E, EI = 8, 512
EC = EI // P
TILES = (2 * B * S + E * (P - 1)) // P


class Tally:

    def __init__(self, nc, name, per_turn, start=None):
        self.sem = nc.alloc_semaphore(name)
        self.per_turn = per_turn
        if per_turn and start is None:
            nc.gpsimd.sem_inc(self.sem, per_turn)

    def at(self, r, k):
        return r * self.per_turn + k


class Ring:

    def __init__(self, ctx, nc, name, banks, jobs):
        self.banks = [ctx.enter_context(nc.psum_tensor(f"{name}_bank{b}", [P, 512], F32)) for b in range(banks)]
        self._filled = [nc.alloc_semaphore(f"{name}_filled{b}") for b in range(banks)]
        self._drained = [nc.alloc_semaphore(f"{name}_drained{b}") for b in range(banks)]
        self.place = {job: (i % banks, i // banks) for i, job in enumerate(jobs)}
        self.uses = [len(jobs[b::banks]) for b in range(banks)]
        for b in range(banks):
            for sem in (self._filled[b], self._drained[b]):
                nc.gpsimd.sem_inc(sem, self.uses[b])

    def bank(self, job):
        return self.banks[self.place[job][0]]

    def filled(self, job):
        return self._filled[self.place[job][0]]

    def drained(self, job):
        return self._drained[self.place[job][0]]

    def full(self, r, job):
        b, turn = self.place[job]
        return r * self.uses[b] + turn + 1

    def free(self, r, job):
        b, turn = self.place[job]
        return r * self.uses[b] + turn


def bc(ap, shape):
    return ap.to_broadcast(shape)


class Stream:

    def __init__(self, ctx, nc):
        def sb(n, s):
            return ctx.enter_context(nc.sbuf_tensor(n, s, F32))
        self.x = sb("stream", [P, B * D])
        self.mean = [sb(f"mean{i}", [P, B]) for i in range(2)]
        self.rstd = [sb(f"rstd{i}", [P, B]) for i in range(2)]
        self.mean_in, self.rstd_in = sb("mean_in", [P, B]), sb("rstd_in", [P, B])
        self.now = 0

    def turn(self):
        self.now ^= 1


def seq(r, t, width=D):
    return bass.ds(r * (G * width) + (t - G) * width, width)


def group(r, width):
    return bass.ds(r * (G * width) - G * width, G * width)


class Rows:

    def __init__(self, ctx, nc, name, dest, mean, rstd, eps):
        def sb(n, s):
            return ctx.enter_context(nc.sbuf_tensor(f"{name}_{n}", s, F32))

        self.dest, self.mean, self.rstd, self.eps = dest, mean, rstd, eps
        self.slot = sb("rows", [P, 2, D])
        self.raw = sb("rows_raw", [P, 2, 6])
        self.mv = sb("rows_mean_var", [P, G, 2])
        self.var = sb("rows_var", [P, G])
        self.mhalf = sb("rows_mhalf", [P, G])
        self.const_ready = Tally(nc, f"{name}_mhalf_ready", 0)
        self.stored = Tally(nc, f"{name}_rows_stored", G)
        self.raw_ready = Tally(nc, f"{name}_rows_stats", G)
        self.aggr_ready = Tally(nc, f"{name}_rows_aggr", G)
        self.mean_stored = Tally(nc, f"{name}_mean_stored", 1)
        self.var_ready = Tally(nc, f"{name}_rstd_step", 2)

    def pool_start(self, pool):
        pool.memset(self.mhalf[:, :], -0.5).then_inc(self.const_ready.sem, 1)
        pool.wait_ge(self.const_ready.sem, 1)

    def wait_slot(self, dve, r, t):
        dve.wait_ge(self.stored.sem, self.stored.at(r, t - 1 if t >= 2 else 0))

    def take_stats(self, dve, r, t, written, count):
        dve.wait_ge(written, count)
        dve.bn_stats(self.raw[:, t % 2, :], self.slot[:, t % 2, :]).then_inc(self.raw_ready.sem, 1)
        dve.wait_ge(self.const_ready.sem, 1)
        dve.wait_ge(self.raw_ready.sem, self.raw_ready.at(r, t + 1))
        if t == 0:
            dve.wait_ge(self.mean_stored.sem, self.mean_stored.at(r, 0))
            dve.wait_ge(self.var_ready.sem, self.var_ready.at(r, 0))
        dve.bn_aggr(self.mv[:, t, :], self.raw[:, t % 2, :]).then_inc(self.aggr_ready.sem, 1)

    def store(self, pool, r, t):
        pool.wait_ge(self.const_ready.sem, 1)
        pool.wait_ge(self.raw_ready.sem, self.raw_ready.at(r, t + 1))
        pool.tensor_copy(self.dest[:, seq(r, t)], self.slot[:, t % 2, :]).then_inc(self.stored.sem, 1)

    def store_stats(self, pool, r):
        pool.wait_ge(self.const_ready.sem, 1)
        pool.wait_ge(self.aggr_ready.sem, self.aggr_ready.at(r, G))
        pool.tensor_copy(self.mean[:, group(r, 1)], self.mv[:, :, 0]).then_inc(self.mean_stored.sem, 1)
        pool.tensor_scalar(self.var[:, :], self.mv[:, :, 1], self.eps, None, ALU.add).then_inc(self.var_ready.sem, 1)
        pool.wait_ge(self.const_ready.sem, 1)
        pool.wait_ge(self.var_ready.sem, self.var_ready.at(r, 1))
        pool.tensor_tensor(self.rstd[:, group(r, 1)], self.var[:, :], self.mhalf[:, :], ALU.pow).then_inc(self.var_ready.sem, 1)


def load_phase(nc, st, io, ident):
    with ExitStack() as ctx:
        x_loaded = Tally(nc, "ld_x_loaded", 0)
        const_loaded = Tally(nc, "ld_const_loaded", 0)
        stats_ready = Tally(nc, "ld_stats_ready", 0)
        half_ready = Tally(nc, "ld_half_ready", 0)
        aggr_ready = Tally(nc, "ld_aggr_ready", 0)
        var_ready = Tally(nc, "ld_var_ready", 0)
        raw = ctx.enter_context(nc.sbuf_tensor("ld_raw", [P, B, 6], F32))
        mv = ctx.enter_context(nc.sbuf_tensor("ld_mv", [P, B, 2], F32))
        var = ctx.enter_context(nc.sbuf_tensor("ld_var", [P, B], F32))
        mhalf = ctx.enter_context(nc.sbuf_tensor("ld_mhalf", [P, B], F32))
        block = ctx.enter_context(nc.Block())

        @block.sync
        def _(sp):
            for q in range(4):
                n = B // 4
                sp.dma_start(st.x[:, q * n * D:(q + 1) * n * D].rearrange("p (n d) -> p n d", n=n),
                             io["x"].rearrange("(n p) d -> p n d", p=P)[:, q * n:(q + 1) * n, :]).then_inc(x_loaded.sem, 16)
            sp.dma_start(ident[:, :], io["ident"]).then_inc(const_loaded.sem, 16)
            sp.wait_ge(const_loaded.sem, 16)

        @block.vector
        def _(dve):
            dve.wait_ge(x_loaded.sem, 64)
            for b in range(B):
                dve.bn_stats(raw[:, b, :], st.x[:, b * D:(b + 1) * D]).then_inc(stats_ready.sem, 1)
            dve.wait_ge(stats_ready.sem, B)
            for b in range(B):
                dve.bn_aggr(mv[:, b, :], raw[:, b, :]).then_inc(aggr_ready.sem, 1)

        @block.gpsimd
        def _(pool):
            pool.memset(mhalf[:, :], -0.5).then_inc(half_ready.sem, 1)
            pool.wait_ge(aggr_ready.sem, B)
            pool.tensor_copy(st.mean[0][:, :], mv[:, :, 0])
            pool.tensor_scalar(var[:, :], mv[:, :, 1], EPS, None, ALU.add).then_inc(var_ready.sem, 1)
            pool.wait_ge(var_ready.sem, 1)
            pool.wait_ge(half_ready.sem, 1)
            pool.tensor_tensor(st.rstd[0][:, :], var[:, :], mhalf[:, :], ALU.pow).then_inc(var_ready.sem, 1)


def attention_phase(nc, st, io, ident, name, kind):
    own = kind == "self"
    biased = kind != "cross"
    KC = KS if own else S
    KU = KL if own else S
    VR = KL if own else S
    VG = 2 if own else 1
    mean, rstd = st.mean[st.now], st.rstd[st.now]
    mean_next, rstd_next = st.mean[st.now ^ 1], st.rstd[st.now ^ 1]

    if own:
        jobs = ([("xT", c) for c in range(CH)] + [("qT", c) for c in range(CH)] + ["logits"]
                + [("kT", c, i) for c in range(CH) for i in range(2)] + [("v", t) for t in range(G)])
    else:
        jobs = ([("xT", c) for c in range(CH)] + [("cT", c) for c in range(CH)]
                + [("qT", c) for c in range(CH)] + [("kT", c) for c in range(CH)]
                + [("v", i) for i in range(G // 2)])
    jobs += [(what, t) for t in range(G) for what in ("oT", "y")]

    with ExitStack() as ctx:
        def sb(n, s, dt=F32):
            return ctx.enter_context(nc.sbuf_tensor(f"{name}_{n}", s, dt))

        def tally(n, per, start=None):
            return Tally(nc, f"{name}_{n}", per, start)

        wq, wk, wv, wo = (sb(n, [P, CH, D]) for n in ("wq", "wk", "wv", "wo"))
        if biased:
            bq, bk = sb("bq", [P, CH]), sb("bk", [P, CH])
            bv, bo = sb("bv", [P, D]), sb("bo", [P, D])
        if own:
            assign = sb("assign", [P, CH, GS])
            rot_q = sb("rot_q", [P, S])
            spread = sb("spread", [P, HH, KS])
            causal = sb("causal", [P, UH, KL], BF16)
            identb = sb("identb", [P, P], BF16)
            ones = sb("ones", [P, P])
            prod = sb("prod", [P, CH, G, GS])
            expo = sb("expo", [P, G, GS])
            pair = sb("pair", [P, G * GS // 2])
            wts = sb("wts", [P, G, GS])
        else:
            spread = sb("spread", [P, HH])
            cin = sb("cin", [P, G, D])
            cT = sb("cT", [P, CH, G * S])
        if kind == "masked":
            mrow = sb("mrow", [P, G * S], U8)
            mask = sb("mask", [P, G * S])
            fill = sb("fill", [P, G, 1, S], BF16)
            parts = sb("parts", [P, 1])
            onesb = sb("onesb", [P, P], BF16)
        xn = sb("xn", [P, G, D])
        xT = sb("xT", [P, CH, G, KC])
        qT = sb("qT", [P, CH, G * S])
        kT = sb("kT", [P, CH, G, KC])
        KB = 4
        kbd = sb("kbd", [P, KB, HH, KC])
        v = sb("v", [VR, G, VG, H, VW])
        sc = sb("sc", [P, 4, UH, KU])
        mx = sb("mx", [P, 4, UH])
        pT = sb("pT", [VR, 2, UH * S])
        rs = sb("rs", [P, 2, H])
        o = sb("o", [P, 2, D])
        oT = sb("oT", [P, 2, CH, P])

        loaded = tally("weights_loaded", 0)
        ctx_loaded = tally("context_loaded", 32 if kind == "masked" else 16, 0)
        const_ready = tally("const_ready", 0)
        xn_ready = tally("xn_ready", G)
        mask_ready = tally("mask_ready", 2)
        prod_ready = tally("prod_ready", CH)
        v_step = tally("v_step", 3 * G)
        cl_ready = tally("cluster_step", 6)
        expo_ready = tally("cluster_exp_ready", 1)
        xc_ready = tally("clusters_ready", CH)
        kbd_ready = tally("kbd_ready", 2 * G)
        mx_ready = tally("rowmax_ready", UNITS)
        ex_ready = tally("exp_ready", UNITS)
        rs_ready = tally("recip_ready", G)
        xb_ready = tally("bias_added", G)
        rows = Rows(ctx, nc, name, st.x, mean_next, rstd_next, EPS)
        proj = Ring(ctx, nc, f"{name}_proj", 2, jobs)
        score = Ring(ctx, nc, f"{name}_score", 2, list(range(UNITS)))
        turned = Ring(ctx, nc, f"{name}_turned", 2, list(range(UNITS)))
        out = Ring(ctx, nc, f"{name}_out", 2, list(range(G)))
        n_const = 4 + (4 if biased else 0) + (5 if own else 1) + (1 if kind == "masked" else 0)
        block = ctx.enter_context(nc.Block())

        @block.sync
        def _(sp):
            for tile, key in ((wq, "wq"), (wk, "wk"), (wv, "wv"), (wo, "wo")):
                sp.dma_start(tile[:, :, :], io[f"{name}_{key}"].rearrange("(c p) o -> p c o", p=P)).then_inc(loaded.sem, 16)
            if biased:
                for tile, key in ((bq, "bq"), (bk, "bk")):
                    sp.dma_start(tile[:, :], io[f"{name}_{key}"]).then_inc(loaded.sem, 16)
                for tile, key in ((bv, "bv"), (bo, "bo")):
                    sp.dma_start(tile[:, :], io[f"{name}_{key}"].partition_broadcast(P)).then_inc(loaded.sem, 16)
            if own:
                sp.dma_start(assign[:, :, :], io[f"{name}_assign"].rearrange("(c p) o -> p c o", p=P)).then_inc(loaded.sem, 16)
                sp.dma_start(rot_q[:, :], io["rot_q"]).then_inc(loaded.sem, 16)
                sp.dma_start(spread[:, :, :], io["rot_k"]).then_inc(loaded.sem, 16)
                sp.dma_start(causal[:, :, :], io["causal"]).then_inc(loaded.sem, 16)
                sp.dma_start(identb[:, :], io["identb"]).then_inc(loaded.sem, 16)
            else:
                sp.dma_start(spread[:, :], io["heads"]).then_inc(loaded.sem, 16)
                if kind == "masked":
                    sp.dma_start(parts[:, :], io["parts"]).then_inc(loaded.sem, 16)
                context = io["ctx"].rearrange("(n p) d -> p n d", p=P)
                sp.dma_start(cin[:, :, :], context[:, 0:G, :]).then_inc(ctx_loaded.sem, 16)
                if kind == "masked":
                    sp.dma_start(mrow[:, :], io["mask"][1, :].partition_broadcast(P)).then_inc(ctx_loaded.sem, 16)
                with sp.Fori(1, GROUPS, 1) as r:
                    sp.wait_ge(proj.filled(("cT", CH - 1)), proj.full(r, ("cT", CH - 1)))
                    sp.dma_start(cin[:, :, :], context[:, bass.ds(r * G, G), :]).then_inc(ctx_loaded.sem, 16)
                    if kind == "masked":
                        sp.wait_ge(mask_ready.sem, mask_ready.at(r, 1))
                        sp.dma_start(mrow[:, :].rearrange("p (a k) -> p a k", a=1),
                                     io["mask"][bass.ds(r + 1, 1), :].partition_broadcast(P)).then_inc(ctx_loaded.sem, 16)
            sp.wait_ge(loaded.sem, 16 * n_const)

        @block.gpsimd
        def _(pool):
            rows.pool_start(pool)
            pool.memset(v[:, :, :, :, HD:VW], 1.0).then_inc(const_ready.sem, 1)
            if own:
                pool.memset(ones[:, :], 1.0).then_inc(const_ready.sem, 1)
            elif kind == "masked":
                pool.memset(onesb[:, :], 1.0).then_inc(const_ready.sem, 1)
            pool.wait_ge(loaded.sem, 16 * n_const)

            with pool.Fori(1, GROUPS + 1, 1) as r:
                if biased:
                    for t in range(G):
                        pool.wait_ge(xn_ready.sem, xn_ready.at(r, t + 1))
                        pool.tensor_tensor(st.x[:, seq(r, t)], st.x[:, seq(r, t)], bo[:, :], ALU.add).then_inc(xb_ready.sem, 1)
                for j in range(2 * G):
                    t, c = j // 2, j % 2
                    job = ("kT", c, t // 2) if own else ("kT", c)
                    pool.wait_ge(proj.drained(job), proj.full(r, job))
                    table = spread[:, :, :] if own else bc(spread[:, :, None], [P, HH, KC])
                    if j >= KB:
                        u = 2 * (j - KB) + 1
                        pool.wait_ge(score.filled(u), score.full(r, u))
                    else:
                        pool.wait_ge(score.filled(1), score.free(r, 1))
                    pool.tensor_tensor(kbd[:, j % KB, :, :], bc(kT[:, c, t, :][:, None, :], [P, HH, KC]),
                                       table, ALU.mult).then_inc(kbd_ready.sem, 1)
                for t in range(G):
                    rows.store(pool, r, t)
                rows.store_stats(pool, r)

        @block.tensor
        def _(pe):
            pe.wait_ge(loaded.sem, 16 * n_const)
            pe.wait_ge(const_ready.sem, 2 if own or kind == "masked" else 1)

            def wait_copied(r, jobs):
                for job in jobs:
                    pe.wait_ge(proj.drained(job), proj.full(r, job))

            def project(r, job, weights, c, moving):
                pe.wait_ge(proj.drained(job), proj.free(r, job))
                n = moving[0].free_size()
                for k in range(CH):
                    mm = pe.matmul(proj.bank(job)[:, 0:n], weights[:, k, c * P:(c + 1) * P], moving[k],
                                   start=(k == 0), stop=(k == CH - 1))
                mm.then_inc(proj.filled(job), 1)

            with pe.Fori(1, GROUPS + 1, 1) as r:
                for c in range(CH):
                    pe.wait_ge(proj.drained(("xT", c)), proj.free(r, ("xT", c)))
                    for t in range(G):
                        pe.wait_ge(xn_ready.sem, xn_ready.at(r, t + 1))
                        mm = pe.transpose(proj.bank(("xT", c))[:, t * P:(t + 1) * P], xn[:, t, c * P:(c + 1) * P], ident[:, :])
                    mm.then_inc(proj.filled(("xT", c)), 1)
                if own:
                    wait_copied(r, [("xT", c) for c in range(CH)])
                    for c in range(CH):
                        project(r, ("qT", c), wq, c, [xT[:, k, :, 0:S] for k in range(CH)])
                    pe.wait_ge(prod_ready.sem, prod_ready.at(r, CH))
                    pe.wait_ge(proj.drained("logits"), proj.free(r, "logits"))
                    for k in range(CH):
                        mm = pe.matmul(proj.bank("logits")[:, 0:G * GS], ones[:, :], prod[:, k, :, :],
                                       start=(k == 0), stop=(k == CH - 1))
                    mm.then_inc(proj.filled("logits"), 1)
                    pe.wait_ge(xc_ready.sem, xc_ready.at(r, CH))
                    for c in range(CH):
                        for i in range(2):
                            project(r, ("kT", c, i), wk, c, [xT[:, k, 2 * i:2 * i + 2, :] for k in range(CH)])
                    for t in range(G):
                        pe.wait_ge(proj.drained(("v", t)), proj.free(r, ("v", t)))
                        for rows, at, n in ((0, 0, GS), (0, GS, GS), (GS, S, NC)):
                            col = D if at == GS else 0
                            for k in range(CH):
                                mm = pe.matmul(proj.bank(("v", t))[rows:rows + n, col:col + D], xT[:, k, t, at:at + n],
                                               wv[:, k, :], start=(k == 0), stop=(k == CH - 1))
                        mm.then_inc(proj.filled(("v", t)), 1)
                else:
                    pe.wait_ge(ctx_loaded.sem, ctx_loaded.at(r, 0))
                    for c in range(CH):
                        pe.wait_ge(proj.drained(("cT", c)), proj.free(r, ("cT", c)))
                        for t in range(G):
                            mm = pe.transpose(proj.bank(("cT", c))[:, t * P:(t + 1) * P], cin[:, t, c * P:(c + 1) * P], ident[:, :])
                        mm.then_inc(proj.filled(("cT", c)), 1)
                    wait_copied(r, [("xT", c) for c in range(CH)])
                    for c in range(CH):
                        project(r, ("qT", c), wq, c, [xT[:, k, :, :] for k in range(CH)])
                    wait_copied(r, [("cT", c) for c in range(CH)])
                    for c in range(CH):
                        project(r, ("kT", c), wk, c, [cT[:, k, :] for k in range(CH)])
                    for i in range(G // 2):
                        pe.wait_ge(proj.drained(("v", i)), proj.free(r, ("v", i)))
                        for t in (2 * i, 2 * i + 1):
                            for k in range(CH):
                                mm = pe.matmul(proj.bank(("v", i))[:, (t % 2) * D:(t % 2 + 1) * D], cT[:, k, t * P:(t + 1) * P],
                                               wv[:, k, :], start=(k == 0), stop=(k == CH - 1))
                        mm.then_inc(proj.filled(("v", i)), 1)
                if kind == "masked":
                    pe.wait_ge(mask_ready.sem, mask_ready.at(r, 2))
                wait_copied(r, [("qT", c) for c in range(CH)])

                def scores(u):
                    t, g = u // 4, u % 4
                    c, half = g // 2, g % 2
                    bank = score.bank(u)
                    pe.wait_ge(score.drained(u), score.free(r, u))
                    if half == 0:
                        pe.wait_ge(kbd_ready.sem, kbd_ready.at(r, u // 2 + 1))
                    keys = kbd[:, (u // 2) % KB, half * UH:(half + 1) * UH, :]
                    if own:
                        view = bank[:, 0:UH * KL].rearrange("p (h k) -> p h k", h=UH)
                        pe.matmul(bank[:, 0:UH * KL], identb[:, :], causal[:, :, :], start=True, stop=False, skip_group_check=True)
                        pe.matmul(view[0:GS, :, 0:GS], qT[:, c, t * S:t * S + GS], keys[:, :, 0:GS],
                                  start=False, stop=True, skip_group_check=True)
                        mm = pe.matmul(view[GS:S, :, :], qT[:, c, t * S + GS:(t + 1) * S], keys[:, :, GS:KS],
                                       start=False, stop=True, skip_group_check=True)
                    elif kind == "masked":
                        pe.matmul(bank[:, :], onesb[:, :], bc(fill[:, t, :, :], [P, UH, S]), start=True, stop=False)
                        mm = pe.matmul(bank[:, :], qT[:, c, t * S:(t + 1) * S], keys, start=False, stop=True)
                    else:
                        mm = pe.matmul(bank[:, :], qT[:, c, t * S:(t + 1) * S], keys, start=True, stop=True)
                    mm.then_inc(score.filled(u), 1)

                def turn(u):
                    pe.wait_ge(ex_ready.sem, ex_ready.at(r, u + 1))
                    pe.wait_ge(turned.drained(u), turned.free(r, u))
                    for h in range(UH):
                        mm = pe.transpose(turned.bank(u)[0:VR, h * P:(h + 1) * P], sc[:, u % 4, h, :], ident[:, :])
                    mm.then_inc(turned.filled(u), 1)

                def values(u):
                    t, g = u // 4, u % 4
                    pe.wait_ge(turned.drained(u), turned.full(r, u))
                    if g == 0:
                        pe.wait_ge(out.drained(t), out.free(r, t))
                        wait_copied(r, [("v", t if own else t // 2)])
                    for h in range(UH):
                        col = (g * UH + h) * VW
                        for i in range(VG):
                            q = slice(i * GS, (i + 1) * GS) if own else slice(0, S)
                            mm = pe.matmul(out.bank(t)[q, col:col + VW], pT[:, u % 2, h * P + q.start:h * P + q.stop],
                                           v[:, t, i, g * UH + h, :], start=True, stop=True)
                    if g == 3:
                        mm.then_inc(out.filled(t), 1)

                def output(t):
                    pe.wait_ge(out.drained(t), out.full(r, t))
                    pe.wait_ge(proj.drained(("oT", t)), proj.free(r, ("oT", t)))
                    for c in range(CH):
                        mm = pe.transpose(proj.bank(("oT", t))[:, c * P:(c + 1) * P], o[:, t % 2, c * P:(c + 1) * P], ident[:, :])
                    mm.then_inc(proj.filled(("oT", t)), 1)

                def output_product(t):
                    wait_copied(r, [("oT", t)])
                    pe.wait_ge(proj.drained(("y", t)), proj.free(r, ("y", t)))
                    for k in range(CH):
                        mm = pe.matmul(proj.bank(("y", t))[:, 0:D], oT[:, t % 2, k, :], wo[:, k, :],
                                       start=(k == 0), stop=(k == CH - 1))
                    mm.then_inc(proj.filled(("y", t)), 1)

                for s in range(UNITS + 8):
                    if s < UNITS:
                        scores(s)
                    if 0 <= s - 2 < UNITS:
                        turn(s - 2)
                    if 0 <= s - 3 < UNITS:
                        values(s - 3)
                    if s >= 8 and (s - 8) % 4 == 0 and (s - 8) // 4 < G:
                        output((s - 8) // 4)
                    if s >= 10 and (s - 10) % 4 == 0 and (s - 10) // 4 < G:
                        output_product((s - 10) // 4)

        @block.scalar
        def _(act):
            act.wait_ge(loaded.sem, 16 * n_const)
            with act.Fori(1, GROUPS + 1, 1) as r:
                def drain(job, write):
                    act.wait_ge(proj.filled(job), proj.full(r, job))
                    write(proj.bank(job)).then_inc(proj.drained(job), 1)

                for c in range(CH):
                    drain(("xT", c), lambda bank: act.copy(
                        xT[:, c, :, 0:S], bank[:, :].rearrange("p (t k) -> p t k", t=G)))
                if own:
                    act.wait_ge(cl_ready.sem, cl_ready.at(r, 2))
                    act.activation(expo[:, :, :], expo[:, :, :], ACT.Exp).then_inc(expo_ready.sem, 1)
                    for c in range(CH):
                        for i in range(2):
                            drain(("kT", c, i), lambda bank: act.activation(
                                kT[:, c, 2 * i:2 * i + 2, :], bank[:, 0:2 * KC].rearrange("p (t k) -> p t k", t=2),
                                ACT.Identity, bias=bk[:, c:c + 1]))
                else:
                    for c in range(CH):
                        drain(("qT", c), lambda bank: act.activation(
                            qT[:, c, :], bank[:, :], ACT.Identity, bias=bq[:, c:c + 1]) if biased else act.copy(qT[:, c, :], bank[:, :]))
                    if not biased:
                        for i in range(G // 2):
                            drain(("v", i), lambda bank: act.copy(
                                v[:, 2 * i:2 * i + 2, 0, :, 0:HD], bank[:, :].rearrange("p (t h d) -> p t h d", t=2, h=H)))

                for s in range(UNITS + 8):
                    if s < UNITS:
                        act.wait_ge(score.drained(s), score.full(r, s))
                        act.activation(sc[:, s % 4, :, :], sc[:, s % 4, :, :], ACT.Exp, scale=HD ** -0.5).then_inc(ex_ready.sem, 1)
                    u = s - 2
                    if 0 <= u < UNITS and u % 2 == 0:
                        act.wait_ge(turned.filled(u), turned.full(r, u))
                        act.copy(pT[:, u % 2, :], turned.bank(u)[0:VR, :]).then_inc(turned.drained(u), 1)
                    if s >= 9 and (s - 9) % 4 == 0 and (s - 9) // 4 < G:
                        t = (s - 9) // 4
                        drain(("oT", t), lambda bank: act.copy(
                            oT[:, t % 2, :, :], bank[:, 0:D].rearrange("p (c k) -> p c k", c=CH)))

        @block.vector
        def _(dve):
            dve.wait_ge(loaded.sem, 16 * n_const)
            dve.wait_ge(const_ready.sem, 1)
            with dve.Fori(1, GROUPS + 1, 1) as r:
                def drain(job, write):
                    dve.wait_ge(proj.filled(job), proj.full(r, job))
                    write(proj.bank(job)).then_inc(proj.drained(job), 1)

                for t in range(G):
                    dve.tensor_scalar(xn[:, t, :], st.x[:, seq(r, t)], mean[:, seq(r, t, 1)],
                                      rstd[:, seq(r, t, 1)], ALU.subtract, ALU.mult).then_inc(xn_ready.sem, 1)
                if own:
                    for c in range(CH):
                        dve.wait_ge(proj.drained(("xT", c)), proj.full(r, ("xT", c)))
                        dve.tensor_tensor(prod[:, c, :, :], xT[:, c, :, 0:GS], bc(assign[:, c, :][:, None, :], [P, G, GS]),
                                          ALU.mult).then_inc(prod_ready.sem, 1)
                    for c in range(CH):
                        drain(("qT", c), lambda bank: dve.scalar_tensor_tensor(
                            qT[:, c, :].rearrange("p (t k) -> p t k", t=G), bank[:, :].rearrange("p (t k) -> p t k", t=G),
                            bq[:, c:c + 1], bc(rot_q[:, None, :], [P, G, S]), ALU.add, ALU.mult))
                    pairs = [P, G * GS // 2, 2]
                    logits = proj.bank("logits")[:, 0:G * GS].rearrange("p (n k) -> p n k", k=2)
                    e2, w2 = (a[:, :, :].rearrange("p t (n k) -> p (t n) k", k=2) for a in (expo, wts))
                    dve.wait_ge(proj.filled("logits"), proj.full(r, "logits"))
                    dve.tensor_reduce(pair[:, :], logits, AX.X, ALU.max).then_inc(cl_ready.sem, 1)
                    dve.wait_ge(cl_ready.sem, cl_ready.at(r, 1))
                    dve.tensor_tensor(e2, logits, bc(pair[:, :, None], pairs), ALU.subtract).then_inc(cl_ready.sem, 1)
                    dve.wait_ge(cl_ready.sem, cl_ready.at(r, 2))
                    dve.wait_ge(expo_ready.sem, expo_ready.at(r, 1))
                    dve.tensor_reduce(pair[:, :], e2, AX.X, ALU.add).then_inc(proj.drained("logits"), 1)
                    dve.wait_ge(proj.drained("logits"), proj.full(r, "logits"))
                    dve.reciprocal(pair[:, :], pair[:, :]).then_inc(cl_ready.sem, 1)
                    dve.wait_ge(cl_ready.sem, cl_ready.at(r, 3))
                    dve.tensor_tensor(w2, e2, bc(pair[:, :, None], pairs), ALU.mult).then_inc(cl_ready.sem, 1)
                    dve.wait_ge(cl_ready.sem, cl_ready.at(r, 4))
                    for c in range(CH):
                        dve.tensor_tensor(prod[:, c, :, :], xT[:, c, :, 0:GS], wts[:, :, :], ALU.mult).then_inc(cl_ready.sem, 1)
                    for c in range(CH):
                        dve.wait_ge(cl_ready.sem, cl_ready.at(r, 5 + c))
                        dve.tensor_reduce(xT[:, c, :, S:KC], prod[:, c, :, :].rearrange("p t (n k) -> p t n k", k=2),
                                          AX.X, ALU.add).then_inc(xc_ready.sem, 1)
                    dve.wait_ge(xc_ready.sem, xc_ready.at(r, CH))
                    for t in range(G):
                        job = ("v", t)
                        dve.wait_ge(proj.filled(job), proj.full(r, job))
                        local = proj.bank(job)[0:GS, :].rearrange("p (i h d) -> p i h d", i=2, h=H)
                        cluster = proj.bank(job)[GS:KL, 0:D].rearrange("p (h d) -> p h d", h=H)
                        bias = bv[:, :].rearrange("p (h d) -> p h d", h=H)
                        for i in range(2):
                            dve.tensor_tensor(v[0:GS, t, i, :, 0:HD], local[:, i], bias[0:GS], ALU.add).then_inc(v_step.sem, 1)
                        dve.tensor_tensor(v[GS:KL, t, 0, :, 0:HD], cluster, bias[GS:KL], ALU.add).then_inc(v_step.sem, 1)
                        dve.tensor_tensor(v[GS:KL, t, 1, :, 0:HD], cluster, bias[GS:KL], ALU.add).then_inc(proj.drained(job), 1)
                else:
                    if kind == "masked":
                        dve.wait_ge(ctx_loaded.sem, ctx_loaded.at(r, 0))
                        dve.tensor_copy(mask[:, :], mrow[:, :]).then_inc(mask_ready.sem, 1)
                        dve.wait_ge(mask_ready.sem, mask_ready.at(r, 1))
                        dve.tensor_scalar(fill[:, :, 0, :], mask[:, :].rearrange("p (t k) -> p t k", t=G), -1.0, parts[:, 0:1],
                                          ALU.add, ALU.mult).then_inc(mask_ready.sem, 1)
                    for c in range(CH):
                        drain(("cT", c), lambda bank: dve.tensor_copy(cT[:, c, :], bank[:, :]))
                    for c in range(CH):
                        out_k = kT[:, c, :, :].rearrange("p t k -> p (t k)")
                        drain(("kT", c), lambda bank: dve.scalar_tensor_tensor(
                            out_k, bank[:, :], bk[:, c:c + 1], mask[:, :], ALU.add, ALU.mult) if kind == "masked"
                            else dve.tensor_copy(out_k, bank[:, :]))
                    if biased:
                        for i in range(G // 2):
                            drain(("v", i), lambda bank: dve.tensor_tensor(
                                v[:, 2 * i:2 * i + 2, 0, :, 0:HD], bank[:, :].rearrange("p (t h d) -> p t h d", t=2, h=H),
                                bc(bv[:, :].rearrange("p (a h d) -> p a h d", a=1, h=H), [P, 2, H, HD]), ALU.add))

                for s in range(UNITS + 8):
                    if s < UNITS:
                        dve.wait_ge(score.filled(s), score.full(r, s))
                        unit = score.bank(s)[:, 0:UH * KU].rearrange("p (h k) -> p h k", h=UH)
                        dve.tensor_reduce(mx[:, s % 4, :], unit, AX.X, ALU.max).then_inc(mx_ready.sem, 1)
                        dve.wait_ge(mx_ready.sem, mx_ready.at(r, s + 1))
                        dve.tensor_tensor(sc[:, s % 4, :, :], unit, bc(mx[:, s % 4, :, None], [P, UH, KU]),
                                          ALU.subtract).then_inc(score.drained(s), 1)
                    u = s - 2
                    if 0 <= u < UNITS and u % 2 == 1:
                        dve.wait_ge(turned.filled(u), turned.full(r, u))
                        dve.tensor_copy(pT[:, u % 2, :], turned.bank(u)[0:VR, :]).then_inc(turned.drained(u), 1)
                    if s >= 7 and (s - 7) % 4 == 0 and (s - 7) // 4 < G:
                        t = (s - 7) // 4
                        dve.wait_ge(out.filled(t), out.full(r, t))
                        heads = out.bank(t)[:, 0:H * VW].rearrange("p (h d) -> p h d", h=H)
                        dve.reciprocal(rs[:, t % 2, :], heads[:, :, HD]).then_inc(rs_ready.sem, 1)
                        dve.wait_ge(rs_ready.sem, rs_ready.at(r, t + 1))
                        dve.tensor_tensor(o[:, t % 2, :].rearrange("p (h d) -> p h d", h=H), heads[:, :, 0:HD],
                                          bc(rs[:, t % 2, :, None], [P, H, HD]), ALU.mult).then_inc(out.drained(t), 1)
                    if s >= 11 and (s - 11) % 4 == 0 and (s - 11) // 4 < G:
                        t = (s - 11) // 4
                        if biased:
                            dve.wait_ge(xb_ready.sem, xb_ready.at(r, t + 1))
                        rows.wait_slot(dve, r, t)
                        drain(("y", t), lambda bank: dve.tensor_tensor(
                            rows.slot[:, t % 2, :], st.x[:, seq(r, t)], bank[:, 0:D], ALU.add))
                        rows.take_stats(dve, r, t, proj.drained(("y", t)), proj.full(r, ("y", t)))
    st.turn()


def bitlinear_phase(nc, st, io, ident):
    mean, rstd = st.mean[st.now], st.rstd[st.now]
    HI = INNER // 2
    halves = [(t, i) for t in range(G) for i in range(2)]
    with ExitStack() as ctx:
        def sb(n, s, dt=F32):
            return ctx.enter_context(nc.sbuf_tensor(f"bit_{n}", s, dt))

        def tally(n, per):
            return Tally(nc, f"bit_{n}", per)

        shapes = {"gate": [P, CH, INNER], "up": [P, CH, INNER], "down": [P, IC, D]}
        names = list(shapes)
        rawf = {n: sb(f"raw_{n}", [P, CH * INNER]) for n in names}
        quant = {n: sb(f"w_{n}", shapes[n], BF16) for n in names}
        identb = sb("identb", [P, P], BF16)
        ones = sb("ones", [P, P])
        sums, wmean, wscale = sb("sums", [P, 3]), sb("wmean", [P, 3]), sb("wscale", [P, 3])
        xn = sb("xn", [P, G, D])
        amax, alim, arec, ascale = (sb(n, [P, G]) for n in ("amax", "alim", "arec", "ascale"))
        dgate, dup, ddown = (sb(n, [P, G]) for n in ("dgate", "dup", "ddown"))
        xq = sb("xq", [P, G, D], BF16)
        xqT = sb("xqT", [P, CH, G * S], BF16)
        sg = sb("sg", [P, 2, HI])
        h = sb("h", [P, 2, INNER])
        hmax, hlim, hrec, hscale = (sb(n, [P, G]) for n in ("hmax", "hlim", "hrec", "hscale"))
        hq = sb("hq", [P, 2, INNER], BF16)
        hqT = sb("hqT", [P, 2, IC, P], BF16)
        round_col = sb("round", [P, 1])

        loaded = tally("weights_loaded", 0)
        ones_ready = tally("ones_ready", 0)
        sums_ready = tally("sums_ready", 0)
        total_ready = tally("total_ready", 0)
        wstep = tally("weight_step", 0)
        ascale_ready = tally("ascale_ready", 1)
        ddown_ready = tally("ddown_ready", G)
        xstep = tally("x_step", G + 5 + G)
        xq_ready = tally("xq_ready", G)
        sg_ready = tally("silu_ready", 2 * G)
        hstep = tally("h_step", 4 * G)
        hr_ready = tally("h_rounded", G)
        hq_ready = tally("hq_ready", G)
        rows = Rows(ctx, nc, "bit", st.x, st.mean[st.now ^ 1], st.rstd[st.now ^ 1], EPS)
        turned = Ring(ctx, nc, "bit_turned", 2, ["xT"] + [("hT", t) for t in range(G)])
        gates = Ring(ctx, nc, "bit_gates", 2, halves)
        ups = Ring(ctx, nc, "bit_ups", 2, halves)
        outs = Ring(ctx, nc, "bit_outs", 2, list(range(G)))
        block = ctx.enter_context(nc.Block())

        @block.sync
        def _(sp):
            for n in names:
                sp.dma_start(rawf[n][:, :].rearrange("p (c o) -> p c o", c=shapes[n][1]),
                             io[f"bit_{n}"].rearrange("(c p) o -> p c o", p=P)).then_inc(loaded.sem, 16)
            sp.dma_start(identb[:, :], io["identb"]).then_inc(loaded.sem, 16)
            sp.wait_ge(loaded.sem, 64)

        @block.gpsimd
        def _(pool):
            rows.pool_start(pool)
            pool.memset(ones[:, :], 1.0).then_inc(ones_ready.sem, 1)
            with pool.Fori(1, GROUPS + 1, 1) as r:
                for t in range(G):
                    rows.store(pool, r, t)
                rows.store_stats(pool, r)

        @block.tensor
        def _(pe):
            pe.wait_ge(loaded.sem, 64)
            pe.wait_ge(ones_ready.sem, 1)
            pe.wait_ge(sums_ready.sem, 3)
            pe.matmul(outs.banks[1][:, 0:3], ones[:, :], sums[:, :], start=True, stop=True).then_inc(total_ready.sem, 1)
            pe.wait_ge(wstep.sem, 12)
            with pe.Fori(1, GROUPS + 1, 1) as r:
                pe.wait_ge(turned.drained("xT"), turned.free(r, "xT"))
                xT = turned.bank("xT")[:, :].bitcast(BF16)
                for t in range(G):
                    pe.wait_ge(xq_ready.sem, xq_ready.at(r, t + 1))
                    for c in range(CH):
                        col = c * G * S + t * S
                        mm = pe.transpose(xT[:, col:col + S], xq[:, t, c * P:(c + 1) * P], identb[:, :])
                mm.then_inc(turned.filled("xT"), 1)
                pe.wait_ge(turned.drained("xT"), turned.full(r, "xT"))

                def widen(t):
                    for i in range(2):
                        for ring, n in ((gates, "gate"), (ups, "up")):
                            pe.wait_ge(ring.drained((t, i)), ring.free(r, (t, i)))
                            for k in range(CH):
                                mm = pe.matmul(ring.bank((t, i))[:, :], xqT[:, k, t * S:(t + 1) * S],
                                               quant[n][:, k, i * HI:(i + 1) * HI], start=(k == 0), stop=(k == CH - 1))
                            mm.then_inc(ring.filled((t, i)), 1)

                def turn(t):
                    pe.wait_ge(turned.drained(("hT", t)), turned.free(r, ("hT", t)))
                    pe.wait_ge(hq_ready.sem, hq_ready.at(r, t + 1))
                    hT = turned.bank(("hT", t))[:, :].bitcast(BF16)
                    for k in range(IC):
                        mm = pe.transpose(hT[:, k * P:(k + 1) * P], hq[:, t % 2, k * P:(k + 1) * P], identb[:, :])
                    mm.then_inc(turned.filled(("hT", t)), 1)

                def narrow(t):
                    pe.wait_ge(turned.drained(("hT", t)), turned.full(r, ("hT", t)))
                    pe.wait_ge(outs.drained(t), outs.free(r, t))
                    for k in range(IC):
                        mm = pe.matmul(outs.bank(t)[:, 0:D], hqT[:, t % 2, k, :], quant["down"][:, k, :],
                                       start=(k == 0), stop=(k == IC - 1))
                    mm.then_inc(outs.filled(t), 1)

                for s in range(G + 3):
                    if s < G:
                        widen(s)
                    if 0 <= s - 2 < G:
                        turn(s - 2)
                    if 0 <= s - 3 < G:
                        narrow(s - 3)

        @block.scalar
        def _(act):
            with act.Fori(1, GROUPS + 1, 1) as r:
                for s in range(G + 1):
                    if s < G:
                        for i in range(2):
                            act.wait_ge(xstep.sem, xstep.at(r, G + 5))
                            act.wait_ge(gates.filled((s, i)), gates.full(r, (s, i)))
                            if (s, i) >= (1, 0):
                                j = 2 * s + i - 2
                                act.wait_ge(ups.drained(halves[j]), ups.full(r, halves[j]))
                            act.activation(sg[:, i, :], gates.bank((s, i))[:, :], ACT.Silu,
                                           scale=dgate[:, s:s + 1]).then_inc(gates.drained((s, i)), 1)
                    if s >= 1:
                        t = s - 1
                        act.wait_ge(hstep.sem, hstep.at(r, 4 * t + 4))
                        act.activation(h[:, t % 2, :], h[:, t % 2, :], ACT.Identity, bias=round_col[:, 0:1],
                                       scale=hscale[:, t:t + 1]).then_inc(hr_ready.sem, 1)

        @block.vector
        def _(dve):
            dve.memset(round_col[:, :], ROUND).then_inc(wstep.sem, 1)
            dve.wait_ge(loaded.sem, 64)
            for i, n in enumerate(names):
                dve.tensor_reduce(sums[:, i:i + 1], rawf[n][:, :], AX.X, ALU.add, apply_absolute_value=True).then_inc(sums_ready.sem, 1)
            dve.wait_ge(total_ready.sem, 1)
            dve.tensor_scalar(wmean[:, :], outs.banks[1][:, 0:3], 1.0 / (D * INNER), 1e-5, ALU.mult, ALU.max).then_inc(wstep.sem, 1)
            dve.wait_ge(wstep.sem, 2)
            dve.reciprocal(wscale[:, :], wmean[:, :]).then_inc(wstep.sem, 1)
            dve.wait_ge(wstep.sem, 3)
            for i, n in enumerate(names):
                dve.tensor_scalar(rawf[n][:, :], rawf[n][:, :], wscale[:, i:i + 1], ROUND, ALU.mult, ALU.add).then_inc(wstep.sem, 1)
            for i, n in enumerate(names):
                dve.wait_ge(wstep.sem, 4 + i)
                dve.tensor_scalar(rawf[n][:, :], rawf[n][:, :], ROUND, 1.0, ALU.subtract, ALU.min).then_inc(wstep.sem, 1)
            for i, n in enumerate(names):
                dve.wait_ge(wstep.sem, 7 + i)
                last = dve.tensor_scalar(quant[n][:, :, :].rearrange("p c o -> p (c o)"), rawf[n][:, :], -1.0, None, ALU.max)
                last.then_inc(wstep.sem, 1)
            with dve.Fori(1, GROUPS + 1, 1) as r:
                for t in range(G):
                    dve.tensor_scalar(xn[:, t, :], st.x[:, seq(r, t)], mean[:, seq(r, t, 1)],
                                      rstd[:, seq(r, t, 1)], ALU.subtract, ALU.mult).then_inc(xstep.sem, 1)
                dve.wait_ge(xstep.sem, xstep.at(r, G))
                dve.tensor_reduce(amax[:, :], xn[:, :, :], AX.X, ALU.max, apply_absolute_value=True).then_inc(xstep.sem, 1)
                dve.wait_ge(xstep.sem, xstep.at(r, G + 1))
                dve.tensor_scalar(alim[:, :], amax[:, :], 1e-5, None, ALU.max).then_inc(xstep.sem, 1)
                dve.wait_ge(xstep.sem, xstep.at(r, G + 2))
                dve.reciprocal(arec[:, :], alim[:, :]).then_inc(xstep.sem, 1)
                dve.tensor_scalar(dgate[:, :], alim[:, :], wmean[:, 0:1], 1.0 / 127, ALU.mult, ALU.mult).then_inc(xstep.sem, 1)
                dve.tensor_scalar(dup[:, :], alim[:, :], wmean[:, 1:2], 1.0 / 127, ALU.mult, ALU.mult).then_inc(xstep.sem, 1)
                dve.wait_ge(xstep.sem, xstep.at(r, G + 5))
                dve.tensor_scalar(ascale[:, :], arec[:, :], 127.0, None, ALU.mult).then_inc(ascale_ready.sem, 1)
                dve.wait_ge(ascale_ready.sem, ascale_ready.at(r, 1))
                for t in range(G):
                    dve.tensor_scalar(xn[:, t, :], xn[:, t, :], ascale[:, t:t + 1], ROUND, ALU.mult, ALU.add).then_inc(xstep.sem, 1)
                for t in range(G):
                    dve.wait_ge(xstep.sem, xstep.at(r, G + 6 + t))
                    dve.tensor_scalar(xq[:, t, :], xn[:, t, :], ROUND, 127.0, ALU.subtract, ALU.min).then_inc(xq_ready.sem, 1)
                dve.wait_ge(turned.filled("xT"), turned.full(r, "xT"))
                dve.tensor_scalar(xqT[:, :, :].rearrange("p c k -> p (c k)"), turned.bank("xT")[:, :].bitcast(BF16),
                                  -128.0, None, ALU.max).then_inc(turned.drained("xT"), 1)

                for s in range(G + 4):
                    if s < G:
                        for i in range(2):
                            dve.wait_ge(ups.filled((s, i)), ups.full(r, (s, i)))
                            dve.wait_ge(gates.drained((s, i)), gates.full(r, (s, i)))
                            dve.scalar_tensor_tensor(h[:, s % 2, i * HI:(i + 1) * HI], ups.bank((s, i))[:, :], dup[:, s:s + 1],
                                                     sg[:, i, :], ALU.mult, ALU.mult).then_inc(ups.drained((s, i)), 1)
                    if 0 <= s - 1 < G:
                        t = s - 1
                        dve.wait_ge(hr_ready.sem, hr_ready.at(r, t + 1))
                        dve.tensor_scalar(hq[:, t % 2, :], h[:, t % 2, :], ROUND, 127.0, ALU.subtract, ALU.min).then_inc(hq_ready.sem, 1)
                    if s < G:
                        dve.wait_ge(ups.drained((s, 0)), ups.full(r, (s, 0)))
                        dve.wait_ge(ups.drained((s, 1)), ups.full(r, (s, 1)))
                        one = slice(s, s + 1)
                        dve.tensor_reduce(hmax[:, one], h[:, s % 2, :], AX.X, ALU.max, apply_absolute_value=True).then_inc(hstep.sem, 1)
                        dve.wait_ge(hstep.sem, hstep.at(r, 4 * s + 1))
                        dve.tensor_scalar(hlim[:, one], hmax[:, one], 1e-5, None, ALU.max).then_inc(hstep.sem, 1)
                        dve.wait_ge(hstep.sem, hstep.at(r, 4 * s + 2))
                        dve.reciprocal(hrec[:, one], hlim[:, one]).then_inc(hstep.sem, 1)
                        dve.tensor_scalar(ddown[:, one], hlim[:, one], wmean[:, 2:3], 1.0 / 127, ALU.mult, ALU.mult).then_inc(ddown_ready.sem, 1)
                        dve.wait_ge(hstep.sem, hstep.at(r, 4 * s + 3))
                        dve.tensor_scalar(hscale[:, one], hrec[:, one], 127.0, None, ALU.mult).then_inc(hstep.sem, 1)
                    if 0 <= s - 2 < G:
                        t = s - 2
                        dve.wait_ge(turned.filled(("hT", t)), turned.full(r, ("hT", t)))
                        dve.tensor_scalar(hqT[:, t % 2, :, :].rearrange("p c k -> p (c k)"), turned.bank(("hT", t))[:, :].bitcast(BF16),
                                          -128.0, None, ALU.max).then_inc(turned.drained(("hT", t)), 1)
                    if 0 <= s - 3 < G:
                        t = s - 3
                        rows.wait_slot(dve, r, t)
                        dve.wait_ge(ddown_ready.sem, ddown_ready.at(r, t + 1))
                        dve.wait_ge(outs.filled(t), outs.full(r, t))
                        dve.scalar_tensor_tensor(rows.slot[:, t % 2, :], outs.bank(t)[:, 0:D], ddown[:, t:t + 1],
                                                 st.x[:, seq(r, t)], ALU.mult, ALU.add).then_inc(outs.drained(t), 1)
                        rows.take_stats(dve, r, t, outs.drained(t), outs.full(r, t))
    st.turn()


def second_layer_self(nc, st, io, ident):
    with ExitStack() as ctx:
        y = ctx.enter_context(nc.sbuf_tensor("inner_stream", [P, B * D], F32))
        performer_phase(nc, st, io, ident, y)
        mlp_phase(nc, st, io, ident, y)


def performer_phase(nc, st, io, ident, y):
    mean, rstd = st.mean[st.now], st.rstd[st.now]
    jobs = ([("xT", c) for c in range(CH)] + [("qT", c) for c in range(CH)] + [("kT", c) for c in range(CH)]
            + ["squares"] + [("v", i) for i in range(G // 2)] + [(what, t) for t in range(G) for what in ("oT", "y")])
    PAIRS = H // 2
    PW = 2 * VW
    mids = [(what, t) for t in range(G) for what in ("kv", "q0", "q1")]
    with ExitStack() as ctx:
        def sb(n, s, dt=F32):
            return ctx.enter_context(nc.sbuf_tensor(f"perf_{n}", s, dt))

        def tally(n, per):
            return Tally(nc, f"perf_{n}", per)

        wq, wk, wv, wo = (sb(n, [P, CH, D]) for n in ("wq", "wk", "wv", "wo"))
        omega = sb("omega", [P, HH * NF])
        half_heads = sb("half_heads", [P, HH])
        floor = sb("floor", [P, 1])
        xn = sb("xn", [P, G, D])
        xT = sb("xT", [P, CH, G * S])
        qk = sb("qk", [P, 2, CH, G * S])
        qk2 = sb("qk2", [P, 2, CH, G * S])
        half2 = sb("half2", [P, G, 2, H])
        v = sb("v", [P, G, H, VW])
        f = sb("f", [P, 4, HH, NF])
        mx, off = sb("mx", [P, 4, HH]), sb("off", [P, 4, HH])
        fT = sb("fT", [P, 2, 4 * P])
        kv = sb("kv", [P, 2, PAIRS, PW])
        rs = sb("rs", [P, 2, H])
        o = sb("o", [P, 2, D])
        oT = sb("oT", [P, 2, CH, P])

        loaded = tally("weights_loaded", 0)
        const_ready = tally("const_ready", 0)
        xn_ready = tally("xn_ready", G)
        square_ready = tally("squares_ready", 2 * CH)
        copied = tally("scaled_ready", CH)
        mx_ready = tally("max_ready", UNITS)
        off_ready = tally("offset_ready", UNITS)
        ex_ready = tally("exp_ready", UNITS)
        f_ready = tally("features_ready", UNITS)
        kv_half = tally("kv_half", G)
        rs_ready = tally("recip_ready", G)
        rows = Rows(ctx, nc, "perf", y, st.mean_in, st.rstd_in, EPS_IN)
        proj = Ring(ctx, nc, "perf_proj", 2, jobs)
        score = Ring(ctx, nc, "perf_score", 2, list(range(UNITS)))
        mid = Ring(ctx, nc, "perf_mid", 2, mids)
        out = Ring(ctx, nc, "perf_out", 2, list(range(G)))
        block = ctx.enter_context(nc.Block())

        @block.sync
        def _(sp):
            for tile, key in ((wq, "wq"), (wk, "wk"), (wv, "wv"), (wo, "wo")):
                sp.dma_start(tile[:, :, :], io[f"perf_{key}"].rearrange("(c p) o -> p c o", p=P)).then_inc(loaded.sem, 16)
            sp.dma_start(omega[:, :], io["omega"]).then_inc(loaded.sem, 16)
            sp.dma_start(half_heads[:, :], io["half_heads"]).then_inc(loaded.sem, 16)
            sp.wait_ge(loaded.sem, 96)

        @block.gpsimd
        def _(pool):
            rows.pool_start(pool)
            pool.memset(v[:, :, :, HD:VW], 1.0).then_inc(const_ready.sem, 1)
            pool.memset(kv[:, :, :, :], 0.0).then_inc(const_ready.sem, 1)
            pool.memset(floor[:, :], 1e-6 * NF ** 0.5).then_inc(const_ready.sem, 1)
            pool.wait_ge(const_ready.sem, 3)
            with pool.Fori(1, GROUPS + 1, 1) as r:
                for s in range(UNITS + 8):
                    if s < UNITS:
                        pool.wait_ge(ex_ready.sem, ex_ready.at(r, s + 1))
                        flat = f[:, s % 4, :, :].rearrange("p h m -> p (h m)")
                        pool.tensor_tensor(flat, flat, bc(floor[:, :], [P, HH * NF]), ALU.add).then_inc(f_ready.sem, 1)
                    if s >= 11 and (s - 11) % 4 == 0 and (s - 11) // 4 < G:
                        t = (s - 11) // 4
                        rows.store(pool, r, t)
                rows.store_stats(pool, r)

        @block.tensor
        def _(pe):
            pe.wait_ge(loaded.sem, 96)
            pe.wait_ge(const_ready.sem, 3)
            with pe.Fori(1, GROUPS + 1, 1) as r:
                for c in range(CH):
                    pe.wait_ge(proj.drained(("xT", c)), proj.free(r, ("xT", c)))
                    for t in range(G):
                        pe.wait_ge(xn_ready.sem, xn_ready.at(r, t + 1))
                        mm = pe.transpose(proj.bank(("xT", c))[:, t * P:(t + 1) * P], xn[:, t, c * P:(c + 1) * P], ident[:, :])
                    mm.then_inc(proj.filled(("xT", c)), 1)
                for c in range(CH):
                    pe.wait_ge(proj.drained(("xT", c)), proj.full(r, ("xT", c)))
                for what, w in (("qT", wq), ("kT", wk)):
                    for c in range(CH):
                        pe.wait_ge(proj.drained((what, c)), proj.free(r, (what, c)))
                        for k in range(CH):
                            mm = pe.matmul(proj.bank((what, c))[:, :], w[:, k, c * P:(c + 1) * P], xT[:, k, :],
                                           start=(k == 0), stop=(k == CH - 1))
                        mm.then_inc(proj.filled((what, c)), 1)
                pe.wait_ge(square_ready.sem, square_ready.at(r, 2 * CH))
                pe.wait_ge(proj.drained("squares"), proj.free(r, "squares"))
                for t in range(G):
                    for w in range(2):
                        for c in range(CH):
                            col = (t * 2 + w) * H + c * HH
                            mm = pe.matmul(proj.bank("squares")[:, col:col + HH], qk2[:, w, c, t * S:(t + 1) * S], half_heads[:, :],
                                           start=True, stop=True)
                mm.then_inc(proj.filled("squares"), 1)
                for i in range(G // 2):
                    pe.wait_ge(proj.drained(("v", i)), proj.free(r, ("v", i)))
                    for t in (2 * i, 2 * i + 1):
                        for k in range(CH):
                            mm = pe.matmul(proj.bank(("v", i))[:, (t % 2) * D:(t % 2 + 1) * D], xT[:, k, t * P:(t + 1) * P],
                                           wv[:, k, :], start=(k == 0), stop=(k == CH - 1))
                    mm.then_inc(proj.filled(("v", i)), 1)

                def features(u):
                    t, w, c = u // 4, 1 - (u % 4) // 2, u % 2
                    pe.wait_ge(score.drained(u), score.free(r, u))
                    pe.matmul(score.bank(u)[:, :], qk[:, w, c, t * S:(t + 1) * S], omega[:, :],
                              start=True, stop=True).then_inc(score.filled(u), 1)

                def use(u):
                    t, c = u // 4, u % 2
                    pe.wait_ge(f_ready.sem, f_ready.at(r, u + 1))
                    keys = u % 4 < 2
                    job = ("kv" if keys else f"q{c}", t)
                    if c == 0 or not keys:
                        pe.wait_ge(mid.drained(job), mid.free(r, job))
                    if keys and c == 0:
                        pe.wait_ge(proj.drained(("v", t // 2)), proj.full(r, ("v", t // 2)))
                    for j in range(4):
                        pair = c * 4 + j
                        two = f[:, u % 4, 2 * j:2 * j + 2, :].rearrange("p h m -> p (h m)")
                        if keys:
                            mm = pe.matmul(mid.bank(job)[:, pair * PW:(pair + 1) * PW], two, v[:, t, 2 * pair:2 * pair + 2, :],
                                           start=True, stop=True)
                        else:
                            mm = pe.transpose(mid.bank(job)[:, j * P:(j + 1) * P], two, ident[:, :])
                    if c == 1 or not keys:
                        mm.then_inc(mid.filled(job), 1)

                def attend(u):
                    t, c = u // 4, u % 2
                    job = (f"q{c}", t)
                    pe.wait_ge(mid.drained(job), mid.full(r, job))
                    if c == 0:
                        pe.wait_ge(mid.drained(("kv", t)), mid.full(r, ("kv", t)))
                        pe.wait_ge(out.drained(t), out.free(r, t))
                    for j in range(4):
                        pair = c * 4 + j
                        mm = pe.matmul(out.bank(t)[:, pair * PW:(pair + 1) * PW], fT[:, c, j * P:(j + 1) * P], kv[:, t % 2, pair, :],
                                       start=True, stop=True)
                    if c == 1:
                        mm.then_inc(out.filled(t), 1)

                def output(t):
                    pe.wait_ge(out.drained(t), out.full(r, t))
                    pe.wait_ge(proj.drained(("oT", t)), proj.free(r, ("oT", t)))
                    for c in range(CH):
                        mm = pe.transpose(proj.bank(("oT", t))[:, c * P:(c + 1) * P], o[:, t % 2, c * P:(c + 1) * P], ident[:, :])
                    mm.then_inc(proj.filled(("oT", t)), 1)

                def output_product(t):
                    pe.wait_ge(proj.drained(("oT", t)), proj.full(r, ("oT", t)))
                    pe.wait_ge(proj.drained(("y", t)), proj.free(r, ("y", t)))
                    for k in range(CH):
                        mm = pe.matmul(proj.bank(("y", t))[:, 0:D], oT[:, t % 2, k, :], wo[:, k, :],
                                       start=(k == 0), stop=(k == CH - 1))
                    mm.then_inc(proj.filled(("y", t)), 1)

                for s in range(UNITS + 8):
                    if s < UNITS:
                        features(s)
                    if 0 <= s - 2 < UNITS:
                        use(s - 2)
                    if 0 <= s - 3 < UNITS and (s - 3) % 4 >= 2:
                        attend(s - 3)
                    if s >= 8 and (s - 8) % 4 == 0 and (s - 8) // 4 < G:
                        output((s - 8) // 4)
                    if s >= 10 and (s - 10) % 4 == 0 and (s - 10) // 4 < G:
                        output_product((s - 10) // 4)

        @block.scalar
        def _(act):
            act.wait_ge(loaded.sem, 96)
            with act.Fori(1, GROUPS + 1, 1) as r:
                def drain(job, write):
                    act.wait_ge(proj.filled(job), proj.full(r, job))
                    write(proj.bank(job)).then_inc(proj.drained(job), 1)

                for c in range(CH):
                    drain(("xT", c), lambda bank: act.copy(xT[:, c, :], bank[:, :]))
                for c in range(CH):
                    drain(("qT", c), lambda bank: act.mul(qk[:, 0, c, :], bank[:, :], HD ** -0.25))
                for c in range(CH):
                    act.wait_ge(proj.drained(("qT", c)), proj.full(r, ("qT", c)))
                    act.activation(qk2[:, 0, c, :], qk[:, 0, c, :], ACT.Square).then_inc(square_ready.sem, 1)
                for i in range(G // 2):
                    drain(("v", i), lambda bank: act.copy(
                        v[:, 2 * i:2 * i + 2, :, 0:HD], bank[:, :].rearrange("p (t h d) -> p t h d", t=2, h=H)))
                for s in range(UNITS + 8):
                    if s < UNITS:
                        act.wait_ge(score.drained(s), score.full(r, s))
                        act.activation(f[:, s % 4, :, :], f[:, s % 4, :, :], ACT.Exp).then_inc(ex_ready.sem, 1)
                    u = s - 2
                    if 0 <= u < UNITS and u % 4 >= 2:
                        job = (f"q{u % 2}", u // 4)
                        act.wait_ge(mid.filled(job), mid.full(r, job))
                        act.copy(fT[:, u % 2, :], mid.bank(job)[:, :]).then_inc(mid.drained(job), 1)
                    if s >= 9 and (s - 9) % 4 == 0 and (s - 9) // 4 < G:
                        t = (s - 9) // 4
                        drain(("oT", t), lambda bank: act.copy(
                            oT[:, t % 2, :, :], bank[:, 0:D].rearrange("p (c k) -> p c k", c=CH)))

        @block.vector
        def _(dve):
            dve.wait_ge(loaded.sem, 96)
            dve.wait_ge(const_ready.sem, 3)
            with dve.Fori(1, GROUPS + 1, 1) as r:
                def drain(job, write):
                    dve.wait_ge(proj.filled(job), proj.full(r, job))
                    write(proj.bank(job)).then_inc(proj.drained(job), 1)

                for t in range(G):
                    dve.tensor_scalar(xn[:, t, :], st.x[:, seq(r, t)], mean[:, seq(r, t, 1)],
                                      rstd[:, seq(r, t, 1)], ALU.subtract, ALU.mult).then_inc(xn_ready.sem, 1)
                for c in range(CH):
                    drain(("kT", c), lambda bank: dve.tensor_scalar(qk[:, 1, c, :], bank[:, :], HD ** -0.25, None, ALU.mult))
                for c in range(CH):
                    dve.wait_ge(proj.drained(("kT", c)), proj.full(r, ("kT", c)))
                    dve.tensor_tensor(qk2[:, 1, c, :], qk[:, 1, c, :], qk[:, 1, c, :], ALU.mult).then_inc(square_ready.sem, 1)
                drain("squares", lambda bank: dve.tensor_copy(half2[:, :, :, :].rearrange("p t w h -> p (t w h)"), bank[:, 0:G * 2 * H]))
                dve.wait_ge(proj.drained("squares"), proj.full(r, "squares"))
                for s in range(UNITS + 8):
                    if s < UNITS:
                        t, w, c = s // 4, 1 - (s % 4) // 2, s % 2
                        dve.wait_ge(score.filled(s), score.full(r, s))
                        unit = score.bank(s)[:, :].rearrange("p (h m) -> p h m", h=HH)
                        dve.tensor_reduce(mx[:, s % 4, :], unit, AX.X, ALU.max).then_inc(mx_ready.sem, 1)
                        dve.wait_ge(mx_ready.sem, mx_ready.at(r, s + 1))
                        dve.tensor_tensor(off[:, s % 4, :], mx[:, s % 4, :], half2[:, t, w, c * HH:(c + 1) * HH], ALU.add).then_inc(off_ready.sem, 1)
                        dve.wait_ge(off_ready.sem, off_ready.at(r, s + 1))
                        dve.tensor_tensor(f[:, s % 4, :, :], unit, bc(off[:, s % 4, :, None], [P, HH, NF]),
                                          ALU.subtract).then_inc(score.drained(s), 1)
                    u = s - 2
                    if 0 <= u < UNITS and u % 4 == 1:
                        t = u // 4
                        job = ("kv", t)
                        dve.wait_ge(mid.filled(job), mid.full(r, job))
                        both = mid.bank(job)[:, 0:PAIRS * PW].rearrange("p (a k) -> p a k", a=PAIRS)
                        dve.tensor_copy(kv[0:NF, t % 2, :, 0:VW], both[0:NF, :, 0:VW]).then_inc(kv_half.sem, 1)
                        dve.tensor_copy(kv[NF:P, t % 2, :, VW:PW], both[NF:P, :, VW:PW]).then_inc(mid.drained(job), 1)
                    if s >= 7 and (s - 7) % 4 == 0 and (s - 7) // 4 < G:
                        t = (s - 7) // 4
                        dve.wait_ge(out.filled(t), out.full(r, t))
                        heads = out.bank(t)[:, 0:H * VW].rearrange("p (h d) -> p h d", h=H)
                        dve.reciprocal(rs[:, t % 2, :], heads[:, :, HD]).then_inc(rs_ready.sem, 1)
                        dve.wait_ge(rs_ready.sem, rs_ready.at(r, t + 1))
                        dve.tensor_tensor(o[:, t % 2, :].rearrange("p (h d) -> p h d", h=H), heads[:, :, 0:HD],
                                          bc(rs[:, t % 2, :, None], [P, H, HD]), ALU.mult).then_inc(out.drained(t), 1)
                    if s >= 11 and (s - 11) % 4 == 0 and (s - 11) // 4 < G:
                        t = (s - 11) // 4
                        rows.wait_slot(dve, r, t)
                        drain(("y", t), lambda bank: dve.tensor_tensor(rows.slot[:, t % 2, :], xn[:, t, :], bank[:, 0:D], ALU.add))
                        rows.take_stats(dve, r, t, proj.drained(("y", t)), proj.full(r, ("y", t)))


def mlp_phase(nc, st, io, ident, y):
    wide = [("xT", c) for c in range(CH)] + [("hT", k) for k in range(IC)]
    with ExitStack() as ctx:
        def sb(n, s, dt=F32):
            return ctx.enter_context(nc.sbuf_tensor(f"mlp_{n}", s, dt))

        def tally(n, per):
            return Tally(nc, f"mlp_{n}", per)

        w1, w2, b1 = sb("w1", [P, CH, INNER]), sb("w2", [P, IC, D]), sb("b1", [P, IC])
        g1, c1, g2, c2, b2 = (sb(n, [P, D]) for n in ("g1", "c1", "g2", "c2", "b2"))
        u = sb("u", [P, G, D])
        ub = sb("ub", [P, G, D])
        uT = sb("uT", [P, CH, G * S])
        hT = sb("hT", [P, IC, G * S])
        z = sb("z", [P, G, D])
        zraw, zmv = sb("zraw", [P, G, 6]), sb("zmv", [P, G, 2])
        zvar, zrstd, mhalf, eps = (sb(n, [P, G]) for n in ("zvar", "zrstd", "mhalf", "eps"))

        loaded = tally("weights_loaded", 0)
        const_ready = tally("const_ready", 0)
        u_step = tally("u_step", G + 1)
        u_ready = tally("u_ready", 1)
        ub_ready = tally("ub_ready", 1)
        zraw_ready = [tally(f"z_stats{t}", 1) for t in range(G)]
        zmv_ready = tally("z_aggr", G)
        zr_ready = tally("z_rstd_step", 2)
        zn_ready = tally("z_norm_step", G + 2)
        x_ready = tally("x_ready", G)
        rows = Rows(ctx, nc, "mlp", st.x, st.mean[st.now ^ 1], st.rstd[st.now ^ 1], EPS)
        hid = Ring(ctx, nc, "mlp_hid", 4, wide)
        outs = Ring(ctx, nc, "mlp_outs", 4, list(range(G)))
        block = ctx.enter_context(nc.Block())

        @block.sync
        def _(sp):
            sp.dma_start(w1[:, :, :], io["mlp_w1"].rearrange("(c p) o -> p c o", p=P)).then_inc(loaded.sem, 16)
            sp.dma_start(w2[:, :, :], io["mlp_w2"].rearrange("(c p) o -> p c o", p=P)).then_inc(loaded.sem, 16)
            sp.dma_start(b1[:, :], io["mlp_b1"]).then_inc(loaded.sem, 16)
            for tile, key in ((g1, "ln1_g"), (c1, "ln1_b"), (g2, "ln2_g"), (c2, "ln2_b"), (b2, "b2")):
                sp.dma_start(tile[:, :], io[f"mlp_{key}"].partition_broadcast(P)).then_inc(loaded.sem, 16)
            sp.wait_ge(loaded.sem, 128)

        @block.gpsimd
        def _(pool):
            rows.pool_start(pool)
            pool.memset(mhalf[:, :], -0.5).then_inc(const_ready.sem, 1)
            pool.memset(eps[:, :], EPS_IN).then_inc(const_ready.sem, 1)
            pool.wait_ge(loaded.sem, 128)
            pool.wait_ge(const_ready.sem, 2)
            with pool.Fori(1, GROUPS + 1, 1) as r:
                pool.wait_ge(u_ready.sem, u_ready.at(r, 1))
                pool.tensor_tensor(ub[:, :, :], u[:, :, :], bc(b2[:, None, :], [P, G, D]), ALU.add).then_inc(ub_ready.sem, 1)
                pool.wait_ge(zmv_ready.sem, zmv_ready.at(r, G))
                pool.tensor_tensor(zvar[:, :], zmv[:, :, 1], eps[:, :], ALU.add).then_inc(zr_ready.sem, 1)
                pool.wait_ge(zr_ready.sem, zr_ready.at(r, 1))
                pool.tensor_tensor(zrstd[:, :], zvar[:, :], mhalf[:, :], ALU.pow).then_inc(zr_ready.sem, 1)
                for t in range(G):
                    rows.store(pool, r, t)
                rows.store_stats(pool, r)

        @block.tensor
        def _(pe):
            pe.wait_ge(loaded.sem, 128)
            with pe.Fori(1, GROUPS + 1, 1) as r:
                pe.wait_ge(u_ready.sem, u_ready.at(r, 1))
                for c in range(CH):
                    job = ("xT", c)
                    pe.wait_ge(hid.drained(job), hid.free(r, job))
                    for t in range(G):
                        mm = pe.transpose(hid.bank(job)[:, t * P:(t + 1) * P], u[:, t, c * P:(c + 1) * P], ident[:, :])
                    mm.then_inc(hid.filled(job), 1)
                for c in range(CH):
                    pe.wait_ge(hid.drained(("xT", c)), hid.full(r, ("xT", c)))
                for i in range(IC):
                    job = ("hT", i)
                    pe.wait_ge(hid.drained(job), hid.free(r, job))
                    for k in range(CH):
                        mm = pe.matmul(hid.bank(job)[:, :], w1[:, k, i * P:(i + 1) * P], uT[:, k, :],
                                       start=(k == 0), stop=(k == CH - 1))
                    mm.then_inc(hid.filled(job), 1)
                for i in range(IC):
                    pe.wait_ge(hid.drained(("hT", i)), hid.full(r, ("hT", i)))
                for t in range(G):
                    pe.wait_ge(outs.drained(t), outs.free(r, t))
                    for i in range(IC):
                        mm = pe.matmul(outs.bank(t)[:, 0:D], hT[:, i, t * S:(t + 1) * S], w2[:, i, :],
                                       start=(i == 0), stop=(i == IC - 1))
                    mm.then_inc(outs.filled(t), 1)

        @block.scalar
        def _(act):
            act.wait_ge(loaded.sem, 128)
            with act.Fori(1, GROUPS + 1, 1) as r:
                for c in range(CH):
                    act.wait_ge(hid.filled(("xT", c)), hid.full(r, ("xT", c)))
                    act.copy(uT[:, c, :], hid.bank(("xT", c))[:, :]).then_inc(hid.drained(("xT", c)), 1)
                for i in range(IC):
                    if i == 0:
                        act.wait_ge(outs.filled(G - 1), outs.free(r, G - 1))
                    act.wait_ge(hid.filled(("hT", i)), hid.full(r, ("hT", i)))
                    act.activation(hT[:, i, :], hid.bank(("hT", i))[:, :], ACT.Gelu, bias=b1[:, i:i + 1]).then_inc(hid.drained(("hT", i)), 1)

        @block.vector
        def _(dve):
            dve.wait_ge(loaded.sem, 128)
            with dve.Fori(1, GROUPS + 1, 1) as r:
                for t in range(G):
                    dve.tensor_scalar(z[:, t, :], y[:, seq(r, t)], st.mean_in[:, seq(r, t, 1)],
                                      st.rstd_in[:, seq(r, t, 1)], ALU.subtract, ALU.mult).then_inc(u_step.sem, 1)
                dve.wait_ge(u_step.sem, u_step.at(r, G))
                dve.tensor_tensor(z[:, :, :], z[:, :, :], bc(g1[:, None, :], [P, G, D]), ALU.mult).then_inc(u_step.sem, 1)
                dve.wait_ge(u_step.sem, u_step.at(r, G + 1))
                dve.tensor_tensor(u[:, :, :], z[:, :, :], bc(c1[:, None, :], [P, G, D]), ALU.add).then_inc(u_ready.sem, 1)
                dve.wait_ge(ub_ready.sem, ub_ready.at(r, 1))
                for t in range(G):
                    dve.wait_ge(outs.filled(t), outs.full(r, t))
                    dve.tensor_tensor(ub[:, t, :], ub[:, t, :], outs.bank(t)[:, 0:D], ALU.add).then_inc(outs.drained(t), 1)
                    dve.wait_ge(outs.drained(t), outs.full(r, t))
                    dve.bn_stats(zraw[:, t, :], ub[:, t, :]).then_inc(zraw_ready[t].sem, 1)
                    dve.wait_ge(loaded.sem, 128)
                    dve.wait_ge(zraw_ready[t].sem, zraw_ready[t].at(r, 1))
                    dve.bn_aggr(zmv[:, t, :], zraw[:, t, :]).then_inc(zmv_ready.sem, 1)
                dve.wait_ge(zr_ready.sem, zr_ready.at(r, 2))
                for t in range(G):
                    dve.tensor_scalar(z[:, t, :], ub[:, t, :], zmv[:, t, 0:1], zrstd[:, t:t + 1],
                                      ALU.subtract, ALU.mult).then_inc(zn_ready.sem, 1)
                dve.wait_ge(zn_ready.sem, zn_ready.at(r, G))
                dve.tensor_tensor(z[:, :, :], z[:, :, :], bc(g2[:, None, :], [P, G, D]), ALU.mult).then_inc(zn_ready.sem, 1)
                dve.wait_ge(zn_ready.sem, zn_ready.at(r, G + 1))
                dve.tensor_tensor(z[:, :, :], z[:, :, :], bc(c2[:, None, :], [P, G, D]), ALU.add).then_inc(zn_ready.sem, 1)
                dve.wait_ge(zn_ready.sem, zn_ready.at(r, G + 2))
                for t in range(G):
                    rows.wait_slot(dve, r, t)
                    dve.tensor_tensor(rows.slot[:, t % 2, :], st.x[:, seq(r, t)], z[:, t, :], ALU.add).then_inc(x_ready.sem, 1)
                    rows.take_stats(dve, r, t, x_ready.sem, x_ready.at(r, t + 1))
    st.turn()


class Tile:

    def __init__(self, r, c):
        self.number = r * 2 + c
        self.slot = c % 2
        self.use = r + c // 2
        self.exists = isinstance(r, int) is False or 0 <= c < TILES


HEAD = 5


def tile_steps(eng, step, tail):
    for c in range(HEAD):
        step(0, c)
    with eng.Fori(1, (TILES - HEAD) // 2 + 1, 1) as r:
        for j in range(2):
            step(r, HEAD - 2 + j)
    for c in range(TILES, TILES + tail):
        step(0, c)


def wait_count(eng, sem, count):
    if not isinstance(count, int) or count > 0:
        eng.wait_ge(sem, count)


def experts_phase(nc, st, io, ident, out):
    mean, rstd = st.mean[st.now], st.rstd[st.now]
    slot_x = nc.dram_tensor("slot_x", (TILES * P, D), F32, kind="Internal").ap()
    slot_y = nc.dram_tensor("slot_y", (TILES * P, D), F32, kind="Internal").ap()
    W1, W2 = CH * 2 * EI, EC * D
    with ExitStack() as ctx:
        def keep(n, s, dt=F32):
            return ctx.enter_context(nc.sbuf_tensor(f"moe_{n}", s, dt))

        w1, w2 = keep("w1", [P, E * W1]), keep("w2", [P, E * W2])
        flag = [keep(f"flag{w}", [P, B * E]) for w in range(2)]
        kept_prob = [keep(f"kept_prob{w}", [P, B * E]) for w in range(2)]
        weight = [keep(f"weight{w}", [P, B]) for w in range(2)]
        place = keep("place", [P, B, 2], I32)
        owner = keep("owner", [1, TILES], I32)
        w_loaded = Tally(nc, "moe_weights_loaded", 0)
        zero_stored = Tally(nc, "moe_zero_stored", 0)

        route_stage(nc, st, io, ident, flag, kept_prob, w1, w2, w_loaded, slot_x, zero_stored)
        sort_stage(nc, io, flag, kept_prob, weight, place, owner)

        with ExitStack() as ctx2:
            xn = ctx2.enter_context(nc.sbuf_tensor("scatter_xn", [P, 2, G, D], F32))
            index = ctx2.enter_context(nc.sbuf_tensor("scatter_index", [P, 2, 2 * G], I32))
            xn_ready = [Tally(nc, f"scatter_xn_ready{k}", 1, 0) for k in range(2)]
            index_ready = [Tally(nc, f"scatter_index_ready{k}", 1, 0) for k in range(2)]
            sent = [Tally(nc, f"scatter_sent{k}", 2 * G * 16, 0) for k in range(2)]
            block = ctx2.enter_context(nc.Block())

            @block.vector
            def _(dve):
                def turn(r):
                    for k in range(2):
                        g = r * 2 + (k - 1)
                        wait_count(dve, sent[k].sem, sent[k].at(r, -2 * G * 16))
                        for t in range(G):
                            norm = dve.tensor_scalar(xn[:, k, t, :], st.x[:, seq(g, t)], mean[:, seq(g, t, 1)],
                                                     rstd[:, seq(g, t, 1)], ALU.subtract, ALU.mult)
                        norm.then_inc(xn_ready[k].sem, 1)

                turn(1)
                with dve.Fori(2, GROUPS // 2 + 1, 1) as r:
                    turn(r)

            @block.gpsimd
            def _(pool):
                pool.wait_ge(zero_stored.sem, 16)

                def turn(r):
                    for k in range(2):
                        pool.wait_ge(zero_stored.sem, 16)
                        wait_count(pool, sent[k].sem, sent[k].at(r, -2 * G * 16))
                        pool.tensor_copy(index[:, k, :].rearrange("p (t w) -> p t w", w=2),
                                         place[:, bass.ds(r * (2 * G) + (k - 2) * G, G), :]).then_inc(index_ready[k].sem, 1)
                        pool.wait_ge(zero_stored.sem, 16)
                        pool.wait_ge(index_ready[k].sem, index_ready[k].at(r, 0))
                        pool.wait_ge(xn_ready[k].sem, xn_ready[k].at(r, 0))
                        for t in range(G):
                            for w in range(2):
                                col = 2 * t + w
                                pool.indirect_dma_start(slot_x, bass.IndirectOffsetOnAxis(index[:, k, col:col + 1], 0),
                                                        xn[:, k, t, :], None).then_inc(sent[k].sem, 16)

                turn(1)
                with pool.Fori(2, GROUPS // 2 + 1, 1) as r:
                    turn(r)
                for k in range(2):
                    pool.wait_ge(sent[k].sem, sent[k].at(GROUPS // 2, 0))

        tiles_stage(nc, ident, w1, w2, W1, W2, owner, w_loaded, slot_x, slot_y)

        with ExitStack() as ctx2:
            got = [ctx2.enter_context(nc.sbuf_tensor(f"gather_got{w}", [P, 2, G, D], F32)) for w in range(2)]
            index = ctx2.enter_context(nc.sbuf_tensor("gather_index", [P, 2, 2 * G], I32))
            index_ready = [Tally(nc, f"gather_index_ready{k}", 1, 0) for k in range(2)]
            arrived = [Tally(nc, f"gather_arrived{k}", 2 * G * 16, 0) for k in range(2)]
            first_added = [Tally(nc, f"gather_first_added{k}", G) for k in range(2)]
            added = [Tally(nc, f"gather_added{k}", 1) for k in range(2)]
            out_stored = Tally(nc, "out_stored", 0)
            block = ctx2.enter_context(nc.Block())

            @block.gpsimd
            def _(pool):
                with pool.Fori(1, GROUPS // 2 + 1, 1) as r:
                    for k in range(2):
                        pool.wait_ge(zero_stored.sem, 16)
                        pool.wait_ge(added[k].sem, added[k].at(r, 0))
                        pool.tensor_copy(index[:, k, :].rearrange("p (t w) -> p t w", w=2),
                                         place[:, bass.ds(r * (2 * G) + (k - 2) * G, G), :]).then_inc(index_ready[k].sem, 1)
                        pool.wait_ge(zero_stored.sem, 16)
                        pool.wait_ge(index_ready[k].sem, index_ready[k].at(r, 0))
                        for t in range(G):
                            for w in range(2):
                                col = 2 * t + w
                                pool.indirect_dma_start(got[w][:, k, t, :], None, slot_y,
                                                        bass.IndirectOffsetOnAxis(index[:, k, col:col + 1], 0)).then_inc(arrived[k].sem, 16)

            @block.vector
            def _(dve):
                with dve.Fori(1, GROUPS // 2 + 1, 1) as r:
                    for k in range(2):
                        g = r * 2 + (k - 1)
                        dve.wait_ge(arrived[k].sem, arrived[k].at(r, 0))
                        for w in range(2):
                            for t in range(G):
                                if w == 1:
                                    dve.wait_ge(first_added[k].sem, first_added[k].at(r, t + 1))
                                here = st.x[:, seq(g, t)]
                                add = dve.scalar_tensor_tensor(here, got[w][:, k, t, :], weight[w][:, seq(g, t, 1)], here,
                                                               ALU.mult, ALU.add)
                                if w == 0:
                                    add.then_inc(first_added[k].sem, 1)
                        add.then_inc(added[k].sem, 1)

            @block.sync
            def _(sp):
                rows = out.rearrange("(n p) d -> p n d", p=P)
                with sp.Fori(1, GROUPS // 2 + 1, 1) as r:
                    for k in range(2):
                        g = r * 2 + (k - 1)
                        sp.wait_ge(added[k].sem, added[k].at(r, 1))
                        sp.dma_start(rows[:, bass.ds(r * (2 * G) + (k - 2) * G, G), :],
                                     st.x[:, group(g, D)].rearrange("p (n d) -> p n d", d=D)).then_inc(out_stored.sem, 16)
                sp.wait_ge(out_stored.sem, 16 * GROUPS)


def route_stage(nc, st, io, ident, flag, kept_prob, w1, w2, w_loaded, slot_x, zero_stored):
    mean, rstd = st.mean[st.now], st.rstd[st.now]
    with ExitStack() as ctx:
        def sb(n, s, dt=F32):
            return ctx.enter_context(nc.sbuf_tensor(f"route_{n}", s, dt))

        def tally(n, per):
            return Tally(nc, f"route_{n}", per)

        router, before = sb("router", [P, CH, E]), sb("before", [P, 1, E * E])
        zero = sb("zero", [P, 1, D])
        xn, xT = sb("xn", [P, 2, G, D]), sb("xT", [P, CH, G * S])
        top, total, recip = sb("top", [P, G]), sb("total", [P, G]), sb("recip", [P, G])
        prob = sb("prob", [P, G, E])
        above, tied = sb("above", [P, G, E, E]), sb("tied", [P, G, E, E])
        rank = sb("rank", [P, G, E])
        loaded = tally("weights_loaded", 0)
        zero_ready = tally("zero_ready", 0)
        xn_ready = tally("xn_ready", G)
        step = tally("step", 13)
        exp_ready = tally("exp_ready", 1)
        ring = Ring(ctx, nc, "route_ring", 3, [("xT", c) for c in range(CH)] + ["logits"])
        block = ctx.enter_context(nc.Block())

        @block.sync
        def _(sp):
            sp.dma_start(router[:, :, :], io["router"].rearrange("(c p) e -> p c e", p=P)).then_inc(loaded.sem, 16)
            sp.dma_start(before[:, 0, :], io["before"]).then_inc(loaded.sem, 16)
            sp.wait_ge(zero_ready.sem, 1)
            sp.dma_start(slot_x.rearrange("(n p) d -> p n d", p=P), bc(zero[:, :, :], [P, TILES, D])).then_inc(zero_stored.sem, 16)
            for e in range(E):
                sp.dma_start(w1[:, :].rearrange("p (e c o) -> p e c o", e=E, c=CH)[:, e],
                             io["moe_w1"][e].rearrange("(c p) o -> p c o", p=P)).then_inc(w_loaded.sem, 16)
                sp.dma_start(w2[:, :].rearrange("p (e c o) -> p e c o", e=E, c=EC)[:, e],
                             io["moe_w2"][e].rearrange("(c p) o -> p c o", p=P)).then_inc(w_loaded.sem, 16)
            sp.wait_ge(loaded.sem, 32)

        @block.gpsimd
        def _(pool):
            pool.memset(zero[:, :, :], 0.0).then_inc(zero_ready.sem, 1)
            pool.wait_ge(zero_stored.sem, 16)

        @block.tensor
        def _(pe):
            pe.wait_ge(loaded.sem, 32)
            with pe.Fori(1, GROUPS + 1, 1) as r:
                for c in range(CH):
                    pe.wait_ge(ring.drained(("xT", c)), ring.free(r, ("xT", c)))
                    for t in range(G):
                        pe.wait_ge(xn_ready.sem, xn_ready.at(r, t + 1))
                        mm = pe.transpose(ring.bank(("xT", c))[:, t * P:(t + 1) * P], xn[:, 0, t, c * P:(c + 1) * P], ident[:, :])
                    mm.then_inc(ring.filled(("xT", c)), 1)
                for c in range(CH):
                    pe.wait_ge(ring.drained(("xT", c)), ring.full(r, ("xT", c)))
                pe.wait_ge(ring.drained("logits"), ring.free(r, "logits"))
                for t in range(G):
                    for k in range(CH):
                        mm = pe.matmul(ring.bank("logits")[:, t * E:(t + 1) * E], xT[:, k, t * S:(t + 1) * S], router[:, k, :],
                                       start=(k == 0), stop=(k == CH - 1))
                mm.then_inc(ring.filled("logits"), 1)

        @block.scalar
        def _(act):
            with act.Fori(1, GROUPS + 1, 1) as r:
                for c in range(CH):
                    act.wait_ge(ring.filled(("xT", c)), ring.full(r, ("xT", c)))
                    act.wait_ge(ring.filled("logits"), ring.free(r, "logits"))
                    act.copy(xT[:, c, :], ring.bank(("xT", c))[:, :]).then_inc(ring.drained(("xT", c)), 1)
                act.wait_ge(step.sem, step.at(r, 2))
                act.activation(prob[:, :, :], prob[:, :, :], ACT.Exp).then_inc(exp_ready.sem, 1)

        @block.vector
        def _(dve):
            dve.wait_ge(loaded.sem, 32)
            with dve.Fori(1, GROUPS + 1, 1) as r:
                for t in range(G):
                    dve.tensor_scalar(xn[:, 0, t, :], st.x[:, seq(r, t)], mean[:, seq(r, t, 1)],
                                      rstd[:, seq(r, t, 1)], ALU.subtract, ALU.mult).then_inc(xn_ready.sem, 1)
                logits = ring.bank("logits")[:, 0:G * E].rearrange("p (t e) -> p t e", e=E)
                dve.wait_ge(ring.filled("logits"), ring.full(r, "logits"))
                dve.tensor_reduce(top[:, :], logits, AX.X, ALU.max).then_inc(step.sem, 1)
                dve.wait_ge(step.sem, step.at(r, 1))
                dve.tensor_tensor(prob[:, :, :], logits, bc(top[:, :, None], [P, G, E]), ALU.subtract).then_inc(step.sem, 1)
                dve.wait_ge(exp_ready.sem, exp_ready.at(r, 1))
                dve.tensor_reduce(total[:, :], prob[:, :, :], AX.X, ALU.add).then_inc(ring.drained("logits"), 1)
                dve.wait_ge(ring.drained("logits"), ring.full(r, "logits"))
                dve.reciprocal(recip[:, :], total[:, :]).then_inc(step.sem, 1)
                dve.wait_ge(step.sem, step.at(r, 3))
                dve.tensor_tensor(prob[:, :, :], prob[:, :, :], bc(recip[:, :, None], [P, G, E]), ALU.mult).then_inc(step.sem, 1)
                dve.wait_ge(step.sem, step.at(r, 4))
                other, this = (bc(a, [P, G, E, E]) for a in (prob[:, :, None, :], prob[:, :, :, None]))
                dve.tensor_tensor(above[:, :, :, :], other, this, ALU.is_gt).then_inc(step.sem, 1)
                dve.tensor_tensor(tied[:, :, :, :], other, this, ALU.is_equal).then_inc(step.sem, 1)
                flat_above, flat_tied = (a[:, :, :, :].rearrange("p t i j -> p t (i j)") for a in (above, tied))
                dve.wait_ge(step.sem, step.at(r, 6))
                dve.tensor_tensor(flat_tied, flat_tied, bc(before[:, :, :], [P, G, E * E]), ALU.mult).then_inc(step.sem, 1)
                dve.wait_ge(step.sem, step.at(r, 7))
                dve.tensor_tensor(flat_above, flat_above, flat_tied, ALU.add).then_inc(step.sem, 1)
                dve.wait_ge(step.sem, step.at(r, 8))
                dve.tensor_reduce(rank[:, :, :], above[:, :, :, :], AX.X, ALU.add).then_inc(step.sem, 1)
                dve.wait_ge(step.sem, step.at(r, 9))
                for w in range(2):
                    dve.tensor_scalar(flag[w][:, group(r, E)].rearrange("p (t e) -> p t e", e=E), rank[:, :, :], float(w), None,
                                      ALU.is_equal).then_inc(step.sem, 1)
                    dve.scalar_tensor_tensor(kept_prob[w][:, group(r, E)].rearrange("p (t e) -> p t e", e=E), rank[:, :, :], float(w),
                                             prob[:, :, :], ALU.is_equal, ALU.mult).then_inc(step.sem, 1)


def sort_stage(nc, io, flag, kept_prob, weight, place, owner):
    with ExitStack() as ctx:
        def sb(n, s, dt=F32):
            return ctx.enter_context(nc.sbuf_tensor(f"sort_{n}", s, dt))

        PAD = B // 2
        EPAD = E // 2
        earlier, ones = sb("earlier", [P, P], BF16), sb("ones", [P, P], BF16)
        tile_no = sb("tile_no", [P, TILES])
        chosen = sb("chosen", [P, B * E], BF16)
        run = [sb(f"run{i}", [P, PAD + B, E]) for i in range(2)]
        need = [sb(f"need{i}", [P, EPAD + E]) for i in range(2)]
        base = sb("base", [P, E])
        slot = sb("slot", [P, B, E])
        mine = [sb(f"mine{w}", [P, B, E]) for w in range(2)]
        reached = sb("reached", [P, TILES, E])
        count = sb("count", [P, TILES])
        position = sb("position", [P, 2, B])
        loaded, cleared = Tally(nc, "sort_loaded", 0), Tally(nc, "sort_cleared", 0)
        chosen_ready, counted = Tally(nc, "sort_chosen_ready", 0), Tally(nc, "sort_counted", 0)
        step = Tally(nc, "sort_step", 0)
        before_bank = ctx.enter_context(nc.psum_tensor("sort_before", [P, 512], F32))
        total_bank = ctx.enter_context(nc.psum_tensor("sort_total", [P, 512], F32))
        block = ctx.enter_context(nc.Block())

        @block.sync
        def _(sp):
            sp.dma_start(earlier[:, :], io["earlier"]).then_inc(loaded.sem, 16)
            sp.dma_start(tile_no[:, :], io["tile_no"]).then_inc(loaded.sem, 16)
            sp.wait_ge(loaded.sem, 32)

        @block.gpsimd
        def _(pool):
            pool.memset(ones[:, :], 1.0).then_inc(cleared.sem, 1)
            for i in range(2):
                pool.memset(run[i][:, 0:PAD, :], 0.0).then_inc(cleared.sem, 1)
                pool.memset(need[i][:, 0:EPAD], 0.0).then_inc(cleared.sem, 1)

        @block.tensor
        def _(pe):
            pe.wait_ge(loaded.sem, 32)
            pe.wait_ge(cleared.sem, 5)
            pe.wait_ge(chosen_ready.sem, 1)
            pe.matmul(before_bank[:, 0:B * E], earlier[:, :], chosen[:, :], start=True, stop=True).then_inc(counted.sem, 1)
            pe.matmul(total_bank[:, 0:B * E], ones[:, :], chosen[:, :], start=True, stop=True).then_inc(counted.sem, 1)

        @block.vector
        def _(dve):
            dve.tensor_tensor(chosen[:, :], flag[0][:, :], flag[1][:, :], ALU.add).then_inc(chosen_ready.sem, 1)
            for w in range(2):
                dve.tensor_reduce(weight[w][:, :], kept_prob[w][:, :].rearrange("p (b e) -> p b e", e=E), AX.X, ALU.add)
            dve.wait_ge(loaded.sem, 32)
            dve.wait_ge(cleared.sem, 5)
            dve.wait_ge(counted.sem, 2)
            dve.tensor_copy(run[0][:, PAD:, :], total_bank[:, 0:B * E].rearrange("p (b e) -> p b e", e=E)).then_inc(step.sem, 1)
            at, n = 0, 1
            for reach in (1, 2, 4, 8, 16):
                dve.wait_ge(step.sem, n)
                dve.tensor_tensor(run[1 - at][:, PAD:, :], run[at][:, PAD:, :], run[at][:, PAD - reach:PAD + B - reach, :],
                                  ALU.add).then_inc(step.sem, 1)
                at, n = 1 - at, n + 1
            run_end = run[at]
            dve.wait_ge(step.sem, n)
            dve.tensor_scalar(need[1][:, EPAD:], run_end[:, PAD + B - 1, :], 1.0 / P, (P - 1) / P - 0.5 + 0.5 / P,
                              ALU.mult, ALU.add).then_inc(step.sem, 1)
            dve.wait_ge(step.sem, n + 1)
            dve.tensor_scalar(base[:, :], need[1][:, EPAD:], ROUND, None, ALU.add).then_inc(step.sem, 1)
            dve.wait_ge(step.sem, n + 2)
            dve.tensor_scalar(need[0][:, EPAD:], base[:, :], -ROUND, None, ALU.add).then_inc(step.sem, 1)
            at, n = 0, n + 3
            for reach in (1, 2, 4):
                dve.wait_ge(step.sem, n)
                dve.tensor_tensor(need[1 - at][:, EPAD:], need[at][:, EPAD:], need[at][:, EPAD - reach:EPAD + E - reach],
                                  ALU.add).then_inc(step.sem, 1)
                at, n = 1 - at, n + 1
            dve.wait_ge(step.sem, n)
            dve.tensor_scalar(base[:, :], need[at][:, EPAD - 1:EPAD + E - 1], float(P), None, ALU.mult).then_inc(step.sem, 1)
            dve.tensor_tensor(slot[:, :, :], before_bank[:, 0:B * E].rearrange("p (b e) -> p b e", e=E),
                              run_end[:, PAD - 1:PAD + B - 1, :], ALU.add).then_inc(step.sem, 1)
            dve.tensor_tensor(reached[:, :, :], bc(tile_no[:, :, None], [P, TILES, E]),
                              bc(need[at][:, None, EPAD:], [P, TILES, E]), ALU.is_ge).then_inc(step.sem, 1)
            dve.wait_ge(step.sem, n + 3)
            dve.tensor_tensor(slot[:, :, :], slot[:, :, :], bc(base[:, None, :], [P, B, E]), ALU.add).then_inc(step.sem, 1)
            dve.tensor_reduce(count[:, :], reached[:, :, :], AX.X, ALU.add).then_inc(step.sem, 1)
            dve.wait_ge(step.sem, n + 5)
            for w in range(2):
                dve.tensor_tensor(mine[w][:, :, :].rearrange("p b e -> p (b e)"), slot[:, :, :].rearrange("p b e -> p (b e)"),
                                  flag[w][:, :], ALU.mult).then_inc(step.sem, 1)
            dve.tensor_scalar(owner[:, :], count[0:1, :], float(E - 1), None, ALU.min)
            dve.wait_ge(step.sem, n + 7)
            for w in range(2):
                dve.tensor_reduce(position[:, w, :], mine[w][:, :, :], AX.X, ALU.add).then_inc(step.sem, 1)
            dve.wait_ge(step.sem, n + 9)
            dve.tensor_copy(place[:, :, :].rearrange("p b w -> p w b"), position[:, :, :])


def tiles_stage(nc, ident, w1, w2, W1, W2, owner, w_loaded, slot_x, slot_y):
    with ExitStack() as ctx:
        def sb(n, s, dt=F32):
            return ctx.enter_context(nc.sbuf_tensor(f"tile_{n}", s, dt))

        def bank(n):
            return ctx.enter_context(nc.psum_tensor(f"tile_{n}_bank", [P, 512], F32))

        def signal(n):
            return nc.alloc_semaphore(f"tile_{n}")

        xr, xT = sb("rows", [P, 2, D]), sb("xT", [P, 2, CH * P])
        sg, y, yT = sb("silu", [P, 2, EI]), sb("y", [P, 2, EI]), sb("yT", [P, 2, EI])
        res = sb("result", [P, 2, D])
        xT_bank, yT_bank = bank("xT"), bank("yT")
        gate_bank, up_bank, res_bank = ([bank(f"{n}{s}") for s in range(2)] for n in ("gate", "up", "res"))
        x_turned, x_kept, gate_full, up_full = signal("x_turned"), signal("x_kept"), signal("gate_full"), signal("up_full")
        silu_ready, y_ready, y_turned, y_kept = signal("silu_ready"), signal("y_ready"), signal("y_turned"), signal("y_kept")
        res_full, res_kept = signal("res_full"), signal("res_kept")
        x_loaded, res_stored = ([signal(f"{n}{s}") for s in range(2)] for n in ("x_loaded", "res_stored"))
        block = ctx.enter_context(nc.Block())

        @block.sync
        def _(sp):
            def step(r, c):
                t = Tile(r, c)
                if t.exists:
                    wait_count(sp, x_turned, t.number - 1)
                    sp.dma_start(xr[:, t.slot, :], slot_x[bass.ds(t.number * P, P), :]).then_inc(x_loaded[t.slot], 16)
                t = Tile(r, c - 5)
                if t.exists:
                    sp.wait_ge(res_kept, t.number + 1)
                    sp.dma_start(slot_y[bass.ds(t.number * P, P), :], res[:, t.slot, :]).then_inc(res_stored[t.slot], 16)

            tile_steps(sp, step, 5)
            for s in range(2):
                sp.wait_ge(res_stored[s], 16 * len(range(s, TILES, 2)))

        @block.tensor
        def _(pe):
            def step(r, c):
                t = Tile(r, c)
                if t.exists:
                    pe.wait_ge(x_loaded[t.slot], (t.use + 1) * 16)
                    wait_count(pe, x_kept, t.number)
                    for k in range(CH):
                        mm = pe.transpose(xT_bank[:, k * P:(k + 1) * P], xr[:, t.slot, k * P:(k + 1) * P], ident[:, :])
                    mm.then_inc(x_turned, 1)
                t = Tile(r, c - 1)
                if t.exists:
                    e = pe.value_load(owner[0:1, bass.ds(t.number, 1)], min_val=0, max_val=E - 1)
                    pe.wait_ge(x_kept, t.number + 1)
                    for banks, col, full, drained in ((gate_bank, 0, gate_full, silu_ready), (up_bank, EI, up_full, y_ready)):
                        wait_count(pe, drained, t.number - 1)
                        for k in range(CH):
                            mm = pe.matmul(banks[t.slot][:, :], xT[:, t.slot, k * P:(k + 1) * P],
                                           w1[:, bass.ds(e * W1 + (k * 2 * EI + col), EI)], start=(k == 0), stop=(k == CH - 1))
                        mm.then_inc(full, 1)
                t = Tile(r, c - 2)
                if t.exists:
                    pe.wait_ge(y_ready, t.number + 1)
                    wait_count(pe, y_kept, t.number)
                    for k in range(EC):
                        mm = pe.transpose(yT_bank[:, k * P:(k + 1) * P], y[:, t.slot, k * P:(k + 1) * P], ident[:, :])
                    mm.then_inc(y_turned, 1)
                t = Tile(r, c - 3)
                if t.exists:
                    e = pe.value_load(owner[0:1, bass.ds(t.number, 1)], min_val=0, max_val=E - 1)
                    pe.wait_ge(y_kept, t.number + 1)
                    wait_count(pe, res_kept, t.number - 1)
                    for k in range(EC):
                        mm = pe.matmul(res_bank[t.slot][:, 0:D], yT[:, t.slot, k * P:(k + 1) * P],
                                       w2[:, bass.ds(e * W2 + k * D, D)], start=(k == 0), stop=(k == EC - 1))
                    mm.then_inc(res_full, 1)

            pe.wait_ge(w_loaded.sem, 16 * 2 * E)
            tile_steps(pe, step, 3)

        @block.scalar
        def _(act):
            def step(r, c):
                t = Tile(r, c)
                if t.exists:
                    act.wait_ge(x_turned, t.number + 1)
                    wait_count(act, up_full, t.number - 1)
                    act.copy(xT[:, t.slot, :], xT_bank[:, 0:CH * P]).then_inc(x_kept, 1)
                t = Tile(r, c - 1)
                if t.exists:
                    act.wait_ge(gate_full, t.number + 1)
                    wait_count(act, y_ready, t.number - 1)
                    act.activation(sg[:, t.slot, :], gate_bank[t.slot][:, :], ACT.Silu).then_inc(silu_ready, 1)
                t = Tile(r, c - 2)
                if t.exists:
                    act.wait_ge(y_turned, t.number + 1)
                    wait_count(act, res_full, t.number - 1)
                    act.copy(yT[:, t.slot, :], yT_bank[:, :]).then_inc(y_kept, 1)

            tile_steps(act, step, 2)

        @block.vector
        def _(dve):
            def step(r, c):
                t = Tile(r, c - 1)
                if t.exists:
                    dve.wait_ge(up_full, t.number + 1)
                    dve.wait_ge(silu_ready, t.number + 1)
                    wait_count(dve, y_turned, t.number - 1)
                    dve.tensor_tensor(y[:, t.slot, :], sg[:, t.slot, :], up_bank[t.slot][:, :], ALU.mult).then_inc(y_ready, 1)
                t = Tile(r, c - 3)
                if t.exists:
                    dve.wait_ge(res_full, t.number + 1)
                    wait_count(dve, res_stored[t.slot], t.use * 16)
                    dve.tensor_copy(res[:, t.slot, :], res_bank[t.slot][:, 0:D]).then_inc(res_kept, 1)

            tile_steps(dve, step, 3)


def program(nc, io, out, phases=(0, 6)):
    with ExitStack() as ctx:
        ident = ctx.enter_context(nc.sbuf_tensor("ident", [P, P], F32))
        st = Stream(ctx, nc)
        load_phase(nc, st, io, ident)
        every = [lambda: attention_phase(nc, st, io, ident, "self", "self"),
                 lambda: attention_phase(nc, st, io, ident, "mask", "masked"),
                 lambda: bitlinear_phase(nc, st, io, ident),
                 lambda: second_layer_self(nc, st, io, ident),
                 lambda: attention_phase(nc, st, io, ident, "cross", "cross"),
                 lambda: experts_phase(nc, st, io, ident, out)]
        for phase in every[phases[0]:phases[1]]:
            with nc.cleanup_on_exit():
                phase()
        if phases[1] < len(every):
            store_phase(nc, st, out)


def store_phase(nc, st, out):
    with ExitStack() as ctx:
        stored = Tally(nc, "stored", 0)
        block = ctx.enter_context(nc.Block())

        @block.sync
        def _(sp):
            sp.dma_start(out.rearrange("(n p) d -> p n d", p=P), st.x[:, :].rearrange("p (n d) -> p n d", n=B)).then_inc(stored.sem, 16)
            sp.wait_ge(stored.sem, 16)


def tables():
    bf16 = mybir.dt.np(BF16)
    pos = np.arange(NC + GS, dtype=np.float32)[:, None]
    div = np.exp(np.arange(0, HD, 2, dtype=np.float32) * np.float32(-np.log(10000.0) / HD))
    ang = (pos * div).astype(np.float32)
    pe = np.stack([np.sin(ang), np.cos(ang)], axis=-1).reshape(NC + GS, HD)
    rot = np.empty((HD, NC + GS), np.float32)
    rot[0::2] = -pe[:, HD // 2:].T
    rot[1::2] = pe[:, :HD // 2].T
    rows = np.tile(rot, (HH, 1))
    heads = np.repeat(np.eye(HH, dtype=np.float32), HD, axis=0)
    local = np.arange(GS)
    q_pos = np.concatenate([local, local])
    k_pos = np.concatenate([local, NC + local, np.arange(NC)])
    rot_k = heads[:, :, None] * rows[:, None, k_pos]
    seen = np.zeros((P, UH, KL), np.float32)
    seen[:, :, 0:GS] = (local[None, :] <= (np.arange(P) % GS)[:, None])[:, None, :]
    seen[GS:, :, GS:] = 1.0
    parts, rest = np.zeros((P, 1), np.float32), np.float64(-MASK_FILL)
    for i in range(3):
        parts[i] = np.float32(np.float64(rest).astype(bf16))
        rest -= np.float64(parts[i, 0])
    assert rest == 0
    return {
        "ident": np.eye(P, dtype=np.float32),
        "identb": np.eye(P, dtype=np.float32).astype(bf16),
        "rot_q": rows[:, q_pos], "rot_k": rot_k, "heads": heads, "parts": parts,
        "half_heads": 0.5 * heads, "before": np.tile(np.tril(np.ones((E, E), np.float32), -1).reshape(1, -1), (P, 1)),
        "earlier": np.triu(np.ones((P, P), np.float32), 1).astype(bf16),
        "tile_no": np.tile(np.arange(TILES, dtype=np.float32), (P, 1)),
        "causal": np.where(seen > 0, 0.0, -1e30).astype(bf16),
    }


def chunked(vec):
    return vec.reshape(-1, P).T


def layout(a):
    swap = np.arange(D).reshape(-1, 2)[:, ::-1].reshape(-1)
    io = dict(tables())
    io["x"] = a["x"].reshape(B * S, D)
    io["ctx"] = a["ctx_1024"].reshape(B * S, D)
    mask = a["mask_BxS2_bf1"].reshape(GROUPS, G * S).view(np.uint8)
    io["mask"] = np.concatenate([mask[:1], mask])
    w, b = a["L0_attn_w_attn"], a["L0_attn_b_attn"]
    io["self_wq"], io["self_wk"], io["self_wv"] = w[0:D][swap].T, w[D:2 * D][swap].T, w[2 * D:].T
    io["self_bq"], io["self_bk"], io["self_bv"] = chunked(b[0:D][swap]), chunked(b[D:2 * D][swap]), b[2 * D:]
    io["self_wo"], io["self_bo"] = a["L0_attn_w_proj"].T, a["L0_attn_b_proj"]
    io["self_assign"] = np.repeat(a["L0_attn_w_assign"][0:NC], 2, axis=0).T
    for n in "qkvo":
        io[f"mask_w{n}"] = a[f"L0_xattn_W{n}"].T
        io[f"cross_w{n}"] = a[f"L1_xattn_w_{n}"].T
    io["mask_bq"], io["mask_bk"] = chunked(a["L0_xattn_bq"]), chunked(a["L0_xattn_bk"])
    for n in ("gate", "up", "down"):
        io[f"bit_{n}"] = a[f"L0_ffn_w_{n}"].T
    io["perf_wq"], io["perf_wk"], io["perf_wv"] = (a[f"L1_attn_w{n}"].reshape(D, D) for n in "qkv")
    io["perf_wo"] = a["L1_attn_wo"]
    omega = np.zeros((HH, HD, HH, NF), np.float32)
    for h in range(HH):
        omega[h, :, h, :] = a["L1_attn_omega"].T
    io["omega"] = omega.reshape(P, HH * NF)
    for n in ("ln1_g", "ln1_b", "ln2_g", "ln2_b", "b2"):
        io[f"mlp_{n}"] = a[f"L1_attn_{n}"]
    io["mlp_w1"], io["mlp_w2"], io["mlp_b1"] = a["L1_attn_w1"], a["L1_attn_w2"], chunked(a["L1_attn_b1"])
    io["moe_w1"] = a["L1_ffn_w1"].transpose(0, 2, 1)
    io["moe_w2"] = a["L1_ffn_w2"].transpose(0, 2, 1)
    io["router"] = a["L1_ffn_router_w"].T
    io["mask_bv"], io["mask_bo"] = a["L0_xattn_bv"], a["L0_xattn_bo"]
    return io


def kernel(**inputs):
    import concourse.bacc as bacc
    from concourse.bass_utils import run_bass_kernel_spmd

    arrays = {n: np.ascontiguousarray(v) for n, v in layout({n: np.asarray(v) for n, v in inputs.items()}).items()}
    nc = bacc.Bacc("TRN2", target_bir_lowering=False, num_devices=1)
    io = {n: nc.dram_tensor(f"in_{n}", v.shape, mybir.dt.from_np(v.dtype), kind="ExternalInput").ap()
          for n, v in arrays.items()}
    out = nc.dram_tensor("out_0", (B * S, D), F32, kind="ExternalOutput").ap()
    program(nc, io, out)
    got = run_bass_kernel_spmd(nc, [{f"in_{n}": v for n, v in arrays.items()}], core_ids=[0])
    return got.results[0]["out_0"].reshape(B, S, D)
```

```python
from contextlib import ExitStack

import numpy as np

import concourse.bass as bass
import concourse.mybir as mybir

F32 = mybir.dt.float32
BF16 = mybir.dt.bfloat16
U8 = mybir.dt.uint8
I32 = mybir.dt.int32
ALU = mybir.AluOpType
ACT = mybir.ActivationFunctionType
AX = mybir.AxisListType

P = 128
B, S, D = 32, 128, 256
CH = D // P
H, HD = 16, 16
HH = H // CH
VW = HD + 1
G = 4
GROUPS = B // G
UH = 4
UNITS = G * H // UH
NC = 32
GS = 64
KS = S + NC
KL = GS + NC
EPS = 1e-5
EPS_IN = 1e-6
ROUND = 1.5 * 2.0**23
MASK_FILL = -1e8
INNER = 1024
IC = INNER // P
NF = 64
E, EI = 8, 512
EC = EI // P
ROW = D + 2
TILES = (2 * B * S + E * (P - 1)) // P


class Tally:

    def __init__(self, nc, name, per_turn, start=None):
        self.sem = nc.alloc_semaphore(name)
        self.per_turn = per_turn
        if per_turn and start is None:
            nc.gpsimd.sem_inc(self.sem, per_turn)

    def at(self, r, k):
        return r * self.per_turn + k


class Ring:

    def __init__(self, ctx, nc, name, banks, jobs, skipped=None):
        self.banks = [ctx.enter_context(nc.psum_tensor(f"{name}_bank{b}", [P, 512], F32)) for b in range(banks)]
        self._filled = [nc.alloc_semaphore(f"{name}_filled{b}") for b in range(banks)]
        self._drained = [nc.alloc_semaphore(f"{name}_drained{b}") for b in range(banks)]
        self.place = {job: (i % banks, i // banks) for i, job in enumerate(jobs)}
        self.uses = [len(jobs[b::banks]) for b in range(banks)]
        skipped = len(jobs) if skipped is None else skipped
        for b in range(banks):
            for sem in (self._filled[b], self._drained[b]):
                nc.gpsimd.sem_inc(sem, len(range(b, skipped, banks)))

    def bank(self, job):
        return self.banks[self.place[job][0]]

    def filled(self, job):
        return self._filled[self.place[job][0]]

    def drained(self, job):
        return self._drained[self.place[job][0]]

    def full(self, r, job):
        b, turn = self.place[job]
        return r * self.uses[b] + turn + 1

    def free(self, r, job):
        b, turn = self.place[job]
        return r * self.uses[b] + turn


def bc(ap, shape):
    return ap.to_broadcast(shape)


class Stream:

    def __init__(self, ctx, nc):
        def sb(n, s):
            return ctx.enter_context(nc.sbuf_tensor(n, s, F32))
        self.x = sb("stream", [P, B * D])
        self.mean = [sb(f"mean{i}", [P, B]) for i in range(2)]
        self.rstd = [sb(f"rstd{i}", [P, B]) for i in range(2)]
        self.mean_in, self.rstd_in = sb("mean_in", [P, B]), sb("rstd_in", [P, B])
        self.now = 0

    def turn(self):
        self.now ^= 1


def seq(r, t, width=D):
    return bass.ds(r * (G * width) + (t - G) * width, width)


def group(r, width):
    return bass.ds(r * (G * width) - G * width, G * width)


class Rows:

    def __init__(self, ctx, nc, name, dest, mean, rstd, eps):
        def sb(n, s):
            return ctx.enter_context(nc.sbuf_tensor(f"{name}_{n}", s, F32))

        self.dest, self.mean, self.rstd, self.eps = dest, mean, rstd, eps
        self.slot = sb("rows", [P, 2, D])
        self.raw = sb("rows_raw", [P, 2, 6])
        self.mv = sb("rows_mean_var", [P, G, 2])
        self.var = sb("rows_var", [P, G])
        self.mhalf = sb("rows_mhalf", [P, G])
        self.const_ready = Tally(nc, f"{name}_mhalf_ready", 0)
        self.stored = Tally(nc, f"{name}_rows_stored", G)
        self.raw_ready = Tally(nc, f"{name}_rows_stats", G)
        self.aggr_ready = Tally(nc, f"{name}_rows_aggr", G)
        self.mean_stored = Tally(nc, f"{name}_mean_stored", 1)
        self.var_ready = Tally(nc, f"{name}_rstd_step", 2)

    def pool_start(self, pool):
        pool.memset(self.mhalf[:, :], -0.5).then_inc(self.const_ready.sem, 1)
        pool.wait_ge(self.const_ready.sem, 1)

    def wait_slot(self, dve, r, t):
        dve.wait_ge(self.stored.sem, self.stored.at(r, t - 1 if t >= 2 else 0))

    def take_stats(self, dve, r, t, written, count):
        dve.wait_ge(written, count)
        dve.bn_stats(self.raw[:, t % 2, :], self.slot[:, t % 2, :]).then_inc(self.raw_ready.sem, 1)
        dve.wait_ge(self.const_ready.sem, 1)
        dve.wait_ge(self.raw_ready.sem, self.raw_ready.at(r, t + 1))
        if t == 0:
            dve.wait_ge(self.mean_stored.sem, self.mean_stored.at(r, 0))
            dve.wait_ge(self.var_ready.sem, self.var_ready.at(r, 0))
        dve.bn_aggr(self.mv[:, t, :], self.raw[:, t % 2, :]).then_inc(self.aggr_ready.sem, 1)

    def store(self, pool, r, t):
        pool.wait_ge(self.const_ready.sem, 1)
        pool.wait_ge(self.raw_ready.sem, self.raw_ready.at(r, t + 1))
        pool.tensor_copy(self.dest[:, seq(r, t)], self.slot[:, t % 2, :]).then_inc(self.stored.sem, 1)

    def store_stats(self, pool, r):
        pool.wait_ge(self.const_ready.sem, 1)
        pool.wait_ge(self.aggr_ready.sem, self.aggr_ready.at(r, G))
        pool.tensor_copy(self.mean[:, group(r, 1)], self.mv[:, :, 0]).then_inc(self.mean_stored.sem, 1)
        pool.tensor_scalar(self.var[:, :], self.mv[:, :, 1], self.eps, None, ALU.add).then_inc(self.var_ready.sem, 1)
        pool.wait_ge(self.const_ready.sem, 1)
        pool.wait_ge(self.var_ready.sem, self.var_ready.at(r, 1))
        pool.tensor_tensor(self.rstd[:, group(r, 1)], self.var[:, :], self.mhalf[:, :], ALU.pow).then_inc(self.var_ready.sem, 1)


class Region:

    def __init__(self, ctx, nc, name, columns):
        self.raw = ctx.enter_context(nc.sbuf_tensor(name, [P, columns], F32))
        self.taken = 0

    def restart(self):
        self.taken = 0
        return self

    def take(self, *shape, dt=F32):
        per_word = 4 // np.dtype(mybir.dt.np(dt)).itemsize
        words = -(-int(np.prod(shape)) // per_word)
        assert self.taken + words <= self.raw.shape[1]
        flat = self.raw[:, self.taken:self.taken + words]
        self.taken += words
        if dt != F32:
            flat = flat.bitcast(dt)
        if len(shape) == 2:
            return flat.rearrange("p (a b) -> p a b", a=shape[0])
        return flat


class AttentionWeights:
    def __init__(self, nc, region, name, kind):
        self.name, self.kind = name, kind
        self.own, self.biased = kind == "self", kind != "cross"
        self.wq, self.wk, self.wv, self.wo = (region.take(CH, D) for _ in range(4))
        if self.biased:
            self.bq, self.bk = region.take(CH), region.take(CH)
            self.bv, self.bo = region.take(D), region.take(D)
        if self.own:
            self.assign = region.take(CH, GS)
            self.rot_q = region.take(S)
            self.spread = region.take(HH, KS)
            self.causal = region.take(UH, KL, dt=BF16)
            self.identb = region.take(P, dt=BF16)
        else:
            self.spread = region.take(HH)
            self.parts = region.take(1)
        self.loaded = Tally(nc, f"{name}_weights_loaded", 0)
        self.total = 16 * (4 + (4 if self.biased else 0) + (5 if self.own else 1) + (1 if kind == "masked" else 0))

    def fetch(self, eng, io):
        done = self.loaded.sem
        for tile, key in ((self.wq, "wq"), (self.wk, "wk"), (self.wv, "wv"), (self.wo, "wo")):
            eng.dma_start(tile[:, :, :], io[f"{self.name}_{key}"].rearrange("(c p) o -> p c o", p=P)).then_inc(done, 16)
        if self.biased:
            for tile, key in ((self.bq, "bq"), (self.bk, "bk")):
                eng.dma_start(tile[:, :], io[f"{self.name}_{key}"]).then_inc(done, 16)
            for tile, key in ((self.bv, "bv"), (self.bo, "bo")):
                eng.dma_start(tile[:, :], io[f"{self.name}_{key}"].partition_broadcast(P)).then_inc(done, 16)
        if self.own:
            eng.dma_start(self.assign[:, :, :], io[f"{self.name}_assign"].rearrange("(c p) o -> p c o", p=P)).then_inc(done, 16)
            eng.dma_start(self.rot_q[:, :], io["rot_q"]).then_inc(done, 16)
            eng.dma_start(self.spread[:, :, :], io["rot_k"]).then_inc(done, 16)
            eng.dma_start(self.causal[:, :, :], io["causal"]).then_inc(done, 16)
            eng.dma_start(self.identb[:, :], io["identb"]).then_inc(done, 16)
        else:
            eng.dma_start(self.spread[:, :], io["heads"]).then_inc(done, 16)
            if self.kind == "masked":
                eng.dma_start(self.parts[:, :], io["parts"]).then_inc(done, 16)


class BitlinearWeights:
    def __init__(self, nc, region):
        self.raw = {n: region.take(CH * INNER) for n in ("gate", "up", "down")}
        self.identb = region.take(P, dt=BF16)
        self.loaded = Tally(nc, "bit_weights_loaded", 0)

    def fetch(self, eng, io):
        for n, chunks in (("gate", CH), ("up", CH), ("down", IC)):
            eng.dma_start(self.raw[n].rearrange("p (c o) -> p c o", c=chunks),
                          io[f"bit_{n}"].rearrange("(c p) o -> p c o", p=P)).then_inc(self.loaded.sem, 16)
        eng.dma_start(self.identb[:, :], io["identb"]).then_inc(self.loaded.sem, 16)


class PerformerWeights:
    def __init__(self, nc, region):
        self.wq, self.wk, self.wv, self.wo = (region.take(CH, D) for _ in range(4))
        self.omega = region.take(HH * NF)
        self.half_heads = region.take(HH)
        self.loaded = Tally(nc, "perf_weights_loaded", 0)

    def fetch(self, eng, io):
        for tile, key in ((self.wq, "wq"), (self.wk, "wk"), (self.wv, "wv"), (self.wo, "wo")):
            eng.dma_start(tile[:, :, :], io[f"perf_{key}"].rearrange("(c p) o -> p c o", p=P)).then_inc(self.loaded.sem, 16)
        eng.dma_start(self.omega[:, :], io["omega"]).then_inc(self.loaded.sem, 16)
        eng.dma_start(self.half_heads[:, :], io["half_heads"]).then_inc(self.loaded.sem, 16)


class MlpWeights:
    def __init__(self, nc, region):
        self.w1, self.w2, self.b1 = region.take(CH, INNER), region.take(IC, D), region.take(IC)
        self.g1, self.c1, self.g2, self.c2, self.b2 = (region.take(D) for _ in range(5))
        self.loaded = Tally(nc, "mlp_weights_loaded", 0)

    def fetch(self, eng, io):
        eng.dma_start(self.w1[:, :, :], io["mlp_w1"].rearrange("(c p) o -> p c o", p=P)).then_inc(self.loaded.sem, 16)
        eng.dma_start(self.w2[:, :, :], io["mlp_w2"].rearrange("(c p) o -> p c o", p=P)).then_inc(self.loaded.sem, 16)
        eng.dma_start(self.b1[:, :], io["mlp_b1"]).then_inc(self.loaded.sem, 16)
        for tile, key in ((self.g1, "ln1_g"), (self.c1, "ln1_b"), (self.g2, "ln2_g"), (self.c2, "ln2_b"), (self.b2, "b2")):
            eng.dma_start(tile[:, :], io[f"mlp_{key}"].partition_broadcast(P)).then_inc(self.loaded.sem, 16)


class RouterTables:
    def __init__(self, nc, region):
        self.router = region.take(CH, E)
        self.earlier = region.take(P, dt=BF16)
        self.tile_no = region.take(TILES)
        self.before = region.take(1, E * E)
        self.home = region.take(2 * B)
        self.spare = region.take(TILES)
        self.loaded = Tally(nc, "moe_tables_loaded", 0)
        self.total = 16 * 6

    def fetch(self, eng, io):
        eng.dma_start(self.router[:, :, :], io["router"].rearrange("(c p) e -> p c e", p=P)).then_inc(self.loaded.sem, 16)
        eng.dma_start(self.earlier[:, :], io["earlier"]).then_inc(self.loaded.sem, 16)
        eng.dma_start(self.tile_no[:, :], io["tile_no"]).then_inc(self.loaded.sem, 16)
        eng.dma_start(self.before[:, 0, :], io["before"]).then_inc(self.loaded.sem, 16)
        eng.dma_start(self.home[:, :], io["home"]).then_inc(self.loaded.sem, 16)
        eng.dma_start(self.spare[:, :], io["spare"]).then_inc(self.loaded.sem, 16)


def wait_count(eng, sem, count):
    if not isinstance(count, int) or count > 0:
        eng.wait_ge(sem, count)


def load_phase(nc, st, io, ident, following):
    with ExitStack() as ctx:
        x_loaded = Tally(nc, "ld_x_loaded", 0)
        const_loaded = Tally(nc, "ld_const_loaded", 0)
        stats_ready = Tally(nc, "ld_stats_ready", 0)
        half_ready = Tally(nc, "ld_half_ready", 0)
        aggr_ready = Tally(nc, "ld_aggr_ready", 0)
        var_ready = Tally(nc, "ld_var_ready", 0)
        raw = ctx.enter_context(nc.sbuf_tensor("ld_raw", [P, B, 6], F32))
        mv = ctx.enter_context(nc.sbuf_tensor("ld_mv", [P, B, 2], F32))
        var = ctx.enter_context(nc.sbuf_tensor("ld_var", [P, B], F32))
        mhalf = ctx.enter_context(nc.sbuf_tensor("ld_mhalf", [P, B], F32))
        block = ctx.enter_context(nc.Block())

        @block.sync
        def _(sp):
            for q in range(4):
                n = B // 4
                sp.dma_start(st.x[:, q * n * D:(q + 1) * n * D].rearrange("p (n d) -> p n d", n=n),
                             io["x"].rearrange("(n p) d -> p n d", p=P)[:, q * n:(q + 1) * n, :]).then_inc(x_loaded.sem, 16)
            sp.dma_start(ident[:, :], io["ident"]).then_inc(const_loaded.sem, 16)
            sp.wait_ge(const_loaded.sem, 16)

        @block.scalar
        def _(act):
            following.fetch(act, io)

        @block.vector
        def _(dve):
            dve.wait_ge(x_loaded.sem, 64)
            for b in range(B):
                dve.bn_stats(raw[:, b, :], st.x[:, b * D:(b + 1) * D]).then_inc(stats_ready.sem, 1)
            dve.wait_ge(stats_ready.sem, B)
            for b in range(B):
                dve.bn_aggr(mv[:, b, :], raw[:, b, :]).then_inc(aggr_ready.sem, 1)

        @block.gpsimd
        def _(pool):
            pool.memset(mhalf[:, :], -0.5).then_inc(half_ready.sem, 1)
            pool.wait_ge(aggr_ready.sem, B)
            pool.tensor_copy(st.mean[0][:, :], mv[:, :, 0])
            pool.tensor_scalar(var[:, :], mv[:, :, 1], EPS, None, ALU.add).then_inc(var_ready.sem, 1)
            pool.wait_ge(var_ready.sem, 1)
            pool.wait_ge(half_ready.sem, 1)
            pool.tensor_tensor(st.rstd[0][:, :], var[:, :], mhalf[:, :], ALU.pow).then_inc(var_ready.sem, 1)


def attention_phase(nc, st, io, ident, name, kind, weights, following):
    own = kind == "self"
    biased = kind != "cross"
    KC = KS if own else S
    KU = KL if own else S
    VR = KL if own else S
    VG = 2 if own else 1
    mean, rstd = st.mean[st.now], st.rstd[st.now]
    mean_next, rstd_next = st.mean[st.now ^ 1], st.rstd[st.now ^ 1]

    if own:
        prepared = ([("xT", c) for c in range(CH)] + ["logits"] + [("qT", c) for c in range(CH)]
                    + [("kT", c, i) for c in range(CH) for i in range(2)] + [("v", t) for t in range(G)])
    else:
        prepared = ([("xT", c) for c in range(CH)] + [("cT", c) for c in range(CH)]
                    + [("qT", c) for c in range(CH)] + [("kT", c) for c in range(CH)]
                    + [("v", i) for i in range(G // 2)])
    STEPS = UNITS + 9

    with ExitStack() as ctx:
        def sb(n, s, dt=F32):
            return ctx.enter_context(nc.sbuf_tensor(f"{name}_{n}", s, dt))

        def tally(n, per, start=None):
            return Tally(nc, f"{name}_{n}", per, start)

        wq, wk, wv, wo, spread = weights.wq, weights.wk, weights.wv, weights.wo, weights.spread
        loaded, all_loaded = weights.loaded, weights.total
        if biased:
            bq, bk, bv, bo = weights.bq, weights.bk, weights.bv, weights.bo
        if own:
            assign, rot_q, causal, identb = weights.assign, weights.rot_q, weights.causal, weights.identb
            ones = sb("ones", [P, P])
            prod = sb("prod", [P, CH, G, GS])
            expo = sb("expo", [P, G, GS])
            pair = sb("pair", [P, G * GS // 2])
            wts = sb("wts", [P, G, GS])
        else:
            cin = sb("cin", [P, G, D])
            cT = sb("cT", [P, CH, G * S])
        if kind == "masked":
            mrow = sb("mrow", [P, G * S], U8)
            mask = sb("mask", [P, G * S])
            fill = sb("fill", [P, G, 1, S], BF16)
            parts = weights.parts
            onesb = sb("onesb", [P, P], BF16)
        xn = sb("xn", [P, G, D])
        xT = sb("xT", [P, CH, G, KC])
        qT = sb("qT", [P, CH, G * S])
        kT = sb("kT", [P, CH, G, KC])
        KB = 4
        kbd = sb("kbd", [P, KB, HH, KC])
        v = sb("v", [VR, G, VG, H, VW])
        sc = sb("sc", [P, 4, UH, KU])
        mx = sb("mx", [P, 4, UH])
        pT = sb("pT", [VR, 4, UH * S])
        rs = sb("rs", [P, 2, H])
        o = sb("o", [P, 2, D])
        oT = sb("oT", [P, 2, CH, P])

        ctx_loaded = tally("context_loaded", 32 if kind == "masked" else 16, 0)
        const_ready = tally("const_ready", 0)
        xn_ready = tally("xn_ready", G, 0)
        mask_ready = tally("mask_ready", 2, 0)
        prod_ready = tally("prod_ready", CH, 0)
        v_step = tally("v_step", 3 * G, 0)
        cl_ready = tally("cluster_step", 6, 0)
        expo_ready = tally("cluster_exp_ready", 1, 0)
        xc_ready = tally("clusters_ready", CH, 0)
        kbd_early, kbd_late = tally("kbd_early", KB, 0), tally("kbd_late", KB)
        mx_ready = tally("rowmax_ready", UNITS)
        ex_ready = tally("exp_ready", UNITS)
        rs_ready = tally("recip_ready", G)
        xb_ready = tally("bias_added", G, 0)
        rows = Rows(ctx, nc, name, st.x, mean_next, rstd_next, EPS)
        wide = Ring(ctx, nc, f"{name}_wide", 3, list(range(UNITS)) + prepared, skipped=UNITS)
        tail = Ring(ctx, nc, f"{name}_tail", 1, [(what, t) for t in range(G) for what in ("oT", "y")])
        turned = Ring(ctx, nc, f"{name}_turned", 2, list(range(UNITS)))
        out = Ring(ctx, nc, f"{name}_out", 2, list(range(G)))
        block = ctx.enter_context(nc.Block())

        @block.sync
        def _(sp):
            if own:
                following.fetch(sp, io)
            else:
                context = io["ctx"].rearrange("(n p) d -> p n d", p=P)
                sp.dma_start(cin[:, :, :], context[:, 0:G, :]).then_inc(ctx_loaded.sem, 16)
                if kind == "masked":
                    sp.dma_start(mrow[:, :], io["mask"][1, :].partition_broadcast(P)).then_inc(ctx_loaded.sem, 16)
                following.fetch(sp, io)
                with sp.Fori(1, GROUPS, 1) as r:
                    sp.wait_ge(wide.filled(("cT", CH - 1)), wide.full(r - 1, ("cT", CH - 1)))
                    sp.dma_start(cin[:, :, :], context[:, bass.ds(r * G, G), :]).then_inc(ctx_loaded.sem, 16)
                    if kind == "masked":
                        sp.wait_ge(mask_ready.sem, mask_ready.at(r - 1, 1))
                        sp.dma_start(mrow[:, :].rearrange("p (a k) -> p a k", a=1),
                                     io["mask"][bass.ds(r + 1, 1), :].partition_broadcast(P)).then_inc(ctx_loaded.sem, 16)

        @block.gpsimd
        def _(pool):
            rows.pool_start(pool)
            pool.memset(v[:, :, :, :, HD:VW], 1.0).then_inc(const_ready.sem, 1)
            if own:
                pool.memset(ones[:, :], 1.0).then_inc(const_ready.sem, 1)
            elif kind == "masked":
                pool.memset(onesb[:, :], 1.0).then_inc(const_ready.sem, 1)
            pool.wait_ge(loaded.sem, all_loaded)

            table = spread[:, :, :] if own else bc(spread[:, :, None], [P, HH, KC])

            def keys(turn, j, scored, ready):
                t, c = j // 2, j % 2
                job = ("kT", c, t // 2) if own else ("kT", c)
                pool.wait_ge(wide.drained(job), wide.full(turn, job))
                pool.wait_ge(*scored)
                pool.tensor_tensor(kbd[:, j % KB, :, :], bc(kT[:, c, t, :][:, None, :], [P, HH, KC]),
                                   table, ALU.mult).then_inc(ready.sem, 1)

            def prepare_rows(r):
                if biased:
                    for t in range(G):
                        pool.wait_ge(xn_ready.sem, xn_ready.at(r, t + 1))
                        pool.tensor_tensor(st.x[:, seq(r + 1, t)], st.x[:, seq(r + 1, t)], bo[:, :], ALU.add).then_inc(xb_ready.sem, 1)

            def prepare_keys(r):
                for j in range(KB):
                    u = 2 * (j + KB) + 1
                    keys(r, j, (wide.filled(u), wide.full(r, u)), kbd_early)

            def attend(r, more):
                for j in range(KB, 2 * G):
                    u = 2 * (j - KB) + 1
                    keys(r - 1, j, (wide.filled(u), wide.full(r, u)), kbd_late)
                if more:
                    prepare_rows(r)
                for t in range(G):
                    if t == 2 and more:
                        prepare_keys(r)
                    rows.store(pool, r, t)
                rows.store_stats(pool, r)

            prepare_rows(0)
            prepare_keys(0)
            with pool.Fori(1, GROUPS, 1) as r:
                attend(r, True)
            attend(GROUPS, False)

        @block.tensor
        def _(pe):
            pe.wait_ge(loaded.sem, all_loaded)
            pe.wait_ge(const_ready.sem, 2 if own or kind == "masked" else 1)

            def wait_copied(turn, jobs):
                for job in jobs:
                    pe.wait_ge(wide.drained(job), wide.full(turn, job))

            def transposed(r, job, source, ready):
                pe.wait_ge(wide.drained(job), wide.free(r, job))
                for t in range(G):
                    if ready:
                        pe.wait_ge(xn_ready.sem, xn_ready.at(r, t + 1))
                    c = job[1]
                    mm = pe.transpose(wide.bank(job)[:, t * P:(t + 1) * P], source[:, t, c * P:(c + 1) * P], ident[:, :])
                mm.then_inc(wide.filled(job), 1)

            def project(r, job, weights, c, moving):
                pe.wait_ge(wide.drained(job), wide.free(r, job))
                n = moving[0].free_size()
                for k in range(CH):
                    mm = pe.matmul(wide.bank(job)[:, 0:n], weights[:, k, c * P:(c + 1) * P], moving[k],
                                   start=(k == 0), stop=(k == CH - 1))
                mm.then_inc(wide.filled(job), 1)

            def prepare(r, part):
                if part == 0:
                    for c in range(CH):
                        transposed(r, ("xT", c), xn, True)
                    if not own:
                        pe.wait_ge(ctx_loaded.sem, ctx_loaded.at(r + 1, 0))
                        for c in range(CH):
                            transposed(r, ("cT", c), cin, False)
                if own and part == 1:
                    pe.wait_ge(prod_ready.sem, prod_ready.at(r, CH))
                    pe.wait_ge(wide.drained("logits"), wide.free(r, "logits"))
                    for k in range(CH):
                        mm = pe.matmul(wide.bank("logits")[:, 0:G * GS], ones[:, :], prod[:, k, :, :],
                                       start=(k == 0), stop=(k == CH - 1))
                    mm.then_inc(wide.filled("logits"), 1)
                if part == 1:
                    wait_copied(r, [("xT", c) for c in range(CH)])
                    for c in range(CH):
                        project(r, ("qT", c), wq, c, [xT[:, k, :, 0:S] for k in range(CH)])
                if not own and part == 2:
                    wait_copied(r, [("cT", c) for c in range(CH)])
                    for c in range(CH):
                        project(r, ("kT", c), wk, c, [cT[:, k, :] for k in range(CH)])
                if own and part == 3:
                    pe.wait_ge(xc_ready.sem, xc_ready.at(r, CH))
                    for c in range(CH):
                        for i in range(2):
                            project(r, ("kT", c, i), wk, c, [xT[:, k, 2 * i:2 * i + 2, :] for k in range(CH)])
                if own and part in (4, 5):
                    for t in range((part - 4) * 2, (part - 4) * 2 + 2):
                        pe.wait_ge(wide.drained(("v", t)), wide.free(r, ("v", t)))
                        for rows, at, n in ((0, 0, GS), (0, GS, GS), (GS, S, NC)):
                            col = D if at == GS else 0
                            for k in range(CH):
                                mm = pe.matmul(wide.bank(("v", t))[rows:rows + n, col:col + D], xT[:, k, t, at:at + n],
                                               wv[:, k, :], start=(k == 0), stop=(k == CH - 1))
                        mm.then_inc(wide.filled(("v", t)), 1)
                if not own and part in (3, 4):
                    i = part - 3
                    pe.wait_ge(wide.drained(("v", i)), wide.free(r, ("v", i)))
                    for t in (2 * i, 2 * i + 1):
                        for k in range(CH):
                            mm = pe.matmul(wide.bank(("v", i))[:, (t % 2) * D:(t % 2 + 1) * D], cT[:, k, t * P:(t + 1) * P],
                                           wv[:, k, :], start=(k == 0), stop=(k == CH - 1))
                    mm.then_inc(wide.filled(("v", i)), 1)

            def attend(r, more):
                if kind == "masked":
                    pe.wait_ge(mask_ready.sem, mask_ready.at(r - 1, 2))
                wait_copied(r - 1, [("qT", c) for c in range(CH)])

                def scores(u):
                    t, g = u // 4, u % 4
                    c, half = g // 2, g % 2
                    bank = wide.bank(u)
                    pe.wait_ge(wide.drained(u), wide.free(r, u))
                    if half == 0:
                        pe.wait_ge(*((kbd_early.sem, kbd_early.at(r - 1, u // 2 + 1)) if u // 2 < KB
                                     else (kbd_late.sem, kbd_late.at(r, u // 2 - KB + 1))))
                    keys = kbd[:, (u // 2) % KB, half * UH:(half + 1) * UH, :]
                    if own:
                        view = bank[:, 0:UH * KL].rearrange("p (h k) -> p h k", h=UH)
                        pe.matmul(bank[:, 0:UH * KL], identb[:, :], causal[:, :, :], start=True, stop=False, skip_group_check=True)
                        pe.matmul(view[0:GS, :, 0:GS], qT[:, c, t * S:t * S + GS], keys[:, :, 0:GS],
                                  start=False, stop=True, skip_group_check=True)
                        mm = pe.matmul(view[GS:S, :, :], qT[:, c, t * S + GS:(t + 1) * S], keys[:, :, GS:KS],
                                       start=False, stop=True, skip_group_check=True)
                    elif kind == "masked":
                        pe.matmul(bank[:, :], onesb[:, :], bc(fill[:, t, :, :], [P, UH, S]), start=True, stop=False)
                        mm = pe.matmul(bank[:, :], qT[:, c, t * S:(t + 1) * S], keys, start=False, stop=True)
                    else:
                        mm = pe.matmul(bank[:, :], qT[:, c, t * S:(t + 1) * S], keys, start=True, stop=True)
                    mm.then_inc(wide.filled(u), 1)

                def turn(u):
                    pe.wait_ge(ex_ready.sem, ex_ready.at(r, u + 1))
                    pe.wait_ge(turned.drained(u), turned.free(r, u))
                    for h in range(UH):
                        mm = pe.transpose(turned.bank(u)[0:VR, h * P:(h + 1) * P], sc[:, u % 4, h, :], ident[:, :])
                    mm.then_inc(turned.filled(u), 1)

                def values(u):
                    t, g = u // 4, u % 4
                    pe.wait_ge(turned.drained(u), turned.full(r, u))
                    if g == 0:
                        pe.wait_ge(out.drained(t), out.free(r, t))
                        wait_copied(r - 1, [("v", t if own else t // 2)])
                    for h in range(UH):
                        col = (g * UH + h) * VW
                        for i in range(VG):
                            q = slice(i * GS, (i + 1) * GS) if own else slice(0, S)
                            mm = pe.matmul(out.bank(t)[q, col:col + VW], pT[:, u % 4, h * P + q.start:h * P + q.stop],
                                           v[:, t, i, g * UH + h, :], start=True, stop=True)
                    if g == 3:
                        mm.then_inc(out.filled(t), 1)

                def output(t):
                    pe.wait_ge(out.drained(t), out.full(r, t))
                    pe.wait_ge(tail.drained(("oT", t)), tail.free(r, ("oT", t)))
                    for c in range(CH):
                        mm = pe.transpose(tail.bank(("oT", t))[:, c * P:(c + 1) * P], o[:, t % 2, c * P:(c + 1) * P], ident[:, :])
                    mm.then_inc(tail.filled(("oT", t)), 1)

                def output_product(t):
                    pe.wait_ge(tail.drained(("oT", t)), tail.full(r, ("oT", t)))
                    pe.wait_ge(tail.drained(("y", t)), tail.free(r, ("y", t)))
                    for k in range(CH):
                        mm = pe.matmul(tail.bank(("y", t))[:, 0:D], oT[:, t % 2, k, :], wo[:, k, :],
                                       start=(k == 0), stop=(k == CH - 1))
                    mm.then_inc(tail.filled(("y", t)), 1)

                for s in range(STEPS):
                    if s < UNITS:
                        scores(s)
                    elif more:
                        prepare(r, s - UNITS)
                    if 0 <= s - 2 < UNITS:
                        turn(s - 2)
                    if 0 <= s - 4 < UNITS:
                        values(s - 4)
                    if s >= 9 and (s - 9) % 4 == 0 and (s - 9) // 4 < G:
                        output((s - 9) // 4)
                    if s >= 11 and (s - 11) % 4 == 0 and (s - 11) // 4 < G:
                        output_product((s - 11) // 4)

            for part in range(STEPS - UNITS):
                prepare(0, part)
            with pe.Fori(1, GROUPS, 1) as r:
                attend(r, True)
            attend(GROUPS, False)

        @block.scalar
        def _(act):
            act.wait_ge(loaded.sem, all_loaded)

            def drain(ring, r, job, write):
                act.wait_ge(ring.filled(job), ring.full(r, job))
                write(ring.bank(job)).then_inc(ring.drained(job), 1)

            def prepare(r, part):
                if part == 0:
                    for c in range(CH):
                        drain(wide, r, ("xT", c), lambda bank: act.copy(
                            xT[:, c, :, 0:S], bank[:, :].rearrange("p (t k) -> p t k", t=G)))
                if own and part == 2:
                    act.wait_ge(cl_ready.sem, cl_ready.at(r, 2))
                    act.activation(expo[:, :, :], expo[:, :, :], ACT.Exp).then_inc(expo_ready.sem, 1)
                if own and part == 3:
                    act.wait_ge(kbd_late.sem, kbd_late.at(r, KB))
                    for c in range(CH):
                        for i in range(2):
                            drain(wide, r, ("kT", c, i), lambda bank: act.activation(
                                kT[:, c, 2 * i:2 * i + 2, :], bank[:, 0:2 * KC].rearrange("p (t k) -> p t k", t=2),
                                ACT.Identity, bias=bk[:, c:c + 1]))
                if not own and part == 1:
                    for c in range(CH):
                        drain(wide, r, ("qT", c), lambda bank: act.activation(
                            qT[:, c, :], bank[:, :], ACT.Identity, bias=bq[:, c:c + 1]) if biased else act.copy(qT[:, c, :], bank[:, :]))
                if kind == "cross" and part in (3, 4):
                    i = part - 3
                    drain(wide, r, ("v", i), lambda bank: act.copy(
                        v[:, 2 * i:2 * i + 2, 0, :, 0:HD], bank[:, :].rearrange("p (t h d) -> p t h d", t=2, h=H)))

            def attend(r, more):
                for s in range(STEPS):
                    if s >= UNITS and more:
                        prepare(r, s - UNITS)
                    if s < UNITS:
                        act.wait_ge(wide.drained(s), wide.full(r, s))
                        act.activation(sc[:, s % 4, :, :], sc[:, s % 4, :, :], ACT.Exp, scale=HD ** -0.5).then_inc(ex_ready.sem, 1)
                    u = s - 2
                    if 0 <= u < UNITS and u % 2 == 0:
                        act.wait_ge(turned.filled(u), turned.full(r, u))
                        act.copy(pT[:, u % 4, :], turned.bank(u)[0:VR, :]).then_inc(turned.drained(u), 1)
                    if s >= 10 and (s - 10) % 4 == 0 and (s - 10) // 4 < G:
                        t = (s - 10) // 4
                        drain(tail, r, ("oT", t), lambda bank: act.copy(
                            oT[:, t % 2, :, :], bank[:, 0:D].rearrange("p (c k) -> p c k", c=CH)))

            for part in range(STEPS - UNITS):
                prepare(0, part)
            with act.Fori(1, GROUPS, 1) as r:
                attend(r, True)
            attend(GROUPS, False)

        @block.vector
        def _(dve):
            dve.wait_ge(loaded.sem, all_loaded)
            dve.wait_ge(const_ready.sem, 1)

            def drain(ring, r, job, write):
                dve.wait_ge(ring.filled(job), ring.full(r, job))
                write(ring.bank(job)).then_inc(ring.drained(job), 1)

            def normalise(r, t):
                dve.tensor_scalar(xn[:, t, :], st.x[:, seq(r + 1, t)], mean[:, seq(r + 1, t, 1)],
                                  rstd[:, seq(r + 1, t, 1)], ALU.subtract, ALU.mult).then_inc(xn_ready.sem, 1)

            def prepare_self(r, part):
                pairs = [P, G * GS // 2, 2]
                logits = wide.bank("logits")[:, 0:G * GS].rearrange("p (n k) -> p n k", k=2)
                e2, w2 = (a[:, :, :].rearrange("p t (n k) -> p (t n) k", k=2) for a in (expo, wts))
                if part == 0:
                    for c in range(CH):
                        dve.wait_ge(wide.drained(("xT", c)), wide.full(r, ("xT", c)))
                        dve.tensor_tensor(prod[:, c, :, :], xT[:, c, :, 0:GS], bc(assign[:, c, :][:, None, :], [P, G, GS]),
                                          ALU.mult).then_inc(prod_ready.sem, 1)
                if part == 1:
                    dve.wait_ge(wide.filled("logits"), wide.full(r, "logits"))
                    dve.tensor_reduce(pair[:, :], logits, AX.X, ALU.max).then_inc(cl_ready.sem, 1)
                    dve.wait_ge(cl_ready.sem, cl_ready.at(r, 1))
                    dve.tensor_tensor(e2, logits, bc(pair[:, :, None], pairs), ALU.subtract).then_inc(cl_ready.sem, 1)
                    for c in range(CH):
                        drain(wide, r, ("qT", c), lambda bank: dve.scalar_tensor_tensor(
                            qT[:, c, :].rearrange("p (t k) -> p t k", t=G), bank[:, :].rearrange("p (t k) -> p t k", t=G),
                            bq[:, c:c + 1], bc(rot_q[:, None, :], [P, G, S]), ALU.add, ALU.mult))
                if part == 2:
                    dve.wait_ge(cl_ready.sem, cl_ready.at(r, 2))
                    dve.wait_ge(expo_ready.sem, expo_ready.at(r, 1))
                    dve.tensor_reduce(pair[:, :], e2, AX.X, ALU.add).then_inc(wide.drained("logits"), 1)
                    dve.wait_ge(wide.drained("logits"), wide.full(r, "logits"))
                    dve.reciprocal(pair[:, :], pair[:, :]).then_inc(cl_ready.sem, 1)
                    dve.wait_ge(cl_ready.sem, cl_ready.at(r, 3))
                    dve.tensor_tensor(w2, e2, bc(pair[:, :, None], pairs), ALU.mult).then_inc(cl_ready.sem, 1)
                    dve.wait_ge(cl_ready.sem, cl_ready.at(r, 4))
                    for c in range(CH):
                        dve.tensor_tensor(prod[:, c, :, :], xT[:, c, :, 0:GS], wts[:, :, :], ALU.mult).then_inc(cl_ready.sem, 1)
                    for c in range(CH):
                        dve.wait_ge(cl_ready.sem, cl_ready.at(r, 5 + c))
                        dve.tensor_reduce(xT[:, c, :, S:KC], prod[:, c, :, :].rearrange("p t (n k) -> p t n k", k=2),
                                          AX.X, ALU.add).then_inc(xc_ready.sem, 1)
                if part in (4, 5):
                    for t in range((part - 4) * 2, (part - 4) * 2 + 2):
                        job = ("v", t)
                        dve.wait_ge(wide.filled(job), wide.full(r, job))
                        local = wide.bank(job)[0:GS, :].rearrange("p (i h d) -> p i h d", i=2, h=H)
                        cluster = wide.bank(job)[GS:KL, 0:D].rearrange("p (h d) -> p h d", h=H)
                        bias = bv[:, :].rearrange("p (h d) -> p h d", h=H)
                        for i in range(2):
                            dve.tensor_tensor(v[0:GS, t, i, :, 0:HD], local[:, i], bias[0:GS], ALU.add).then_inc(v_step.sem, 1)
                        dve.tensor_tensor(v[GS:KL, t, 0, :, 0:HD], cluster, bias[GS:KL], ALU.add).then_inc(v_step.sem, 1)
                        dve.tensor_tensor(v[GS:KL, t, 1, :, 0:HD], cluster, bias[GS:KL], ALU.add).then_inc(wide.drained(job), 1)

            def prepare_context(r, part):
                if part == 0:
                    for c in range(CH):
                        drain(wide, r, ("cT", c), lambda bank: dve.tensor_copy(cT[:, c, :], bank[:, :]))
                if kind == "masked" and part == 1:
                    dve.wait_ge(ctx_loaded.sem, ctx_loaded.at(r + 1, 0))
                    dve.tensor_copy(mask[:, :], mrow[:, :]).then_inc(mask_ready.sem, 1)
                    dve.wait_ge(mask_ready.sem, mask_ready.at(r, 1))
                    dve.tensor_scalar(fill[:, :, 0, :], mask[:, :].rearrange("p (t k) -> p t k", t=G), -1.0, parts[:, 0:1],
                                      ALU.add, ALU.mult).then_inc(mask_ready.sem, 1)
                if part == 2:
                    dve.wait_ge(kbd_late.sem, kbd_late.at(r, KB))
                    for c in range(CH):
                        out_k = kT[:, c, :, :].rearrange("p t k -> p (t k)")
                        drain(wide, r, ("kT", c), lambda bank: dve.scalar_tensor_tensor(
                            out_k, bank[:, :], bk[:, c:c + 1], mask[:, :], ALU.add, ALU.mult) if kind == "masked"
                            else dve.tensor_copy(out_k, bank[:, :]))
                if biased and part in (3, 4):
                    i = part - 3
                    drain(wide, r, ("v", i), lambda bank: dve.tensor_tensor(
                        v[:, 2 * i:2 * i + 2, 0, :, 0:HD], bank[:, :].rearrange("p (t h d) -> p t h d", t=2, h=H),
                        bc(bv[:, :].rearrange("p (a h d) -> p a h d", a=1, h=H), [P, 2, H, HD]), ALU.add))

            prepare = prepare_self if own else prepare_context

            def attend(r, more):
                for s in range(STEPS):
                    if s >= UNITS and more:
                        prepare(r, s - UNITS)
                    if 8 <= s < 8 + G and more:
                        normalise(r, s - 8)
                    if s < UNITS:
                        dve.wait_ge(wide.filled(s), wide.full(r, s))
                        unit = wide.bank(s)[:, 0:UH * KU].rearrange("p (h k) -> p h k", h=UH)
                        dve.tensor_reduce(mx[:, s % 4, :], unit, AX.X, ALU.max).then_inc(mx_ready.sem, 1)
                        dve.wait_ge(mx_ready.sem, mx_ready.at(r, s + 1))
                        dve.tensor_tensor(sc[:, s % 4, :, :], unit, bc(mx[:, s % 4, :, None], [P, UH, KU]),
                                          ALU.subtract).then_inc(wide.drained(s), 1)
                    u = s - 2
                    if 0 <= u < UNITS and u % 2 == 1:
                        dve.wait_ge(turned.filled(u), turned.full(r, u))
                        dve.tensor_copy(pT[:, u % 4, :], turned.bank(u)[0:VR, :]).then_inc(turned.drained(u), 1)
                    if s >= 8 and (s - 8) % 4 == 0 and (s - 8) // 4 < G:
                        t = (s - 8) // 4
                        dve.wait_ge(out.filled(t), out.full(r, t))
                        heads = out.bank(t)[:, 0:H * VW].rearrange("p (h d) -> p h d", h=H)
                        dve.reciprocal(rs[:, t % 2, :], heads[:, :, HD]).then_inc(rs_ready.sem, 1)
                        dve.wait_ge(rs_ready.sem, rs_ready.at(r, t + 1))
                        dve.tensor_tensor(o[:, t % 2, :].rearrange("p (h d) -> p h d", h=H), heads[:, :, 0:HD],
                                          bc(rs[:, t % 2, :, None], [P, H, HD]), ALU.mult).then_inc(out.drained(t), 1)
                    if s >= 12 and (s - 12) % 4 == 0 and (s - 12) // 4 < G:
                        t = (s - 12) // 4
                        if biased:
                            dve.wait_ge(xb_ready.sem, xb_ready.at(r - 1, t + 1))
                        rows.wait_slot(dve, r, t)
                        drain(tail, r, ("y", t), lambda bank: dve.tensor_tensor(
                            rows.slot[:, t % 2, :], st.x[:, seq(r, t)], bank[:, 0:D], ALU.add))
                        rows.take_stats(dve, r, t, tail.drained(("y", t)), tail.full(r, ("y", t)))

            for t in range(G):
                normalise(0, t)
            for part in range(STEPS - UNITS):
                prepare(0, part)
            with dve.Fori(1, GROUPS, 1) as r:
                attend(r, True)
            attend(GROUPS, False)
    st.turn()


def bitlinear_phase(nc, st, io, weights, following):
    mean, rstd = st.mean[st.now], st.rstd[st.now]
    HI = INNER // 2
    STEPS = G + 4
    halves = [(t, i) for t in range(G) for i in range(2)]
    with ExitStack() as ctx:
        def sb(n, s, dt=F32):
            return ctx.enter_context(nc.sbuf_tensor(f"bit_{n}", s, dt))

        def tally(n, per, start=None):
            return Tally(nc, f"bit_{n}", per, start)

        shapes = {"gate": [P, CH, INNER], "up": [P, CH, INNER], "down": [P, IC, D]}
        names = list(shapes)
        rawf, identb, loaded = weights.raw, weights.identb, weights.loaded
        quant = {n: sb(f"w_{n}", shapes[n], BF16) for n in names}
        ones = sb("ones", [P, P])
        sums, wmean, wscale = sb("sums", [P, 3]), sb("wmean", [P, 3]), sb("wscale", [P, 3])
        xn = sb("xn", [P, G, D])
        amax, alim, arec, ascale = (sb(n, [P, G]) for n in ("amax", "alim", "arec", "ascale"))
        dgate, dup, ddown = (sb(n, [P, G]) for n in ("dgate", "dup", "ddown"))
        xq = sb("xq", [P, G, D], BF16)
        xqT = sb("xqT", [P, CH, G * S], BF16)
        sg = sb("sg", [P, 2, HI])
        h = sb("h", [P, 2, INNER])
        hmax, hlim, hrec, hscale = (sb(n, [P, G]) for n in ("hmax", "hlim", "hrec", "hscale"))
        hq = sb("hq", [P, 2, INNER], BF16)
        hqT = sb("hqT", [P, 2, IC, P], BF16)
        round_col = sb("round", [P, 1])

        ones_ready = tally("ones_ready", 0)
        sums_ready = tally("sums_ready", 0)
        total_ready = tally("total_ready", 0)
        wstep = tally("weight_step", 0)
        ascale_ready = tally("ascale_ready", 1, 0)
        ddown_ready = tally("ddown_ready", G)
        xstep = tally("x_step", G + 5, 0)
        xr_ready = tally("x_rounded", G, 0)
        xq_ready = tally("xq_ready", 1, 0)
        sg_ready = tally("silu_ready", 2 * G)
        hstep = tally("h_step", 4 * G)
        hr_ready = tally("h_rounded", G)
        hq_ready = tally("hq_ready", G - 1)
        hq_last = tally("hq_last", 1)
        rows = Rows(ctx, nc, "bit", st.x, st.mean[st.now ^ 1], st.rstd[st.now ^ 1], EPS)
        turned = Ring(ctx, nc, "bit_turned", 2, [("hT", t) for t in range(G)] + ["xT"], skipped=G)
        gates = Ring(ctx, nc, "bit_gates", 2, halves)
        ups = Ring(ctx, nc, "bit_ups", 2, halves)
        outs = Ring(ctx, nc, "bit_outs", 2, list(range(G)))
        block = ctx.enter_context(nc.Block())

        @block.sync
        def _(sp):
            following.fetch(sp, io)

        @block.gpsimd
        def _(pool):
            rows.pool_start(pool)
            pool.memset(ones[:, :], 1.0).then_inc(ones_ready.sem, 1)
            pool.wait_ge(wstep.sem, 1)
            with pool.Fori(1, GROUPS + 1, 1) as r:
                for s in range(1, STEPS):
                    if s - 1 < G - 1:
                        t = s - 1
                        pool.wait_ge(hr_ready.sem, hr_ready.at(r, t + 1))
                        before = (r, ("hT", t - 2)) if t >= 2 else (r - 1, ("hT", t + 2))
                        pool.wait_ge(turned.filled(before[1]), turned.full(*before))
                        pool.tensor_tensor(hq[:, t % 2, :], h[:, t % 2, :], bc(round_col[:, :], [P, INNER]),
                                           ALU.subtract).then_inc(hq_ready.sem, 1)
                    if 0 <= s - 4 < G:
                        rows.store(pool, r, s - 4)
                rows.store_stats(pool, r)

        @block.tensor
        def _(pe):
            pe.wait_ge(loaded.sem, 64)
            pe.wait_ge(ones_ready.sem, 1)
            pe.wait_ge(sums_ready.sem, 3)
            pe.matmul(outs.banks[1][:, 0:3], ones[:, :], sums[:, :], start=True, stop=True).then_inc(total_ready.sem, 1)
            pe.wait_ge(wstep.sem, 12)

            def prepare(r):
                pe.wait_ge(turned.drained("xT"), turned.free(r, "xT"))
                pe.wait_ge(xq_ready.sem, xq_ready.at(r, 1))
                xT = turned.bank("xT")[:, :].bitcast(BF16)
                for t in range(G):
                    for c in range(CH):
                        col = c * G * S + t * S
                        mm = pe.transpose(xT[:, col:col + S], xq[:, t, c * P:(c + 1) * P], identb[:, :])
                mm.then_inc(turned.filled("xT"), 1)

            def layer(r, more):
                pe.wait_ge(turned.drained("xT"), turned.full(r - 1, "xT"))

                def widen(t):
                    for i in range(2):
                        for ring, n in ((gates, "gate"), (ups, "up")):
                            pe.wait_ge(ring.drained((t, i)), ring.free(r, (t, i)))
                            for k in range(CH):
                                mm = pe.matmul(ring.bank((t, i))[:, :], xqT[:, k, t * S:(t + 1) * S],
                                               quant[n][:, k, i * HI:(i + 1) * HI], start=(k == 0), stop=(k == CH - 1))
                            mm.then_inc(ring.filled((t, i)), 1)

                def turn(t):
                    pe.wait_ge(turned.drained(("hT", t)), turned.free(r, ("hT", t)))
                    pe.wait_ge(*((hq_ready.sem, hq_ready.at(r, t + 1)) if t < G - 1 else (hq_last.sem, hq_last.at(r, 1))))
                    hT = turned.bank(("hT", t))[:, :].bitcast(BF16)
                    for k in range(IC):
                        mm = pe.transpose(hT[:, k * P:(k + 1) * P], hq[:, t % 2, k * P:(k + 1) * P], identb[:, :])
                    mm.then_inc(turned.filled(("hT", t)), 1)

                def narrow(t):
                    pe.wait_ge(turned.drained(("hT", t)), turned.full(r, ("hT", t)))
                    pe.wait_ge(outs.drained(t), outs.free(r, t))
                    for k in range(IC):
                        mm = pe.matmul(outs.bank(t)[:, 0:D], hqT[:, t % 2, k, :], quant["down"][:, k, :],
                                       start=(k == 0), stop=(k == IC - 1))
                    mm.then_inc(outs.filled(t), 1)

                for s in range(G + 3):
                    if s < G:
                        widen(s)
                    if s - 2 == G - 1 and more:
                        prepare(r)
                    if 0 <= s - 2 < G:
                        turn(s - 2)
                    if 0 <= s - 3 < G:
                        narrow(s - 3)

            prepare(0)
            with pe.Fori(1, GROUPS, 1) as r:
                layer(r, True)
            layer(GROUPS, False)

        @block.scalar
        def _(act):
            def prepare(r):
                act.wait_ge(ascale_ready.sem, ascale_ready.at(r, 1))
                for t in range(G):
                    act.activation(xn[:, t, :], xn[:, t, :], ACT.Identity, bias=round_col[:, 0:1],
                                   scale=ascale[:, t:t + 1]).then_inc(xr_ready.sem, 1)

            def layer(r, more):
                for s in range(G + 1):
                    if s < G:
                        for i in range(2):
                            act.wait_ge(xstep.sem, xstep.at(r - 1, G + 5))
                            act.wait_ge(gates.filled((s, i)), gates.full(r, (s, i)))
                            if (s, i) >= (1, 0):
                                j = 2 * s + i - 2
                                act.wait_ge(ups.drained(halves[j]), ups.full(r, halves[j]))
                            act.activation(sg[:, i, :], gates.bank((s, i))[:, :], ACT.Silu,
                                           scale=dgate[:, s:s + 1]).then_inc(gates.drained((s, i)), 1)
                    if s >= 1:
                        t = s - 1
                        act.wait_ge(hstep.sem, hstep.at(r, 4 * t + 4))
                        act.activation(h[:, t % 2, :], h[:, t % 2, :], ACT.Identity, bias=round_col[:, 0:1],
                                       scale=hscale[:, t:t + 1]).then_inc(hr_ready.sem, 1)
                    if s == 3 and more:
                        prepare(r)

            prepare(0)
            with act.Fori(1, GROUPS, 1) as r:
                layer(r, True)
            layer(GROUPS, False)

        @block.vector
        def _(dve):
            dve.memset(round_col[:, :], ROUND).then_inc(wstep.sem, 1)
            dve.wait_ge(loaded.sem, 64)
            for i, n in enumerate(names):
                dve.tensor_reduce(sums[:, i:i + 1], rawf[n][:, :], AX.X, ALU.add, apply_absolute_value=True).then_inc(sums_ready.sem, 1)
            dve.wait_ge(total_ready.sem, 1)
            dve.tensor_scalar(wmean[:, :], outs.banks[1][:, 0:3], 1.0 / (D * INNER), 1e-5, ALU.mult, ALU.max).then_inc(wstep.sem, 1)
            dve.wait_ge(wstep.sem, 2)
            dve.reciprocal(wscale[:, :], wmean[:, :]).then_inc(wstep.sem, 1)
            dve.wait_ge(wstep.sem, 3)
            for i, n in enumerate(names):
                dve.tensor_scalar(rawf[n][:, :], rawf[n][:, :], wscale[:, i:i + 1], ROUND, ALU.mult, ALU.add).then_inc(wstep.sem, 1)
            for i, n in enumerate(names):
                dve.wait_ge(wstep.sem, 4 + i)
                dve.tensor_scalar(rawf[n][:, :], rawf[n][:, :], ROUND, 1.0, ALU.subtract, ALU.min).then_inc(wstep.sem, 1)
            for i, n in enumerate(names):
                dve.wait_ge(wstep.sem, 7 + i)
                last = dve.tensor_scalar(quant[n][:, :, :].rearrange("p c o -> p (c o)"), rawf[n][:, :], -1.0, None, ALU.max)
                last.then_inc(wstep.sem, 1)

            def normalise(r):
                wait_count(dve, xq_ready.sem, xq_ready.at(r, 0))
                for t in range(G):
                    dve.tensor_scalar(xn[:, t, :], st.x[:, seq(r + 1, t)], mean[:, seq(r + 1, t, 1)],
                                      rstd[:, seq(r + 1, t, 1)], ALU.subtract, ALU.mult).then_inc(xstep.sem, 1)

            def limit(r):
                dve.wait_ge(xstep.sem, xstep.at(r, G))
                dve.tensor_reduce(amax[:, :], xn[:, :, :], AX.X, ALU.max, apply_absolute_value=True).then_inc(xstep.sem, 1)
                dve.wait_ge(xstep.sem, xstep.at(r, G + 1))
                dve.tensor_scalar(alim[:, :], amax[:, :], 1e-5, None, ALU.max).then_inc(xstep.sem, 1)
                dve.wait_ge(xstep.sem, xstep.at(r, G + 2))
                dve.reciprocal(arec[:, :], alim[:, :]).then_inc(xstep.sem, 1)
                dve.wait_ge(xstep.sem, xstep.at(r, G + 3))
                dve.tensor_scalar(ascale[:, :], arec[:, :], 127.0, None, ALU.mult).then_inc(ascale_ready.sem, 1)

            def scales(r):
                dve.wait_ge(gates.drained(halves[-1]), gates.full(r, halves[-1]))
                dve.tensor_scalar(dgate[:, :], alim[:, :], wmean[:, 0:1], 1.0 / 127, ALU.mult, ALU.mult).then_inc(xstep.sem, 1)
                dve.tensor_scalar(dup[:, :], alim[:, :], wmean[:, 1:2], 1.0 / 127, ALU.mult, ALU.mult).then_inc(xstep.sem, 1)

            def whole_rows(r):
                dve.wait_ge(xr_ready.sem, xr_ready.at(r, G))
                if not isinstance(r, int):
                    dve.wait_ge(turned.filled("xT"), turned.full(r - 1, "xT"))
                dve.tensor_scalar(xq[:, :, :], xn[:, :, :], ROUND, None, ALU.subtract).then_inc(xq_ready.sem, 1)

            def clip_rows(r):
                dve.wait_ge(turned.filled("xT"), turned.full(r, "xT"))
                dve.tensor_scalar(xqT[:, :, :].rearrange("p c k -> p (c k)"), turned.bank("xT")[:, :].bitcast(BF16),
                                  127.0, -128.0, ALU.min, ALU.max).then_inc(turned.drained("xT"), 1)

            def layer(r, more):
                for s in range(STEPS):
                    if s < G:
                        dve.wait_ge(hq_ready.sem, hq_ready.at(r, s - 1 if s >= 2 else 0))
                        if s == 1:
                            dve.wait_ge(hq_last.sem, hq_last.at(r, 0))
                        for i in range(2):
                            dve.wait_ge(ups.filled((s, i)), ups.full(r, (s, i)))
                            dve.wait_ge(gates.drained((s, i)), gates.full(r, (s, i)))
                            dve.scalar_tensor_tensor(h[:, s % 2, i * HI:(i + 1) * HI], ups.bank((s, i))[:, :], dup[:, s:s + 1],
                                                     sg[:, i, :], ALU.mult, ALU.mult).then_inc(ups.drained((s, i)), 1)
                    if s < G:
                        dve.wait_ge(ups.drained((s, 0)), ups.full(r, (s, 0)))
                        dve.wait_ge(ups.drained((s, 1)), ups.full(r, (s, 1)))
                        one = slice(s, s + 1)
                        dve.tensor_reduce(hmax[:, one], h[:, s % 2, :], AX.X, ALU.max, apply_absolute_value=True).then_inc(hstep.sem, 1)
                        dve.wait_ge(hstep.sem, hstep.at(r, 4 * s + 1))
                        dve.tensor_scalar(hlim[:, one], hmax[:, one], 1e-5, None, ALU.max).then_inc(hstep.sem, 1)
                        dve.wait_ge(hstep.sem, hstep.at(r, 4 * s + 2))
                        dve.reciprocal(hrec[:, one], hlim[:, one]).then_inc(hstep.sem, 1)
                        dve.tensor_scalar(ddown[:, one], hlim[:, one], wmean[:, 2:3], 1.0 / 127, ALU.mult, ALU.mult).then_inc(ddown_ready.sem, 1)
                        dve.wait_ge(hstep.sem, hstep.at(r, 4 * s + 3))
                        dve.tensor_scalar(hscale[:, one], hrec[:, one], 127.0, None, ALU.mult).then_inc(hstep.sem, 1)
                    if s == 4:
                        if more:
                            whole_rows(r)
                            scales(r)
                        t = G - 1
                        dve.wait_ge(hr_ready.sem, hr_ready.at(r, t + 1))
                        dve.wait_ge(turned.filled(("hT", t - 2)), turned.full(r, ("hT", t - 2)))
                        dve.tensor_scalar(hq[:, t % 2, :], h[:, t % 2, :], ROUND, None, ALU.subtract).then_inc(hq_last.sem, 1)
                    if s == 5 and more:
                        clip_rows(r)
                    if 0 <= s - 2 < G:
                        t = s - 2
                        dve.wait_ge(turned.filled(("hT", t)), turned.full(r, ("hT", t)))
                        dve.tensor_scalar(hqT[:, t % 2, :, :].rearrange("p c k -> p (c k)"), turned.bank(("hT", t))[:, :].bitcast(BF16),
                                          127.0, -128.0, ALU.min, ALU.max).then_inc(turned.drained(("hT", t)), 1)
                    if more and s == 1:
                        normalise(r)
                    if more and s == 2:
                        limit(r)
                    if 0 <= s - 3 < G:
                        t = s - 3
                        rows.wait_slot(dve, r, t)
                        dve.wait_ge(ddown_ready.sem, ddown_ready.at(r, t + 1))
                        dve.wait_ge(outs.filled(t), outs.full(r, t))
                        dve.scalar_tensor_tensor(rows.slot[:, t % 2, :], outs.bank(t)[:, 0:D], ddown[:, t:t + 1],
                                                 st.x[:, seq(r, t)], ALU.mult, ALU.add).then_inc(outs.drained(t), 1)
                        rows.take_stats(dve, r, t, outs.drained(t), outs.full(r, t))

            normalise(0)
            limit(0)
            scales(0)
            whole_rows(0)
            clip_rows(0)
            with dve.Fori(1, GROUPS, 1) as r:
                layer(r, True)
            layer(GROUPS, False)
    st.turn()


def second_layer_self(nc, st, io, ident, weights, mlp_weights, following):
    with ExitStack() as ctx:
        y = ctx.enter_context(nc.sbuf_tensor("inner_stream", [P, B * D], F32))
        performer_phase(nc, st, io, ident, y, weights, mlp_weights)
        mlp_phase(nc, st, io, ident, y, mlp_weights, following)


def performer_phase(nc, st, io, ident, y, weights, following):
    mean, rstd = st.mean[st.now], st.rstd[st.now]
    prepared = ([("xT", c) for c in range(CH)] + [("qT", c) for c in range(CH)] + [("kT", c) for c in range(CH)]
                + [("v", 0), "squares", ("v", 1)])
    STEPS = UNITS + 9
    FS = 8
    PAIRS = H // 2
    PW = 2 * VW
    mids = [(what, t) for t in range(G) for what in ("kv", "q0", "q1")]
    with ExitStack() as ctx:
        def sb(n, s, dt=F32):
            return ctx.enter_context(nc.sbuf_tensor(f"perf_{n}", s, dt))

        def tally(n, per, start=None):
            return Tally(nc, f"perf_{n}", per, start)

        wq, wk, wv, wo, loaded = weights.wq, weights.wk, weights.wv, weights.wo, weights.loaded
        omega, half_heads = weights.omega, weights.half_heads
        floor = sb("floor", [P, 1])
        xn = sb("xn", [P, G, D])
        kept = sb("kept", [P, G, D])
        xT = sb("xT", [P, CH, G * S])
        qk = sb("qk", [P, 2, CH, G * S])
        qk2 = sb("qk2", [P, 2, CH, G * S])
        half2 = sb("half2", [P, G, 2, H])
        v = sb("v", [P, G, H, VW])
        f = sb("f", [P, FS, HH, NF])
        mx, off = sb("mx", [P, FS, HH]), sb("off", [P, FS, HH])
        fT = sb("fT", [P, 2, 4 * P])
        kv = sb("kv", [P, 2, PAIRS, PW])
        rs = sb("rs", [P, 2, H])
        o = sb("o", [P, 2, D])
        oT = sb("oT", [P, 2, CH, P])

        const_ready = tally("const_ready", 0)
        xn_ready = tally("xn_ready", G, 0)
        square_ready = tally("squares_ready", 2 * CH, 0)
        kept_ready = tally("kept_ready", 1)
        mx_ready = tally("max_ready", UNITS)
        off_ready = tally("offset_ready", UNITS)
        ex_ready = tally("exp_ready", UNITS)
        f_ready = tally("features_ready", UNITS)
        kv_half = tally("kv_half", G)
        rs_ready = tally("recip_ready", G)
        rows = Rows(ctx, nc, "perf", y, st.mean_in, st.rstd_in, EPS_IN)
        wide = Ring(ctx, nc, "perf_wide", 3, list(range(UNITS)) + prepared, skipped=UNITS)
        tail = Ring(ctx, nc, "perf_tail", 1, [(what, t) for t in range(G) for what in ("oT", "y")])
        mid = Ring(ctx, nc, "perf_mid", 2, mids)
        out = Ring(ctx, nc, "perf_out", 2, list(range(G)))
        block = ctx.enter_context(nc.Block())

        @block.sync
        def _(sp):
            following.fetch(sp, io)

        @block.gpsimd
        def _(pool):
            rows.pool_start(pool)
            pool.memset(v[:, :, :, HD:VW], 1.0).then_inc(const_ready.sem, 1)
            pool.memset(kv[:, :, :, :], 0.0).then_inc(const_ready.sem, 1)
            pool.memset(floor[:, :], 1e-6 * NF ** 0.5).then_inc(const_ready.sem, 1)
            pool.wait_ge(const_ready.sem, 3)
            with pool.Fori(1, GROUPS + 1, 1) as r:
                for s in range(STEPS):
                    if s < UNITS:
                        pool.wait_ge(ex_ready.sem, ex_ready.at(r, s + 1))
                        flat = f[:, s % FS, :, :].rearrange("p h m -> p (h m)")
                        pool.tensor_tensor(flat, flat, bc(floor[:, :], [P, HH * NF]), ALU.add).then_inc(f_ready.sem, 1)
                    if s >= 12 and (s - 12) % 4 == 0 and (s - 12) // 4 < G:
                        t = (s - 12) // 4
                        rows.store(pool, r, t)
                rows.store_stats(pool, r)

        @block.tensor
        def _(pe):
            pe.wait_ge(loaded.sem, 96)
            pe.wait_ge(const_ready.sem, 3)

            def projected(r, job, w, c):
                pe.wait_ge(wide.drained(job), wide.free(r, job))
                for k in range(CH):
                    mm = pe.matmul(wide.bank(job)[:, :], w[:, k, c * P:(c + 1) * P], xT[:, k, :],
                                   start=(k == 0), stop=(k == CH - 1))
                mm.then_inc(wide.filled(job), 1)

            def prepare(r, part):
                if part == 0:
                    for c in range(CH):
                        pe.wait_ge(wide.drained(("xT", c)), wide.free(r, ("xT", c)))
                        for t in range(G):
                            pe.wait_ge(xn_ready.sem, xn_ready.at(r, t + 1))
                            mm = pe.transpose(wide.bank(("xT", c))[:, t * P:(t + 1) * P], xn[:, t, c * P:(c + 1) * P], ident[:, :])
                        mm.then_inc(wide.filled(("xT", c)), 1)
                if part == 1:
                    for c in range(CH):
                        pe.wait_ge(wide.drained(("xT", c)), wide.full(r, ("xT", c)))
                    for c in range(CH):
                        projected(r, ("qT", c), wq, c)
                if part == 2:
                    for c in range(CH):
                        projected(r, ("kT", c), wk, c)
                if part in (3, 5):
                    i = (part - 3) // 2
                    pe.wait_ge(wide.drained(("v", i)), wide.free(r, ("v", i)))
                    for t in (2 * i, 2 * i + 1):
                        for k in range(CH):
                            mm = pe.matmul(wide.bank(("v", i))[:, (t % 2) * D:(t % 2 + 1) * D], xT[:, k, t * P:(t + 1) * P],
                                           wv[:, k, :], start=(k == 0), stop=(k == CH - 1))
                    mm.then_inc(wide.filled(("v", i)), 1)
                if part == 4:
                    pe.wait_ge(square_ready.sem, square_ready.at(r, 2 * CH))
                    pe.wait_ge(wide.drained("squares"), wide.free(r, "squares"))
                    for t in range(G):
                        for w in range(2):
                            for c in range(CH):
                                col = (t * 2 + w) * H + c * HH
                                mm = pe.matmul(wide.bank("squares")[:, col:col + HH], qk2[:, w, c, t * S:(t + 1) * S], half_heads[:, :],
                                               start=True, stop=True)
                    mm.then_inc(wide.filled("squares"), 1)

            def attend(r, more):
                for what in ("qT", "kT"):
                    for c in range(CH):
                        pe.wait_ge(wide.drained((what, c)), wide.full(r - 1, (what, c)))

                def features(u):
                    t, w, c = u // 4, 1 - (u % 4) // 2, u % 2
                    pe.wait_ge(wide.drained(u), wide.free(r, u))
                    pe.matmul(wide.bank(u)[:, :], qk[:, w, c, t * S:(t + 1) * S], omega[:, :],
                              start=True, stop=True).then_inc(wide.filled(u), 1)

                def use(u):
                    t, c = u // 4, u % 2
                    pe.wait_ge(f_ready.sem, f_ready.at(r, u + 1))
                    keys = u % 4 < 2
                    job = ("kv" if keys else f"q{c}", t)
                    if c == 0 or not keys:
                        pe.wait_ge(mid.drained(job), mid.free(r, job))
                    if keys and c == 0:
                        pe.wait_ge(wide.drained(("v", t // 2)), wide.full(r - 1, ("v", t // 2)))
                    for j in range(4):
                        pair = c * 4 + j
                        two = f[:, u % FS, 2 * j:2 * j + 2, :].rearrange("p h m -> p (h m)")
                        if keys:
                            mm = pe.matmul(mid.bank(job)[:, pair * PW:(pair + 1) * PW], two, v[:, t, 2 * pair:2 * pair + 2, :],
                                           start=True, stop=True)
                        else:
                            mm = pe.transpose(mid.bank(job)[:, j * P:(j + 1) * P], two, ident[:, :])
                    if c == 1 or not keys:
                        mm.then_inc(mid.filled(job), 1)

                def combine(u):
                    t, c = u // 4, u % 2
                    job = (f"q{c}", t)
                    pe.wait_ge(mid.drained(job), mid.full(r, job))
                    if c == 0:
                        pe.wait_ge(mid.drained(("kv", t)), mid.full(r, ("kv", t)))
                        pe.wait_ge(out.drained(t), out.free(r, t))
                    for j in range(4):
                        pair = c * 4 + j
                        mm = pe.matmul(out.bank(t)[:, pair * PW:(pair + 1) * PW], fT[:, c, j * P:(j + 1) * P], kv[:, t % 2, pair, :],
                                       start=True, stop=True)
                    if c == 1:
                        mm.then_inc(out.filled(t), 1)

                def output(t):
                    pe.wait_ge(out.drained(t), out.full(r, t))
                    pe.wait_ge(tail.drained(("oT", t)), tail.free(r, ("oT", t)))
                    for c in range(CH):
                        mm = pe.transpose(tail.bank(("oT", t))[:, c * P:(c + 1) * P], o[:, t % 2, c * P:(c + 1) * P], ident[:, :])
                    mm.then_inc(tail.filled(("oT", t)), 1)

                def output_product(t):
                    pe.wait_ge(tail.drained(("oT", t)), tail.full(r, ("oT", t)))
                    pe.wait_ge(tail.drained(("y", t)), tail.free(r, ("y", t)))
                    for k in range(CH):
                        mm = pe.matmul(tail.bank(("y", t))[:, 0:D], oT[:, t % 2, k, :], wo[:, k, :],
                                       start=(k == 0), stop=(k == CH - 1))
                    mm.then_inc(tail.filled(("y", t)), 1)

                for s in range(STEPS):
                    if s < UNITS:
                        features(s)
                    elif more:
                        prepare(r, s - UNITS)
                    if 0 <= s - 3 < UNITS:
                        use(s - 3)
                    if 0 <= s - 4 < UNITS and (s - 4) % 4 >= 2:
                        combine(s - 4)
                    if s >= 9 and (s - 9) % 4 == 0 and (s - 9) // 4 < G:
                        output((s - 9) // 4)
                    if s >= 11 and (s - 11) % 4 == 0 and (s - 11) // 4 < G:
                        output_product((s - 11) // 4)

            for part in range(STEPS - UNITS):
                prepare(0, part)
            with pe.Fori(1, GROUPS, 1) as r:
                attend(r, True)
            attend(GROUPS, False)

        @block.scalar
        def _(act):
            act.wait_ge(loaded.sem, 96)

            def drain(ring, r, job, write):
                act.wait_ge(ring.filled(job), ring.full(r, job))
                write(ring.bank(job)).then_inc(ring.drained(job), 1)

            def prepare(r, part):
                if part == 0:
                    for c in range(CH):
                        drain(wide, r, ("xT", c), lambda bank: act.copy(xT[:, c, :], bank[:, :]))
                if part == 1:
                    for c in range(CH):
                        drain(wide, r, ("qT", c), lambda bank: act.mul(qk[:, 0, c, :], bank[:, :], HD ** -0.25))
                if part == 2:
                    for c in range(CH):
                        act.wait_ge(wide.drained(("qT", c)), wide.full(r, ("qT", c)))
                        act.activation(qk2[:, 0, c, :], qk[:, 0, c, :], ACT.Square).then_inc(square_ready.sem, 1)
                if part in (3, 5):
                    i = (part - 3) // 2
                    drain(wide, r, ("v", i), lambda bank: act.copy(
                        v[:, 2 * i:2 * i + 2, :, 0:HD], bank[:, :].rearrange("p (t h d) -> p t h d", t=2, h=H)))

            def attend(r, more):
                act.wait_ge(xn_ready.sem, xn_ready.at(r - 1, G))
                act.wait_ge(tail.drained(("y", G - 1)), tail.free(r, ("oT", 0)))
                act.copy(kept[:, :, :], xn[:, :, :]).then_inc(kept_ready.sem, 1)
                for s in range(STEPS):
                    if s >= UNITS and more:
                        prepare(r, s - UNITS)
                    if s < UNITS:
                        act.wait_ge(wide.drained(s), wide.full(r, s))
                        act.activation(f[:, s % FS, :, :], f[:, s % FS, :, :], ACT.Exp).then_inc(ex_ready.sem, 1)
                    u = s - 3
                    if 0 <= u < UNITS and u % 4 >= 2:
                        job = (f"q{u % 2}", u // 4)
                        act.wait_ge(mid.filled(job), mid.full(r, job))
                        act.copy(fT[:, u % 2, :], mid.bank(job)[:, :]).then_inc(mid.drained(job), 1)
                    if s >= 10 and (s - 10) % 4 == 0 and (s - 10) // 4 < G:
                        t = (s - 10) // 4
                        drain(tail, r, ("oT", t), lambda bank: act.copy(
                            oT[:, t % 2, :, :], bank[:, 0:D].rearrange("p (c k) -> p c k", c=CH)))

            for part in range(STEPS - UNITS):
                prepare(0, part)
            with act.Fori(1, GROUPS, 1) as r:
                attend(r, True)
            attend(GROUPS, False)

        @block.vector
        def _(dve):
            dve.wait_ge(loaded.sem, 96)
            dve.wait_ge(const_ready.sem, 3)

            def drain(ring, r, job, write):
                dve.wait_ge(ring.filled(job), ring.full(r, job))
                write(ring.bank(job)).then_inc(ring.drained(job), 1)

            def normalise(r, t):
                dve.tensor_scalar(xn[:, t, :], st.x[:, seq(r + 1, t)], mean[:, seq(r + 1, t, 1)],
                                  rstd[:, seq(r + 1, t, 1)], ALU.subtract, ALU.mult).then_inc(xn_ready.sem, 1)

            def prepare(r, part):
                if part == 2:
                    for c in range(CH):
                        drain(wide, r, ("kT", c), lambda bank: dve.tensor_scalar(qk[:, 1, c, :], bank[:, :], HD ** -0.25, None, ALU.mult))
                if part == 3:
                    for c in range(CH):
                        dve.wait_ge(wide.drained(("kT", c)), wide.full(r, ("kT", c)))
                        dve.tensor_tensor(qk2[:, 1, c, :], qk[:, 1, c, :], qk[:, 1, c, :], ALU.mult).then_inc(square_ready.sem, 1)
                if part == 4:
                    drain(wide, r, "squares", lambda bank: dve.tensor_copy(
                        half2[:, :, :, :].rearrange("p t w h -> p (t w h)"), bank[:, 0:G * 2 * H]))

            def attend(r, more):
                dve.wait_ge(wide.drained("squares"), wide.full(r - 1, "squares"))
                for s in range(STEPS):
                    if s >= UNITS and more:
                        prepare(r, s - UNITS)
                    if 8 <= s < 8 + G and more:
                        if s == 8:
                            dve.wait_ge(kept_ready.sem, kept_ready.at(r, 1))
                        normalise(r, s - 8)
                    if s < UNITS:
                        t, w, c = s // 4, 1 - (s % 4) // 2, s % 2
                        dve.wait_ge(wide.filled(s), wide.full(r, s))
                        unit = wide.bank(s)[:, :].rearrange("p (h m) -> p h m", h=HH)
                        dve.tensor_reduce(mx[:, s % FS, :], unit, AX.X, ALU.max).then_inc(mx_ready.sem, 1)
                        dve.wait_ge(mx_ready.sem, mx_ready.at(r, s + 1))
                        dve.tensor_tensor(off[:, s % FS, :], mx[:, s % FS, :], half2[:, t, w, c * HH:(c + 1) * HH], ALU.add).then_inc(off_ready.sem, 1)
                        dve.wait_ge(off_ready.sem, off_ready.at(r, s + 1))
                        dve.tensor_tensor(f[:, s % FS, :, :], unit, bc(off[:, s % FS, :, None], [P, HH, NF]),
                                          ALU.subtract).then_inc(wide.drained(s), 1)
                    u = s - 3
                    if 0 <= u < UNITS and u % 4 == 1:
                        t = u // 4
                        job = ("kv", t)
                        dve.wait_ge(mid.filled(job), mid.full(r, job))
                        both = mid.bank(job)[:, 0:PAIRS * PW].rearrange("p (a k) -> p a k", a=PAIRS)
                        dve.tensor_copy(kv[0:NF, t % 2, :, 0:VW], both[0:NF, :, 0:VW]).then_inc(kv_half.sem, 1)
                        dve.tensor_copy(kv[NF:P, t % 2, :, VW:PW], both[NF:P, :, VW:PW]).then_inc(mid.drained(job), 1)
                    if s >= 8 and (s - 8) % 4 == 0 and (s - 8) // 4 < G:
                        t = (s - 8) // 4
                        dve.wait_ge(out.filled(t), out.full(r, t))
                        heads = out.bank(t)[:, 0:H * VW].rearrange("p (h d) -> p h d", h=H)
                        dve.reciprocal(rs[:, t % 2, :], heads[:, :, HD]).then_inc(rs_ready.sem, 1)
                        dve.wait_ge(rs_ready.sem, rs_ready.at(r, t + 1))
                        dve.tensor_tensor(o[:, t % 2, :].rearrange("p (h d) -> p h d", h=H), heads[:, :, 0:HD],
                                          bc(rs[:, t % 2, :, None], [P, H, HD]), ALU.mult).then_inc(out.drained(t), 1)
                    if s >= 12 and (s - 12) % 4 == 0 and (s - 12) // 4 < G:
                        t = (s - 12) // 4
                        rows.wait_slot(dve, r, t)
                        if t == 0:
                            dve.wait_ge(kept_ready.sem, kept_ready.at(r, 1))
                        drain(tail, r, ("y", t), lambda bank: dve.tensor_tensor(rows.slot[:, t % 2, :], kept[:, t, :], bank[:, 0:D], ALU.add))
                        rows.take_stats(dve, r, t, tail.drained(("y", t)), tail.full(r, ("y", t)))

            for t in range(G):
                normalise(0, t)
            for part in range(STEPS - UNITS):
                prepare(0, part)
            with dve.Fori(1, GROUPS, 1) as r:
                attend(r, True)
            attend(GROUPS, False)


def mlp_phase(nc, st, io, ident, y, weights, following):
    wide = [("hT", k) for k in range(IC)] + [("xT", c) for c in range(CH)]
    with ExitStack() as ctx:
        def sb(n, s, dt=F32):
            return ctx.enter_context(nc.sbuf_tensor(f"mlp_{n}", s, dt))

        def tally(n, per, start=None):
            return Tally(nc, f"mlp_{n}", per, start)

        w1, w2, b1, loaded = weights.w1, weights.w2, weights.b1, weights.loaded
        g1, c1, g2, c2, b2 = weights.g1, weights.c1, weights.g2, weights.c2, weights.b2
        u = sb("u", [P, G, D])
        ub = sb("ub", [P, G, D])
        uT = sb("uT", [P, CH, G * S])
        hT = sb("hT", [P, IC, G * S])
        n1, z = sb("n1", [P, G, D]), sb("z", [P, G, D])
        zraw, zmv = sb("zraw", [P, G, 6]), sb("zmv", [P, G, 2])
        zvar, zrstd, mhalf, eps = (sb(n, [P, G]) for n in ("zvar", "zrstd", "mhalf", "eps"))

        const_ready = tally("const_ready", 0)
        u_step = tally("u_step", G + 1, 0)
        u_ready = tally("u_ready", 1, 0)
        ub_ready = tally("ub_ready", 1)
        zraw_ready = [tally(f"z_stats{t}", 1) for t in range(G)]
        zmv_ready = tally("z_aggr", G)
        zr_ready = tally("z_rstd_step", 2)
        zn_ready = tally("z_norm_step", G + 2)
        x_ready = tally("x_ready", G)
        rows = Rows(ctx, nc, "mlp", st.x, st.mean[st.now ^ 1], st.rstd[st.now ^ 1], EPS)
        hid = Ring(ctx, nc, "mlp_hid", 4, wide, skipped=IC)
        outs = Ring(ctx, nc, "mlp_outs", 4, list(range(G)))
        block = ctx.enter_context(nc.Block())

        @block.sync
        def _(sp):
            following.fetch(sp, io)

        @block.gpsimd
        def _(pool):
            rows.pool_start(pool)
            pool.memset(mhalf[:, :], -0.5).then_inc(const_ready.sem, 1)
            pool.memset(eps[:, :], EPS_IN).then_inc(const_ready.sem, 1)
            pool.wait_ge(loaded.sem, 128)
            pool.wait_ge(const_ready.sem, 2)
            with pool.Fori(1, GROUPS + 1, 1) as r:
                pool.wait_ge(zn_ready.sem, zn_ready.at(r - 1, G))
                pool.wait_ge(u_ready.sem, u_ready.at(r - 1, 1))
                pool.tensor_tensor(ub[:, :, :], u[:, :, :], bc(b2[:, None, :], [P, G, D]), ALU.add).then_inc(ub_ready.sem, 1)
                pool.wait_ge(zmv_ready.sem, zmv_ready.at(r, G))
                pool.tensor_tensor(zvar[:, :], zmv[:, :, 1], eps[:, :], ALU.add).then_inc(zr_ready.sem, 1)
                pool.wait_ge(zr_ready.sem, zr_ready.at(r, 1))
                pool.tensor_tensor(zrstd[:, :], zvar[:, :], mhalf[:, :], ALU.pow).then_inc(zr_ready.sem, 1)
                for t in range(G):
                    rows.store(pool, r, t)
                rows.store_stats(pool, r)

        @block.tensor
        def _(pe):
            pe.wait_ge(loaded.sem, 128)

            def prepare(r):
                pe.wait_ge(u_ready.sem, u_ready.at(r, 1))
                for c in range(CH):
                    job = ("xT", c)
                    pe.wait_ge(hid.drained(job), hid.free(r, job))
                    for t in range(G):
                        mm = pe.transpose(hid.bank(job)[:, t * P:(t + 1) * P], u[:, t, c * P:(c + 1) * P], ident[:, :])
                    mm.then_inc(hid.filled(job), 1)

            def layer(r, more):
                for c in range(CH):
                    pe.wait_ge(hid.drained(("xT", c)), hid.full(r - 1, ("xT", c)))
                for i in range(IC):
                    job = ("hT", i)
                    pe.wait_ge(hid.drained(job), hid.free(r, job))
                    for k in range(CH):
                        mm = pe.matmul(hid.bank(job)[:, :], w1[:, k, i * P:(i + 1) * P], uT[:, k, :],
                                       start=(k == 0), stop=(k == CH - 1))
                    mm.then_inc(hid.filled(job), 1)
                if more:
                    prepare(r)
                for i in range(IC - 4, IC):
                    pe.wait_ge(hid.drained(("hT", i)), hid.full(r, ("hT", i)))
                for t in range(G):
                    pe.wait_ge(outs.drained(t), outs.free(r, t))
                    for i in range(IC):
                        mm = pe.matmul(outs.bank(t)[:, 0:D], hT[:, i, t * S:(t + 1) * S], w2[:, i, :],
                                       start=(i == 0), stop=(i == IC - 1))
                    mm.then_inc(outs.filled(t), 1)

            prepare(0)
            with pe.Fori(1, GROUPS, 1) as r:
                layer(r, True)
            layer(GROUPS, False)

        @block.scalar
        def _(act):
            act.wait_ge(loaded.sem, 128)

            def prepare(r):
                for c in range(CH):
                    act.wait_ge(hid.filled(("xT", c)), hid.full(r, ("xT", c)))
                    act.copy(uT[:, c, :], hid.bank(("xT", c))[:, :]).then_inc(hid.drained(("xT", c)), 1)

            def layer(r, more):
                for i in range(IC):
                    if i == 0:
                        act.wait_ge(outs.filled(G - 1), outs.free(r, G - 1))
                    act.wait_ge(hid.filled(("hT", i)), hid.full(r, ("hT", i)))
                    act.activation(hT[:, i, :], hid.bank(("hT", i))[:, :], ACT.Gelu, bias=b1[:, i:i + 1]).then_inc(hid.drained(("hT", i)), 1)
                if more:
                    prepare(r)

            prepare(0)
            with act.Fori(1, GROUPS, 1) as r:
                layer(r, True)
            layer(GROUPS, False)

        @block.vector
        def _(dve):
            dve.wait_ge(loaded.sem, 128)

            def prepare(r):
                wait_count(dve, u_ready.sem, u_ready.at(r, 0))
                for t in range(G):
                    dve.tensor_scalar(n1[:, t, :], y[:, seq(r + 1, t)], st.mean_in[:, seq(r + 1, t, 1)],
                                      st.rstd_in[:, seq(r + 1, t, 1)], ALU.subtract, ALU.mult).then_inc(u_step.sem, 1)
                dve.wait_ge(u_step.sem, u_step.at(r, G))
                dve.tensor_tensor(n1[:, :, :], n1[:, :, :], bc(g1[:, None, :], [P, G, D]), ALU.mult).then_inc(u_step.sem, 1)
                dve.wait_ge(u_step.sem, u_step.at(r, G + 1))
                dve.wait_ge(ub_ready.sem, ub_ready.at(r, 1))
                for c in range(CH):
                    if not isinstance(r, int):
                        dve.wait_ge(hid.filled(("xT", c)), hid.full(r - 1, ("xT", c)))
                dve.tensor_tensor(u[:, :, :], n1[:, :, :], bc(c1[:, None, :], [P, G, D]), ALU.add).then_inc(u_ready.sem, 1)

            def layer(r, more):
                if more:
                    prepare(r)
                dve.wait_ge(ub_ready.sem, ub_ready.at(r, 1))
                for t in range(G):
                    dve.wait_ge(outs.filled(t), outs.full(r, t))
                    dve.tensor_tensor(ub[:, t, :], ub[:, t, :], outs.bank(t)[:, 0:D], ALU.add).then_inc(outs.drained(t), 1)
                    dve.wait_ge(outs.drained(t), outs.full(r, t))
                    dve.bn_stats(zraw[:, t, :], ub[:, t, :]).then_inc(zraw_ready[t].sem, 1)
                    dve.wait_ge(loaded.sem, 128)
                    dve.wait_ge(zraw_ready[t].sem, zraw_ready[t].at(r, 1))
                    dve.bn_aggr(zmv[:, t, :], zraw[:, t, :]).then_inc(zmv_ready.sem, 1)
                dve.wait_ge(zr_ready.sem, zr_ready.at(r, 2))
                for t in range(G):
                    dve.tensor_scalar(z[:, t, :], ub[:, t, :], zmv[:, t, 0:1], zrstd[:, t:t + 1],
                                      ALU.subtract, ALU.mult).then_inc(zn_ready.sem, 1)
                dve.wait_ge(zn_ready.sem, zn_ready.at(r, G))
                dve.tensor_tensor(z[:, :, :], z[:, :, :], bc(g2[:, None, :], [P, G, D]), ALU.mult).then_inc(zn_ready.sem, 1)
                dve.wait_ge(zn_ready.sem, zn_ready.at(r, G + 1))
                dve.tensor_tensor(z[:, :, :], z[:, :, :], bc(c2[:, None, :], [P, G, D]), ALU.add).then_inc(zn_ready.sem, 1)
                dve.wait_ge(zn_ready.sem, zn_ready.at(r, G + 2))
                for t in range(G):
                    rows.wait_slot(dve, r, t)
                    dve.tensor_tensor(rows.slot[:, t % 2, :], st.x[:, seq(r, t)], z[:, t, :], ALU.add).then_inc(x_ready.sem, 1)
                    rows.take_stats(dve, r, t, x_ready.sem, x_ready.at(r, t + 1))

            prepare(0)
            with dve.Fori(1, GROUPS, 1) as r:
                layer(r, True)
            layer(GROUPS, False)
    st.turn()


class Tile:

    def __init__(self, r, c):
        self.number = r * 2 + c
        self.slot = c % 2
        self.use = r + c // 2
        self.exists = isinstance(r, int) is False or 0 <= c < TILES


HEAD = 5


def tile_steps(eng, step, tail):
    for c in range(HEAD):
        step(0, c)
    with eng.Fori(1, (TILES - HEAD) // 2 + 1, 1) as r:
        for j in range(2):
            step(r, HEAD - 2 + j)
    for c in range(TILES, TILES + tail):
        step(0, c)


def experts_phase(nc, st, io, ident, out, tables):
    mean, rstd = st.mean[st.now], st.rstd[st.now]
    slot_x = nc.dram_tensor("slot_x", (TILES * P, ROW), F32, kind="Internal").ap()
    pair = nc.dram_tensor("pair", (2 * B * S + TILES * P, D), F32, kind="Internal").ap()
    W1, W2 = CH * 2 * EI, EC * D
    with ExitStack() as ctx:
        def keep(n, s, dt=F32):
            return ctx.enter_context(nc.sbuf_tensor(f"moe_{n}", s, dt))

        w1, w2 = keep("w1", [P, E * W1]), keep("w2", [P, E * W2])
        logits = keep("logits", [P, B * E])
        unused = keep("unused", [P, 1, ROW])
        weight = [keep(f"weight{w}", [P, B]) for w in range(2)]
        place = keep("place", [P, B, 2], I32)
        owner = keep("owner", [1, TILES], I32)
        w_loaded = Tally(nc, "moe_weights_loaded", 0)
        zero_stored = Tally(nc, "moe_zero_stored", 0)

        route_stage(nc, st, io, ident, logits, tables, unused, w1, w2, w_loaded, slot_x, zero_stored)
        sort_stage(nc, logits, tables, weight, place, owner)

        with ExitStack() as ctx2:
            xn = ctx2.enter_context(nc.sbuf_tensor("scatter_xn", [P, 2, G, 2, ROW], F32))
            index = ctx2.enter_context(nc.sbuf_tensor("scatter_index", [P, 2, 2 * G], I32))
            xn_ready = [Tally(nc, f"scatter_xn_ready{k}", 1, 0) for k in range(2)]
            index_ready = [Tally(nc, f"scatter_index_ready{k}", 1, 0) for k in range(2)]
            row_step = Tally(nc, "scatter_row_step", 4 * (G + 2))
            sent = [Tally(nc, f"scatter_sent{k}", 2 * G * 16, 0) for k in range(2)]
            block = ctx2.enter_context(nc.Block())

            @block.vector
            def _(dve):
                def turn(r):
                    for k in range(2):
                        g = r * 2 + (k - 1)
                        wait_count(dve, sent[k].sem, sent[k].at(r, -2 * G * 16))
                        for w in range(2):
                            for t in range(G):
                                dve.tensor_scalar(xn[:, k, t, w, 0:D], st.x[:, seq(g, t)], mean[:, seq(g, t, 1)],
                                                  rstd[:, seq(g, t, 1)], ALU.subtract, ALU.mult).then_inc(row_step.sem, 1)
                            dve.tensor_scalar(xn[:, k, :, w, D], tables.home[:, bass.ds(g * G + (w * B - G), G)], 1.0, None,
                                              ALU.mult).then_inc(row_step.sem, 1)
                            dve.tensor_scalar(xn[:, k, :, w, D + 1], weight[w][:, group(g, 1)], 1.0, None,
                                              ALU.mult).then_inc(row_step.sem, 1)
                        dve.wait_ge(row_step.sem, row_step.at(r, (k + 1) * 2 * (G + 2)))
                        dve.sem_inc(xn_ready[k].sem, 1)

                turn(1)
                with dve.Fori(2, GROUPS // 2 + 1, 1) as r:
                    turn(r)

            @block.gpsimd
            def _(pool):
                pool.wait_ge(zero_stored.sem, 16)

                def turn(r):
                    for k in range(2):
                        pool.wait_ge(zero_stored.sem, 16)
                        wait_count(pool, sent[k].sem, sent[k].at(r, -2 * G * 16))
                        pool.tensor_copy(index[:, k, :].rearrange("p (t w) -> p t w", w=2),
                                         place[:, bass.ds(r * (2 * G) + (k - 2) * G, G), :]).then_inc(index_ready[k].sem, 1)
                        pool.wait_ge(zero_stored.sem, 16)
                        pool.wait_ge(index_ready[k].sem, index_ready[k].at(r, 0))
                        pool.wait_ge(xn_ready[k].sem, xn_ready[k].at(r, 0))
                        for t in range(G):
                            for w in range(2):
                                col = 2 * t + w
                                pool.indirect_dma_start(slot_x, bass.IndirectOffsetOnAxis(index[:, k, col:col + 1], 0),
                                                        xn[:, k, t, w, :], None).then_inc(sent[k].sem, 16)

                turn(1)
                with pool.Fori(2, GROUPS // 2 + 1, 1) as r:
                    turn(r)
                for k in range(2):
                    pool.wait_ge(sent[k].sem, sent[k].at(GROUPS // 2, 0))

        tiles_stage(nc, ident, w1, w2, W1, W2, owner, w_loaded, slot_x, pair, tables)

        with ExitStack() as ctx2:
            res = ctx2.enter_context(nc.sbuf_tensor("sum_res", [P, 2, 2, G * D], F32))
            arrived = [Tally(nc, f"sum_arrived{k}", 32, 0) for k in range(2)]
            first_added = [Tally(nc, f"sum_first_added{k}", 1) for k in range(2)]
            added = [Tally(nc, f"sum_added{k}", 1) for k in range(2)]
            out_stored = Tally(nc, "out_stored", 0)
            block = ctx2.enter_context(nc.Block())

            @block.sync
            def _(sp):
                rows = pair.rearrange("(n p) d -> p n d", p=P)
                with sp.Fori(1, GROUPS // 2 + 1, 1) as r:
                    for k in range(2):
                        sp.wait_ge(added[k].sem, added[k].at(r, 0))
                        for w in range(2):
                            sp.dma_start(res[:, k, w, :].rearrange("p (n d) -> p n d", d=D),
                                         rows[:, bass.ds(r * (2 * G) + (w * B + (k - 2) * G), G), :]).then_inc(arrived[k].sem, 16)

            @block.vector
            def _(dve):
                with dve.Fori(1, GROUPS // 2 + 1, 1) as r:
                    for k in range(2):
                        here = st.x[:, group(r * 2 + (k - 1), D)]
                        dve.wait_ge(arrived[k].sem, arrived[k].at(r, 0))
                        dve.tensor_tensor(here, here, res[:, k, 0, :], ALU.add).then_inc(first_added[k].sem, 1)
                        dve.wait_ge(first_added[k].sem, first_added[k].at(r, 1))
                        dve.tensor_tensor(here, here, res[:, k, 1, :], ALU.add).then_inc(added[k].sem, 1)

            @block.scalar
            def _(act):
                rows = out.rearrange("(n p) d -> p n d", p=P)
                with act.Fori(1, GROUPS // 2 + 1, 1) as r:
                    for k in range(2):
                        act.wait_ge(added[k].sem, added[k].at(r, 1))
                        act.dma_start(rows[:, bass.ds(r * (2 * G) + (k - 2) * G, G), :],
                                      st.x[:, group(r * 2 + (k - 1), D)].rearrange("p (n d) -> p n d", d=D)).then_inc(out_stored.sem, 16)
                act.wait_ge(out_stored.sem, 16 * GROUPS)


def route_stage(nc, st, io, ident, logits, tables, unused, w1, w2, w_loaded, slot_x, zero_stored):
    mean, rstd = st.mean[st.now], st.rstd[st.now]
    with ExitStack() as ctx:
        def sb(n, s, dt=F32):
            return ctx.enter_context(nc.sbuf_tensor(f"route_{n}", s, dt))

        router, loaded = tables.router, tables.loaded
        xn, xT = sb("xn", [P, 2, G, D]), sb("xT", [P, 2, CH, G * S])
        zero_ready = Tally(nc, "route_zero_ready", 0)
        xn_ready = [Tally(nc, f"route_xn_ready{k}", G) for k in range(2)]
        turned = Ring(ctx, nc, "route_turned", 4, [(k, c) for k in range(2) for c in range(CH)])
        ring = Ring(ctx, nc, "route_logits", 2, list(range(2)))
        block = ctx.enter_context(nc.Block())

        @block.sync
        def _(sp):
            sp.wait_ge(zero_ready.sem, 2)
            sp.dma_start(slot_x.rearrange("(n p) d -> p n d", p=P), bc(unused[:, :, :], [P, TILES, ROW])).then_inc(zero_stored.sem, 16)
            for e in range(E):
                sp.dma_start(w1[:, :].rearrange("p (e c o) -> p e c o", e=E, c=CH)[:, e],
                             io["moe_w1"][e].rearrange("(c p) o -> p c o", p=P)).then_inc(w_loaded.sem, 16)
                sp.dma_start(w2[:, :].rearrange("p (e c o) -> p e c o", e=E, c=EC)[:, e],
                             io["moe_w2"][e].rearrange("(c p) o -> p c o", p=P)).then_inc(w_loaded.sem, 16)

        @block.gpsimd
        def _(pool):
            pool.memset(unused[:, :, :], 0.0).then_inc(zero_ready.sem, 1)
            pool.wait_ge(zero_ready.sem, 1)
            pool.memset(unused[:, 0, D:D + 1], float(2 * B * S + TILES * P)).then_inc(zero_ready.sem, 1)

        @block.tensor
        def _(pe):
            pe.wait_ge(loaded.sem, tables.total)
            with pe.Fori(1, GROUPS // 2 + 1, 1) as r:
                for k in range(2):
                    for c in range(CH):
                        pe.wait_ge(turned.drained((k, c)), turned.free(r, (k, c)))
                        for t in range(G):
                            pe.wait_ge(xn_ready[k].sem, xn_ready[k].at(r, t + 1))
                            mm = pe.transpose(turned.bank((k, c))[:, t * P:(t + 1) * P], xn[:, k, t, c * P:(c + 1) * P], ident[:, :])
                        mm.then_inc(turned.filled((k, c)), 1)
                for k in range(2):
                    for c in range(CH):
                        pe.wait_ge(turned.drained((k, c)), turned.full(r, (k, c)))
                    pe.wait_ge(ring.drained(k), ring.free(r, k))
                    for t in range(G):
                        for c in range(CH):
                            mm = pe.matmul(ring.bank(k)[:, t * E:(t + 1) * E], xT[:, k, c, t * S:(t + 1) * S], router[:, c, :],
                                           start=(c == 0), stop=(c == CH - 1))
                    mm.then_inc(ring.filled(k), 1)

        @block.scalar
        def _(act):
            with act.Fori(1, GROUPS // 2 + 1, 1) as r:
                for k in range(2):
                    for c in range(CH):
                        act.wait_ge(turned.filled((k, c)), turned.full(r, (k, c)))
                        act.wait_ge(ring.filled(k), ring.free(r, k))
                        act.copy(xT[:, k, c, :], turned.bank((k, c))[:, :]).then_inc(turned.drained((k, c)), 1)

        @block.vector
        def _(dve):
            with dve.Fori(1, GROUPS // 2 + 1, 1) as r:
                for k in range(2):
                    g = r * 2 + (k - 1)
                    for t in range(G):
                        dve.tensor_scalar(xn[:, k, t, :], st.x[:, seq(g, t)], mean[:, seq(g, t, 1)],
                                          rstd[:, seq(g, t, 1)], ALU.subtract, ALU.mult).then_inc(xn_ready[k].sem, 1)
                for k in range(2):
                    g = r * 2 + (k - 1)
                    dve.wait_ge(ring.filled(k), ring.full(r, k))
                    dve.tensor_scalar(logits[:, group(g, E)], ring.bank(k)[:, 0:G * E], 1.0, None, ALU.mult).then_inc(ring.drained(k), 1)


def sort_stage(nc, logits, tables, weight, place, owner):
    with ExitStack() as ctx:
        def sb(n, s, dt=F32):
            return ctx.enter_context(nc.sbuf_tensor(f"sort_{n}", s, dt))

        PAD = B // 2
        EPAD = E // 2
        earlier, tile_no, before, loaded = tables.earlier, tables.tile_no, tables.before, tables.loaded
        ones = sb("ones", [P, P], BF16)
        chosen = sb("chosen", [P, B * E], BF16)
        top, total, recip = sb("top", [P, B]), sb("total", [P, B]), sb("recip", [P, B])
        prob, rank = sb("prob", [P, B, E]), sb("rank", [P, B, E])
        above, tied = sb("above", [P, B, E, E]), sb("tied", [P, B, E, E])
        flag = [sb(f"flag{w}", [P, B * E]) for w in range(2)]
        kept_prob = [sb(f"kept_prob{w}", [P, B, E]) for w in range(2)]
        run = [sb(f"run{i}", [P, PAD + B, E]) for i in range(2)]
        need = [sb(f"need{i}", [P, EPAD + E]) for i in range(2)]
        base = sb("base", [P, E])
        slot = sb("slot", [P, B, E])
        mine = [sb(f"mine{w}", [P, B, E]) for w in range(2)]
        reached = sb("reached", [P, TILES, E])
        count = sb("count", [P, TILES])
        position = sb("position", [P, 2, B])
        cleared = Tally(nc, "sort_cleared", 0)
        route_step, exp_ready = Tally(nc, "sort_route_step", 0), Tally(nc, "sort_exp_ready", 0)
        chosen_ready, counted = Tally(nc, "sort_chosen_ready", 0), Tally(nc, "sort_counted", 0)
        step = Tally(nc, "sort_step", 0)
        before_bank = ctx.enter_context(nc.psum_tensor("sort_before_bank", [P, 512], F32))
        total_bank = ctx.enter_context(nc.psum_tensor("sort_total_bank", [P, 512], F32))
        block = ctx.enter_context(nc.Block())

        @block.gpsimd
        def _(pool):
            pool.memset(ones[:, :], 1.0).then_inc(cleared.sem, 1)
            for i in range(2):
                pool.memset(run[i][:, 0:PAD, :], 0.0).then_inc(cleared.sem, 1)
                pool.memset(need[i][:, 0:EPAD], 0.0).then_inc(cleared.sem, 1)

        @block.tensor
        def _(pe):
            pe.wait_ge(loaded.sem, tables.total)
            pe.wait_ge(cleared.sem, 5)
            pe.wait_ge(chosen_ready.sem, 1)
            pe.matmul(before_bank[:, 0:B * E], earlier[:, :], chosen[:, :], start=True, stop=True).then_inc(counted.sem, 1)
            pe.matmul(total_bank[:, 0:B * E], ones[:, :], chosen[:, :], start=True, stop=True).then_inc(counted.sem, 1)

        @block.scalar
        def _(act):
            act.wait_ge(route_step.sem, 2)
            act.activation(prob[:, :, :], prob[:, :, :], ACT.Exp).then_inc(exp_ready.sem, 1)

        @block.vector
        def _(dve):
            each = logits[:, :].rearrange("p (b e) -> p b e", e=E)
            dve.tensor_reduce(top[:, :], each, AX.X, ALU.max).then_inc(route_step.sem, 1)
            dve.wait_ge(route_step.sem, 1)
            dve.tensor_tensor(prob[:, :, :], each, bc(top[:, :, None], [P, B, E]), ALU.subtract).then_inc(route_step.sem, 1)
            dve.wait_ge(exp_ready.sem, 1)
            dve.tensor_reduce(total[:, :], prob[:, :, :], AX.X, ALU.add).then_inc(route_step.sem, 1)
            dve.wait_ge(route_step.sem, 3)
            dve.reciprocal(recip[:, :], total[:, :]).then_inc(route_step.sem, 1)
            dve.wait_ge(route_step.sem, 4)
            dve.tensor_tensor(prob[:, :, :], prob[:, :, :], bc(recip[:, :, None], [P, B, E]), ALU.mult).then_inc(route_step.sem, 1)
            dve.wait_ge(loaded.sem, tables.total)
            dve.wait_ge(route_step.sem, 5)
            other, this = (bc(a, [P, B, E, E]) for a in (prob[:, :, None, :], prob[:, :, :, None]))
            dve.tensor_tensor(above[:, :, :, :], other, this, ALU.is_gt).then_inc(route_step.sem, 1)
            dve.tensor_tensor(tied[:, :, :, :], other, this, ALU.is_equal).then_inc(route_step.sem, 1)
            flat_above, flat_tied = (a[:, :, :, :].rearrange("p t i j -> p t (i j)") for a in (above, tied))
            dve.wait_ge(route_step.sem, 7)
            dve.tensor_tensor(flat_tied, flat_tied, bc(before[:, :, :], [P, B, E * E]), ALU.mult).then_inc(route_step.sem, 1)
            dve.wait_ge(route_step.sem, 8)
            dve.tensor_tensor(flat_above, flat_above, flat_tied, ALU.add).then_inc(route_step.sem, 1)
            dve.wait_ge(route_step.sem, 9)
            dve.tensor_reduce(rank[:, :, :], above[:, :, :, :], AX.X, ALU.add).then_inc(route_step.sem, 1)
            dve.wait_ge(route_step.sem, 10)
            for w in range(2):
                dve.tensor_scalar(flag[w][:, :].rearrange("p (b e) -> p b e", e=E), rank[:, :, :], float(w), None,
                                  ALU.is_equal).then_inc(route_step.sem, 1)
            dve.wait_ge(route_step.sem, 12)
            dve.tensor_tensor(chosen[:, :], flag[0][:, :], flag[1][:, :], ALU.add).then_inc(chosen_ready.sem, 1)
            for w in range(2):
                dve.scalar_tensor_tensor(kept_prob[w][:, :, :], rank[:, :, :], float(w), prob[:, :, :],
                                         ALU.is_equal, ALU.mult).then_inc(route_step.sem, 1)
            dve.wait_ge(route_step.sem, 14)
            for w in range(2):
                dve.tensor_reduce(weight[w][:, :], kept_prob[w][:, :, :], AX.X, ALU.add)
            dve.wait_ge(cleared.sem, 5)
            dve.wait_ge(counted.sem, 2)
            dve.tensor_copy(run[0][:, PAD:, :], total_bank[:, 0:B * E].rearrange("p (b e) -> p b e", e=E)).then_inc(step.sem, 1)
            at, n = 0, 1
            for reach in (1, 2, 4, 8, 16):
                dve.wait_ge(step.sem, n)
                dve.tensor_tensor(run[1 - at][:, PAD:, :], run[at][:, PAD:, :], run[at][:, PAD - reach:PAD + B - reach, :],
                                  ALU.add).then_inc(step.sem, 1)
                at, n = 1 - at, n + 1
            run_end = run[at]
            dve.wait_ge(step.sem, n)
            dve.tensor_scalar(need[1][:, EPAD:], run_end[:, PAD + B - 1, :], 1.0 / P, (P - 1) / P - 0.5 + 0.5 / P,
                              ALU.mult, ALU.add).then_inc(step.sem, 1)
            dve.wait_ge(step.sem, n + 1)
            dve.tensor_scalar(base[:, :], need[1][:, EPAD:], ROUND, None, ALU.add).then_inc(step.sem, 1)
            dve.wait_ge(step.sem, n + 2)
            dve.tensor_scalar(need[0][:, EPAD:], base[:, :], -ROUND, None, ALU.add).then_inc(step.sem, 1)
            at, n = 0, n + 3
            for reach in (1, 2, 4):
                dve.wait_ge(step.sem, n)
                dve.tensor_tensor(need[1 - at][:, EPAD:], need[at][:, EPAD:], need[at][:, EPAD - reach:EPAD + E - reach],
                                  ALU.add).then_inc(step.sem, 1)
                at, n = 1 - at, n + 1
            dve.wait_ge(step.sem, n)
            dve.tensor_scalar(base[:, :], need[at][:, EPAD - 1:EPAD + E - 1], float(P), None, ALU.mult).then_inc(step.sem, 1)
            dve.tensor_tensor(slot[:, :, :], before_bank[:, 0:B * E].rearrange("p (b e) -> p b e", e=E),
                              run_end[:, PAD - 1:PAD + B - 1, :], ALU.add).then_inc(step.sem, 1)
            dve.tensor_tensor(reached[:, :, :], bc(tile_no[:, :, None], [P, TILES, E]),
                              bc(need[at][:, None, EPAD:], [P, TILES, E]), ALU.is_ge).then_inc(step.sem, 1)
            dve.wait_ge(step.sem, n + 3)
            dve.tensor_tensor(slot[:, :, :], slot[:, :, :], bc(base[:, None, :], [P, B, E]), ALU.add).then_inc(step.sem, 1)
            dve.tensor_reduce(count[:, :], reached[:, :, :], AX.X, ALU.add).then_inc(step.sem, 1)
            dve.wait_ge(step.sem, n + 5)
            for w in range(2):
                dve.tensor_tensor(mine[w][:, :, :].rearrange("p b e -> p (b e)"), slot[:, :, :].rearrange("p b e -> p (b e)"),
                                  flag[w][:, :], ALU.mult).then_inc(step.sem, 1)
            dve.tensor_scalar(owner[:, :], count[0:1, :], float(E - 1), None, ALU.min)
            dve.wait_ge(step.sem, n + 7)
            for w in range(2):
                dve.tensor_reduce(position[:, w, :], mine[w][:, :, :], AX.X, ALU.add).then_inc(step.sem, 1)
            dve.wait_ge(step.sem, n + 9)
            dve.tensor_copy(place[:, :, :].rearrange("p b w -> p w b"), position[:, :, :])


def tiles_stage(nc, ident, w1, w2, W1, W2, owner, w_loaded, slot_x, pair, tables):
    with ExitStack() as ctx:
        def sb(n, s, dt=F32):
            return ctx.enter_context(nc.sbuf_tensor(f"tile_{n}", s, dt))

        def bank(n):
            return ctx.enter_context(nc.psum_tensor(f"tile_{n}_bank", [P, 512], F32))

        def signal(n):
            return nc.alloc_semaphore(f"tile_{n}")

        xr, xT = sb("rows", [P, 2, ROW]), sb("xT", [P, 2, CH * P])
        tag = sb("tag", [P, 2, 2])
        home, weight = sb("home", [P, 2], I32), sb("weight", [P, 2])
        sg, y, yT = sb("silu", [P, 2, EI]), sb("y", [P, 2, EI]), sb("yT", [P, 2, EI])
        res = sb("result", [P, 2, D])
        xT_bank, yT_bank = bank("xT"), bank("yT")
        gate_bank, up_bank, res_bank = ([bank(f"{n}{s}") for s in range(2)] for n in ("gate", "up", "res"))
        x_turned, x_kept, gate_full, up_full = signal("x_turned"), signal("x_kept"), signal("gate_full"), signal("up_full")
        silu_ready, y_ready, y_turned, y_kept = signal("silu_ready"), signal("y_ready"), signal("y_turned"), signal("y_kept")
        res_full = signal("res_full")
        tag_kept, home_ready, weight_ready = signal("tag_kept"), signal("home_ready"), signal("weight_ready")
        res_kept = [signal(f"res_kept{s}") for s in range(2)]
        x_loaded, res_sent = ([signal(f"{n}{s}") for s in range(2)] for n in ("x_loaded", "res_sent"))
        block = ctx.enter_context(nc.Block())

        @block.sync
        def _(sp):
            def step(r, c):
                t = Tile(r, c)
                if t.exists:
                    wait_count(sp, x_turned, t.number - 1)
                    wait_count(sp, tag_kept, t.number - 1)
                    sp.dma_start(xr[:, t.slot, :], slot_x[bass.ds(t.number * P, P), :]).then_inc(x_loaded[t.slot], 16)

            tile_steps(sp, step, 0)

        @block.gpsimd
        def _(pool):
            pool.wait_ge(w_loaded.sem, 16 * 2 * E)

            def step(r, c):
                t = Tile(r, c - HEAD)
                if t.exists:
                    pool.wait_ge(w_loaded.sem, 16 * 2 * E)
                    pool.wait_ge(res_kept[t.slot], r + ((c - HEAD) // 2 + 1))
                    pool.indirect_dma_start(pair, bass.IndirectOffsetOnAxis(home[:, t.slot:t.slot + 1], 0),
                                            res[:, t.slot, :], None).then_inc(res_sent[t.slot], 16)

            tile_steps(pool, step, HEAD)
            for s in range(2):
                pool.wait_ge(res_sent[s], 16 * len(range(s, TILES, 2)))

        @block.tensor
        def _(pe):
            def step(r, c):
                t = Tile(r, c)
                if t.exists:
                    pe.wait_ge(x_loaded[t.slot], (t.use + 1) * 16)
                    wait_count(pe, x_kept, t.number)
                    for k in range(CH):
                        mm = pe.transpose(xT_bank[:, k * P:(k + 1) * P], xr[:, t.slot, k * P:(k + 1) * P], ident[:, :])
                    mm.then_inc(x_turned, 1)
                t = Tile(r, c - 1)
                if t.exists:
                    e = pe.value_load(owner[0:1, bass.ds(t.number, 1)], min_val=0, max_val=E - 1)
                    pe.wait_ge(x_kept, t.number + 1)
                    for banks, col, full, drained in ((gate_bank, 0, gate_full, silu_ready), (up_bank, EI, up_full, y_ready)):
                        wait_count(pe, drained, t.number - 1)
                        for k in range(CH):
                            mm = pe.matmul(banks[t.slot][:, :], xT[:, t.slot, k * P:(k + 1) * P],
                                           w1[:, bass.ds(e * W1 + (k * 2 * EI + col), EI)], start=(k == 0), stop=(k == CH - 1))
                        mm.then_inc(full, 1)
                t = Tile(r, c - 2)
                if t.exists:
                    pe.wait_ge(y_ready, t.number + 1)
                    wait_count(pe, y_kept, t.number)
                    for k in range(EC):
                        mm = pe.transpose(yT_bank[:, k * P:(k + 1) * P], y[:, t.slot, k * P:(k + 1) * P], ident[:, :])
                    mm.then_inc(y_turned, 1)
                t = Tile(r, c - 3)
                if t.exists:
                    e = pe.value_load(owner[0:1, bass.ds(t.number, 1)], min_val=0, max_val=E - 1)
                    pe.wait_ge(y_kept, t.number + 1)
                    wait_count(pe, res_kept[t.slot], t.use)
                    for k in range(EC):
                        mm = pe.matmul(res_bank[t.slot][:, 0:D], yT[:, t.slot, k * P:(k + 1) * P],
                                       w2[:, bass.ds(e * W2 + k * D, D)], start=(k == 0), stop=(k == EC - 1))
                    mm.then_inc(res_full, 1)

            pe.wait_ge(w_loaded.sem, 16 * 2 * E)
            tile_steps(pe, step, 3)

        @block.scalar
        def _(act):
            def step(r, c):
                t = Tile(r, c)
                if t.exists:
                    act.wait_ge(x_turned, t.number + 1)
                    wait_count(act, up_full, t.number - 1)
                    act.copy(xT[:, t.slot, :], xT_bank[:, 0:CH * P]).then_inc(x_kept, 1)
                t = Tile(r, c - 1)
                if t.exists:
                    act.wait_ge(gate_full, t.number + 1)
                    wait_count(act, y_ready, t.number - 1)
                    act.activation(sg[:, t.slot, :], gate_bank[t.slot][:, :], ACT.Silu).then_inc(silu_ready, 1)
                t = Tile(r, c - 2)
                if t.exists:
                    act.wait_ge(y_turned, t.number + 1)
                    wait_count(act, res_full, t.number - 1)
                    act.copy(yT[:, t.slot, :], yT_bank[:, :]).then_inc(y_kept, 1)

            tile_steps(act, step, 2)

        @block.vector
        def _(dve):
            def step(r, c):
                t = Tile(r, c - 1)
                if t.exists:
                    dve.wait_ge(up_full, t.number + 1)
                    dve.wait_ge(silu_ready, t.number + 1)
                    wait_count(dve, y_turned, t.number - 1)
                    dve.tensor_tensor(y[:, t.slot, :], sg[:, t.slot, :], up_bank[t.slot][:, :], ALU.mult).then_inc(y_ready, 1)
                t = Tile(r, c - 2)
                if t.exists:
                    wait_count(dve, res_sent[t.slot], t.use * 16)
                    dve.wait_ge(tag_kept, t.number + 1)
                    dve.tensor_tensor(home[:, t.slot:t.slot + 1], tag[:, t.slot, 0:1],
                                      tables.spare[:, bass.ds(t.number, 1)], ALU.min).then_inc(home_ready, 1)
                    dve.tensor_copy(weight[:, t.slot:t.slot + 1], tag[:, t.slot, 1:2]).then_inc(weight_ready, 1)
                t = Tile(r, c)
                if t.exists:
                    dve.wait_ge(x_loaded[t.slot], (t.use + 1) * 16)
                    wait_count(dve, home_ready, t.number - 1)
                    wait_count(dve, weight_ready, t.number - 1)
                    dve.tensor_copy(tag[:, t.slot, :], xr[:, t.slot, D:ROW]).then_inc(tag_kept, 1)
                t = Tile(r, c - 3)
                if t.exists:
                    dve.wait_ge(res_full, t.number + 1)
                    dve.wait_ge(home_ready, t.number + 1)
                    dve.wait_ge(weight_ready, t.number + 1)
                    wait_count(dve, res_sent[t.slot], t.use * 16)
                    dve.tensor_scalar(res[:, t.slot, :], res_bank[t.slot][:, 0:D], weight[:, t.slot:t.slot + 1], None,
                                      ALU.mult).then_inc(res_kept[t.slot], 1)

            tile_steps(dve, step, 3)


def program(nc, io, out, phases=(0, 6)):
    with ExitStack() as ctx:
        ident = ctx.enter_context(nc.sbuf_tensor("ident", [P, P], F32))
        st = Stream(ctx, nc)
        even = Region(ctx, nc, "weights_even", 3 * CH * INNER + P // 2)
        odd = Region(ctx, nc, "weights_odd", 4 * CH * D + 3 * D)
        w_self = AttentionWeights(nc, even.restart(), "self", "self")
        w_mask = AttentionWeights(nc, odd.restart(), "mask", "masked")
        w_bit = BitlinearWeights(nc, even.restart())
        w_perf = PerformerWeights(nc, odd.restart())
        w_mlp = MlpWeights(nc, even.restart())
        w_cross = AttentionWeights(nc, odd.restart(), "cross", "cross")
        tables = RouterTables(nc, even.restart())
        load_phase(nc, st, io, ident, (w_self, w_mask, w_bit, w_perf, w_cross, tables)[phases[0]])
        every = [lambda: attention_phase(nc, st, io, ident, "self", "self", w_self, w_mask),
                 lambda: attention_phase(nc, st, io, ident, "mask", "masked", w_mask, w_bit),
                 lambda: bitlinear_phase(nc, st, io, w_bit, w_perf),
                 lambda: second_layer_self(nc, st, io, ident, w_perf, w_mlp, w_cross),
                 lambda: attention_phase(nc, st, io, ident, "cross", "cross", w_cross, tables),
                 lambda: experts_phase(nc, st, io, ident, out, tables)]
        for phase in every[phases[0]:phases[1]]:
            with nc.cleanup_on_exit():
                phase()
        if phases[1] < len(every):
            store_phase(nc, st, out)


def store_phase(nc, st, out):
    with ExitStack() as ctx:
        stored = Tally(nc, "stored", 0)
        block = ctx.enter_context(nc.Block())

        @block.sync
        def _(sp):
            sp.dma_start(out.rearrange("(n p) d -> p n d", p=P), st.x[:, :].rearrange("p (n d) -> p n d", n=B)).then_inc(stored.sem, 16)
            sp.wait_ge(stored.sem, 16)


def tables():
    bf16 = mybir.dt.np(BF16)
    pos = np.arange(NC + GS, dtype=np.float32)[:, None]
    div = np.exp(np.arange(0, HD, 2, dtype=np.float32) * np.float32(-np.log(10000.0) / HD))
    ang = (pos * div).astype(np.float32)
    pe = np.stack([np.sin(ang), np.cos(ang)], axis=-1).reshape(NC + GS, HD)
    rot = np.empty((HD, NC + GS), np.float32)
    rot[0::2] = -pe[:, HD // 2:].T
    rot[1::2] = pe[:, :HD // 2].T
    rows = np.tile(rot, (HH, 1))
    heads = np.repeat(np.eye(HH, dtype=np.float32), HD, axis=0)
    local = np.arange(GS)
    q_pos = np.concatenate([local, local])
    k_pos = np.concatenate([local, NC + local, np.arange(NC)])
    rot_k = heads[:, :, None] * rows[:, None, k_pos]
    seen = np.zeros((P, UH, KL), np.float32)
    seen[:, :, 0:GS] = (local[None, :] <= (np.arange(P) % GS)[:, None])[:, None, :]
    seen[GS:, :, GS:] = 1.0
    parts, rest = np.zeros((P, 1), np.float32), np.float64(-MASK_FILL)
    for i in range(3):
        parts[i] = np.float32(np.float64(rest).astype(bf16))
        rest -= np.float64(parts[i, 0])
    assert rest == 0
    return {
        "ident": np.eye(P, dtype=np.float32),
        "identb": np.eye(P, dtype=np.float32).astype(bf16),
        "rot_q": rows[:, q_pos], "rot_k": rot_k, "heads": heads, "parts": parts,
        "half_heads": 0.5 * heads, "before": np.tile(np.tril(np.ones((E, E), np.float32), -1).reshape(1, -1), (P, 1)),
        "earlier": np.triu(np.ones((P, P), np.float32), 1).astype(bf16),
        "home": np.arange(2 * B, dtype=np.float32) * S + np.arange(P, dtype=np.float32)[:, None],
        "spare": np.arange(TILES, dtype=np.float32) * P + np.arange(P, dtype=np.float32)[:, None] + 2 * B * S,
        "tile_no": np.tile(np.arange(TILES, dtype=np.float32), (P, 1)),
        "causal": np.where(seen > 0, 0.0, -1e30).astype(bf16),
    }


def chunked(vec):
    return vec.reshape(-1, P).T


def layout(a):
    swap = np.arange(D).reshape(-1, 2)[:, ::-1].reshape(-1)
    io = dict(tables())
    io["x"] = a["x"].reshape(B * S, D)
    io["ctx"] = a["ctx_1024"].reshape(B * S, D)
    mask = a["mask_BxS2_bf1"].reshape(GROUPS, G * S).view(np.uint8)
    io["mask"] = np.concatenate([mask[:1], mask])
    w, b = a["L0_attn_w_attn"], a["L0_attn_b_attn"]
    io["self_wq"], io["self_wk"], io["self_wv"] = w[0:D][swap].T, w[D:2 * D][swap].T, w[2 * D:].T
    io["self_bq"], io["self_bk"], io["self_bv"] = chunked(b[0:D][swap]), chunked(b[D:2 * D][swap]), b[2 * D:]
    io["self_wo"], io["self_bo"] = a["L0_attn_w_proj"].T, a["L0_attn_b_proj"]
    io["self_assign"] = np.repeat(a["L0_attn_w_assign"][0:NC], 2, axis=0).T
    for n in "qkvo":
        io[f"mask_w{n}"] = a[f"L0_xattn_W{n}"].T
        io[f"cross_w{n}"] = a[f"L1_xattn_w_{n}"].T
    io["mask_bq"], io["mask_bk"] = chunked(a["L0_xattn_bq"]), chunked(a["L0_xattn_bk"])
    for n in ("gate", "up", "down"):
        io[f"bit_{n}"] = a[f"L0_ffn_w_{n}"].T
    io["perf_wq"], io["perf_wk"], io["perf_wv"] = (a[f"L1_attn_w{n}"].reshape(D, D) for n in "qkv")
    io["perf_wo"] = a["L1_attn_wo"]
    omega = np.zeros((HH, HD, HH, NF), np.float32)
    for h in range(HH):
        omega[h, :, h, :] = a["L1_attn_omega"].T
    io["omega"] = omega.reshape(P, HH * NF)
    for n in ("ln1_g", "ln1_b", "ln2_g", "ln2_b", "b2"):
        io[f"mlp_{n}"] = a[f"L1_attn_{n}"]
    io["mlp_w1"], io["mlp_w2"], io["mlp_b1"] = a["L1_attn_w1"], a["L1_attn_w2"], chunked(a["L1_attn_b1"])
    io["moe_w1"] = a["L1_ffn_w1"].transpose(0, 2, 1)
    io["moe_w2"] = a["L1_ffn_w2"].transpose(0, 2, 1)
    io["router"] = a["L1_ffn_router_w"].T
    io["mask_bv"], io["mask_bo"] = a["L0_xattn_bv"], a["L0_xattn_bo"]
    return io


def kernel(**inputs):
    import concourse.bacc as bacc
    from concourse.bass_utils import run_bass_kernel_spmd

    arrays = {n: np.ascontiguousarray(v) for n, v in layout({n: np.asarray(v) for n, v in inputs.items()}).items()}
    nc = bacc.Bacc("TRN2", target_bir_lowering=False, num_devices=1)
    io = {n: nc.dram_tensor(f"in_{n}", v.shape, mybir.dt.from_np(v.dtype), kind="ExternalInput").ap()
          for n, v in arrays.items()}
    out = nc.dram_tensor("out_0", (B * S, D), F32, kind="ExternalOutput").ap()
    program(nc, io, out)
    got = run_bass_kernel_spmd(nc, [{f"in_{n}": v for n, v in arrays.items()}], core_ids=[0])
    return got.results[0]["out_0"].reshape(B, S, D)
```
